# Optimizing a Trainium2 kernel written in Bass

```python
import numpy as np
import jax
import jax.numpy as jnp

def _softmax(x, axis=-1):
    return jax.nn.softmax(x, axis=axis)

def _gelu(x):
    return jax.nn.gelu(x, approximate=True)

def _silu(x):
    return jax.nn.silu(x)

def _sigmoid(x):
    return jax.nn.sigmoid(x)

def _layernorm(x, axis=-1, eps=1e-05):
    m = jnp.mean(x, axis=axis, keepdims=True)
    v = jnp.var(x, axis=axis, keepdims=True)
    return (x - m) / jnp.sqrt(v + eps)

def _scatter_add(tgt, idx, src, axis=0):
    return tgt.at[idx].add(src)

def _segment_sum(src, seg, n):
    return jax.ops.segment_sum(src, seg, n)
kernel_name = 'mk_audio_tower_d1_tok_aud1d768_r4_49bbab'

def setup_inputs(seed: int=0):
    np.random.seed(seed)
    _w = jnp.asarray

    def _rec_inputs():
        import jax
        import jax.numpy as jnp
        _rk = jax.random.key(seed)
        x = -6.41493e-05 + 1.00002 * jax.random.normal(jax.random.fold_in(_rk, 1), (8, 80000), jnp.float32)
        return x
    x = _rec_inputs()

    def _L0_tok_setup():
        import jax, jax.numpy as jnp
        import numpy as np
        import math
        SR = 4000
        FRAME_LEN = 100
        FRAME_STEP = 160
        N_FILTERS = 40
        N_MFCC = 13
        EMBED = 192
        BATCH = 64
        AUDIO_LEN = 40000
        N_FFT_BINS = FRAME_LEN // 2 + 1

        def _mel_filterbank():
            low_mel = 2595.0 * math.log10(1.0 + 0.0 / 700.0)
            high_mel = 2595.0 * math.log10(1.0 + SR // 2 / 700.0)
            mel_points = np.linspace(low_mel, high_mel, N_FILTERS + 2)
            hz_points = 700.0 * (10.0 ** (mel_points / 2595.0) - 1.0)
            bin_points = np.floor((FRAME_LEN + 1) * hz_points / SR)
            filt = np.zeros((N_FILTERS, N_FFT_BINS), dtype=np.float32)
            for i in range(1, N_FILTERS + 1):
                l, c, r = (bin_points[i - 1], bin_points[i], bin_points[i + 1])
                for j in range(int(l), int(c)):
                    filt[i - 1, j] = (j - l) / (c - l)
                for j in range(int(c), int(r)):
                    filt[i - 1, j] = (r - j) / (r - c)
            return jnp.asarray(filt)

        def _dct_matrix():
            k = np.arange(N_MFCC)[:, None]
            j = np.arange(N_FILTERS)[None, :]
            m = np.cos(np.pi * k * (2 * j + 1) / (2 * N_FILTERS)) * math.sqrt(2.0 / N_FILTERS)
            return jnp.asarray(m.astype(np.float32))
        key = jax.random.key(seed)
        kx, kw = jax.random.split(key)
        x = jax.random.normal(kx, (BATCH, AUDIO_LEN), dtype=jnp.float32)
        bound = 1.0 / math.sqrt(N_MFCC)
        w_proj = jax.random.uniform(kw, (N_MFCC, EMBED), minval=-bound, maxval=bound, dtype=jnp.float32)
        b_proj = jnp.zeros((EMBED,), dtype=jnp.float32)
        return {'x': x, 'mel_filters': _mel_filterbank(), 'dct': _dct_matrix(), 'w_proj': w_proj, 'b_proj': b_proj}
    _L0_tok_all = _L0_tok_setup()
    _L0_tok_in = {k: v for k, v in _L0_tok_all.items() if k in ('mel_filters', 'dct', 'w_proj', 'b_proj')}
    del _L0_tok_all

    def _L0_attn_setup():
        import jax, jax.numpy as jnp
        import numpy as np
        B, L, D, H = (2, 256, 192, 12)
        DH = D // H

        def _reference_tuple_inner(x, W_qkv, b_qkv, W_gate, b_gate, W_proj, b_proj, ln_g, ln_b):
            Bx, Lx, Dx = x.shape
            dh = Dx // H
            mu = jnp.mean(x, axis=-1, keepdims=True)
            var = jnp.var(x, axis=-1, keepdims=True)
            xn = (x - mu) / jnp.sqrt(var + 1e-05) * ln_g + ln_b
            qkv = xn @ W_qkv + b_qkv
            q, k, v = jnp.split(qkv, 3, axis=-1)
            gate = jax.nn.sigmoid(x @ W_gate + b_gate)
            k = k * gate

            def heads(t):
                return t.reshape(Bx, Lx, H, dh).transpose(0, 2, 1, 3)
            q_f = jax.nn.elu(heads(q).astype(jnp.float32)) + 1.0
            k_f = jax.nn.elu(heads(k).astype(jnp.float32)) + 1.0
            v_f = heads(v).astype(jnp.float32)
            kv_cum = jnp.cumsum(k_f[..., :, None] * v_f[..., None, :], axis=2)
            out_num = jnp.einsum('bhld,bhlde->bhle', q_f, kv_cum)
            k_cum = jnp.cumsum(k_f, axis=2)
            out_den = jnp.sum(q_f * k_cum, axis=-1, keepdims=True) + 1e-06
            attn = (out_num / out_den).astype(x.dtype)
            attn = attn.transpose(0, 2, 1, 3).reshape(Bx, Lx, Dx)
            return (attn @ W_proj + b_proj, gate)
        key = jax.random.key(seed)
        ks = jax.random.split(key, 4)
        s = 0.02
        return {'x': jax.random.normal(ks[0], (B, L, D), jnp.float32), 'W_qkv': jax.random.normal(ks[1], (D, 3 * D), jnp.float32) * s, 'b_qkv': jnp.zeros((3 * D,), jnp.float32), 'W_gate': jax.random.normal(ks[2], (D, D), jnp.float32) * s, 'b_gate': jnp.zeros((D,), jnp.float32), 'W_proj': jax.random.normal(ks[3], (D, D), jnp.float32) * s, 'b_proj': jnp.zeros((D,), jnp.float32), 'ln_g': jnp.ones((D,), jnp.float32), 'ln_b': jnp.zeros((D,), jnp.float32)}
    _L0_attn_all = _L0_attn_setup()
    _L0_attn_in = {k: v for k, v in _L0_attn_all.items() if k in ('W_qkv', 'b_qkv', 'W_gate', 'b_gate', 'W_proj', 'b_proj', 'ln_g', 'ln_b')}
    del _L0_attn_all

    def _L0_ffn_setup():
        import jax, jax.numpy as jnp
        import numpy as np
        B, S, D = (2, 512, 192)
        E, K, F = (8, 2, 384)

        def _swiglu(xf, wg, wu, wd):
            return jax.nn.silu(xf @ wg.T) * (xf @ wu.T) @ wd.T
        key = jax.random.key(seed)
        ks = jax.random.split(key, 9)
        scale = 0.02
        x = jax.random.normal(ks[0], (B, S, D), dtype=jnp.float32)
        w_router = jax.random.normal(ks[1], (E, D), dtype=jnp.float32) * scale
        expert_bias = jnp.zeros((E,), dtype=jnp.float32)
        Wg = jax.random.normal(ks[2], (E, F, D), dtype=jnp.float32) * scale
        Wu = jax.random.normal(ks[3], (E, F, D), dtype=jnp.float32) * scale
        Wd = jax.random.normal(ks[4], (E, D, F), dtype=jnp.float32) * scale
        sg = jax.random.normal(ks[5], (F, D), dtype=jnp.float32) * scale
        su = jax.random.normal(ks[6], (F, D), dtype=jnp.float32) * scale
        sd = jax.random.normal(ks[7], (D, F), dtype=jnp.float32) * scale
        return {'x': x, 'w_router': w_router, 'expert_bias': expert_bias, 'Wg': Wg, 'Wu': Wu, 'Wd': Wd, 'sg': sg, 'su': su, 'sd': sd}
    _L0_ffn_all = _L0_ffn_setup()
    _L0_ffn_in = {k: v for k, v in _L0_ffn_all.items() if k in ('w_router', 'expert_bias', 'Wg', 'Wu', 'Wd', 'sg', 'su', 'sd')}
    del _L0_ffn_all
    return {'x': x, 'L0_tok_mel_filters': _L0_tok_in['mel_filters'], 'L0_tok_dct': _L0_tok_in['dct'], 'L0_tok_w_proj': _L0_tok_in['w_proj'], 'L0_tok_b_proj': _L0_tok_in['b_proj'], 'L0_attn_W_qkv': _L0_attn_in['W_qkv'], 'L0_attn_b_qkv': _L0_attn_in['b_qkv'], 'L0_attn_W_gate': _L0_attn_in['W_gate'], 'L0_attn_b_gate': _L0_attn_in['b_gate'], 'L0_attn_W_proj': _L0_attn_in['W_proj'], 'L0_attn_b_proj': _L0_attn_in['b_proj'], 'L0_attn_ln_g': _L0_attn_in['ln_g'], 'L0_attn_ln_b': _L0_attn_in['ln_b'], 'L0_ffn_w_router': _L0_ffn_in['w_router'], 'L0_ffn_expert_bias': _L0_ffn_in['expert_bias'], 'L0_ffn_Wg': _L0_ffn_in['Wg'], 'L0_ffn_Wu': _L0_ffn_in['Wu'], 'L0_ffn_Wd': _L0_ffn_in['Wd'], 'L0_ffn_sg': _L0_ffn_in['sg'], 'L0_ffn_su': _L0_ffn_in['su'], 'L0_ffn_sd': _L0_ffn_in['sd']}

def reference(x, L0_tok_mel_filters, L0_tok_dct, L0_tok_w_proj, L0_tok_b_proj, L0_attn_W_qkv, L0_attn_b_qkv, L0_attn_W_gate, L0_attn_b_gate, L0_attn_W_proj, L0_attn_b_proj, L0_attn_ln_g, L0_attn_ln_b, L0_ffn_w_router, L0_ffn_expert_bias, L0_ffn_Wg, L0_ffn_Wu, L0_ffn_Wd, L0_ffn_sg, L0_ffn_su, L0_ffn_sd):
    import jax
    import jax.numpy as jnp

    def _L0_tok_ref(x, mel_filters, dct, w_proj, b_proj):
        import jax, jax.numpy as jnp
        import numpy as np
        import math
        SR = 4000
        FRAME_LEN = 100
        FRAME_STEP = 160
        N_FILTERS = 40
        N_MFCC = 13
        EMBED = 192
        BATCH = 64
        AUDIO_LEN = 40000
        N_FFT_BINS = FRAME_LEN // 2 + 1

        def _mel_filterbank():
            low_mel = 2595.0 * math.log10(1.0 + 0.0 / 700.0)
            high_mel = 2595.0 * math.log10(1.0 + SR // 2 / 700.0)
            mel_points = np.linspace(low_mel, high_mel, N_FILTERS + 2)
            hz_points = 700.0 * (10.0 ** (mel_points / 2595.0) - 1.0)
            bin_points = np.floor((FRAME_LEN + 1) * hz_points / SR)
            filt = np.zeros((N_FILTERS, N_FFT_BINS), dtype=np.float32)
            for i in range(1, N_FILTERS + 1):
                l, c, r = (bin_points[i - 1], bin_points[i], bin_points[i + 1])
                for j in range(int(l), int(c)):
                    filt[i - 1, j] = (j - l) / (c - l)
                for j in range(int(c), int(r)):
                    filt[i - 1, j] = (r - j) / (r - c)
            return jnp.asarray(filt)

        def _dct_matrix():
            k = np.arange(N_MFCC)[:, None]
            j = np.arange(N_FILTERS)[None, :]
            m = np.cos(np.pi * k * (2 * j + 1) / (2 * N_FILTERS)) * math.sqrt(2.0 / N_FILTERS)
            return jnp.asarray(m.astype(np.float32))
        B, T = x.shape
        n_frames = 1 + (T - FRAME_LEN) // FRAME_STEP
        idx = jnp.arange(n_frames)[:, None] * FRAME_STEP + jnp.arange(FRAME_LEN)[None, :]
        frames = x[:, idx]
        window = 0.54 - 0.46 * jnp.cos(2.0 * jnp.pi * jnp.arange(FRAME_LEN, dtype=jnp.float32) / (FRAME_LEN - 1))
        windowed = frames * window
        fft = jnp.fft.rfft(windowed, axis=-1)
        power = fft.real ** 2 + fft.imag ** 2
        mel_energies = jnp.einsum('bnf,mf->bnm', power, mel_filters)
        log_energies = jnp.log(mel_energies + 1e-06)
        mfcc = jnp.einsum('bnm,km->bnk', log_energies, dct)
        out = mfcc @ w_proj + b_proj
        return out

    def _L0_attn_ref(x, W_qkv, b_qkv, W_gate, b_gate, W_proj, b_proj, ln_g, ln_b):
        import jax, jax.numpy as jnp
        import numpy as np
        B, L, D, H = (2, 256, 192, 12)
        DH = D // H

        def _reference_tuple_inner(x, W_qkv, b_qkv, W_gate, b_gate, W_proj, b_proj, ln_g, ln_b):
            Bx, Lx, Dx = x.shape
            dh = Dx // H
            mu = jnp.mean(x, axis=-1, keepdims=True)
            var = jnp.var(x, axis=-1, keepdims=True)
            xn = (x - mu) / jnp.sqrt(var + 1e-05) * ln_g + ln_b
            qkv = xn @ W_qkv + b_qkv
            q, k, v = jnp.split(qkv, 3, axis=-1)
            gate = jax.nn.sigmoid(x @ W_gate + b_gate)
            k = k * gate

            def heads(t):
                return t.reshape(Bx, Lx, H, dh).transpose(0, 2, 1, 3)
            q_f = jax.nn.elu(heads(q).astype(jnp.float32)) + 1.0
            k_f = jax.nn.elu(heads(k).astype(jnp.float32)) + 1.0
            v_f = heads(v).astype(jnp.float32)
            kv_cum = jnp.cumsum(k_f[..., :, None] * v_f[..., None, :], axis=2)
            out_num = jnp.einsum('bhld,bhlde->bhle', q_f, kv_cum)
            k_cum = jnp.cumsum(k_f, axis=2)
            out_den = jnp.sum(q_f * k_cum, axis=-1, keepdims=True) + 1e-06
            attn = (out_num / out_den).astype(x.dtype)
            attn = attn.transpose(0, 2, 1, 3).reshape(Bx, Lx, Dx)
            return (attn @ W_proj + b_proj, gate)
        return _reference_tuple_inner(x, W_qkv, b_qkv, W_gate, b_gate, W_proj, b_proj, ln_g, ln_b)[0]

    def _L0_ffn_ref(x, w_router, expert_bias, Wg, Wu, Wd, sg, su, sd):
        import jax, jax.numpy as jnp
        import numpy as np
        B, S, D = (2, 512, 192)
        E, K, F = (8, 2, 384)

        def _swiglu(xf, wg, wu, wd):
            return jax.nn.silu(xf @ wg.T) * (xf @ wu.T) @ wd.T
        b, s, d = x.shape
        xf = x.reshape(-1, d)
        T = xf.shape[0]
        e = w_router.shape[0]
        logits = xf @ w_router.T
        scores = jax.nn.softmax(logits, axis=-1)
        selection = scores + expert_bias[None, :]
        _, top_idx = jax.lax.top_k(selection, K)
        top_s = jnp.take_along_axis(scores, top_idx, axis=-1)
        top_s = top_s / (jnp.sum(top_s, axis=-1, keepdims=True) + 1e-09)
        comb = jnp.zeros((T, e), dtype=x.dtype).at[jnp.arange(T)[:, None], top_idx].add(top_s)

        def body(acc, p):
            wg, wu, wd, c = p
            return (acc + c[:, None] * _swiglu(xf, wg, wu, wd), None)
        routed, _ = jax.lax.scan(body, jnp.zeros_like(xf), (Wg, Wu, Wd, comb.T))
        out = routed + _swiglu(xf, sg, su, sd)
        return out.reshape(b, s, d)
    h = _L0_tok_ref(x, L0_tok_mel_filters, L0_tok_dct, L0_tok_w_proj, L0_tok_b_proj)
    h = h + _L0_attn_ref(_layernorm(h, axis=-1), L0_attn_W_qkv, L0_attn_b_qkv, L0_attn_W_gate, L0_attn_b_gate, L0_attn_W_proj, L0_attn_b_proj, L0_attn_ln_g, L0_attn_ln_b)
    h = h + _L0_ffn_ref(_layernorm(h, axis=-1), L0_ffn_w_router, L0_ffn_expert_bias, L0_ffn_Wg, L0_ffn_Wu, L0_ffn_Wd, L0_ffn_sg, L0_ffn_su, L0_ffn_sd)
    return h

_drawn_inputs = setup_inputs


def setup_inputs(seed=0):
    import zlib

    import numpy as np

    out = dict(_drawn_inputs(seed))
    spreads = {'L0_tok_b_proj': (0.0, 0.332),
     'L0_attn_b_qkv': (0.0, 0.8),
     'L0_attn_b_gate': (0.0, 0.8),
     'L0_attn_b_proj': (0.0, 0.314),
     'L0_attn_ln_g': (1.0, 0.6),
     'L0_attn_ln_b': (0.0, 0.8),
     'L0_ffn_expert_bias': (0.0, 0.8)}
    factors = {'L0_attn_W_qkv': 2.68,
     'L0_attn_W_gate': 8.0,
     'L0_ffn_w_router': 8.0,
     'L0_ffn_Wg': 8.0,
     'L0_ffn_Wu': 8.0,
     'L0_ffn_Wd': 8.0,
     'L0_ffn_sg': 8.0,
     'L0_ffn_su': 8.0,
     'L0_ffn_sd': 8.0}
    for name, (base, spread) in spreads.items():
        noise = np.random.default_rng([zlib.crc32(name.encode()), seed]).standard_normal(out[name].shape)
        drawn = base * np.exp(spread * noise) if base else spread * noise
        out[name] = jnp.asarray(drawn.astype(out[name].dtype))
    for name, factor in factors.items():
        out[name] = (out[name] * factor).astype(out[name].dtype)
    return out
```

```python
from contextlib import ExitStack

import numpy as np

import concourse.bass as bass
from concourse import mybir

F32 = mybir.dt.float32
F32R = mybir.dt.float32r
ACT = mybir.ActivationFunctionType
ALU = mybir.AluOpType
AX = mybir.AxisListType

P = 128
N_SEQ = 8
FRAME = 100
STEP = 160
N_TOK = 500
N_BLK = 4
BLK = N_TOK // N_BLK
D = 192
REST = D - P
HEADS = 12
DH = D // HEADS
HEADS_MAIN = P // DH
N_MEL = 40
N_BINS = FRAME // 2 + 1
N_MFCC = 13
N_EXP = 8
F = 384
N_CHUNK = F // P
LN_EPS = 1e-5
VA = DH + 1
GRP = 4
N_GRP = HEADS // GRP
COL_Q, COL_K, COL_V, COL_G, COL_P, COL_R = 0, D, 2 * D, 3 * D, 4 * D, 5 * D
N_PACK = 5 * D + N_EXP


def at_least(engine, semaphore, value):
    if not isinstance(value, int) or value > 0:
        engine.wait_ge(semaphore, value)


def stand(engine, passed):
    engine.sem_inc(passed, 1)


def build(nc, frames, dft, mel2, dct, w_mfcc, b_tok, w_pack, b_qk_col, b_v, b_gate_col, ln_b_col, ln_g_col,
          b_proj, head_main, head_rest, exp_bias, w_up, w_down, out):
    with ExitStack() as ctx:
        def sb(name, shape, dt=F32):
            return ctx.enter_context(nc.sbuf_tensor(name, shape, dt))

        def sem(name):
            return ctx.enter_context(nc.semaphore(name))

        bank = [ctx.enter_context(nc.psum_tensor(f"bank{i}", [P, 512], F32)) for i in range(8)]

        h_all = sb("h_all", [BLK, N_SEQ, N_BLK, D])
        x_all = sb("x_all", [P, N_SEQ, 3, N_TOK], F32R)
        logits = sb("logits", [BLK, N_SEQ * N_BLK, N_EXP])
        comb = sb("comb", [BLK, 1 + N_EXP, N_SEQ * N_BLK])
        ident = sb("ident", [P, P])
        stage_up = sb("stage_up", [P, 2, 2 * F])
        stage_down = sb("stage_down", [P, N_CHUNK, D])
        stage_in = sem("stage_in")
        passed = sem("passed")
        loaded = sem("loaded")
        loaded_more = sem("loaded_more")
        made = sem("made")

        def load_expert(sp, e):
            sp.dma_start(stage_up[:, 0, :], w_up[e, 0:P, :]).then_inc(stage_in, 16)
            sp.dma_start(stage_up[0:REST, 1, :], w_up[e, P:D, :]).then_inc(stage_in, 16)
            sp.dma_start(stage_up[REST:P, 1, :], w_up[e, P:D, :]).then_inc(stage_in, 16)
            sp.dma_start(stage_down[:], w_down[e]).then_inc(stage_in, 16)

        attn_stage(nc, passed, sem, bank, h_all, x_all, logits, ident, made, loaded, loaded_more, load_expert, frames, dft, mel2,
                   dct, w_mfcc, b_tok, w_pack, b_qk_col, b_v, b_gate_col, ln_b_col, ln_g_col, b_proj, head_main,
                   head_rest)
        moe_stage(nc, passed, sem, bank, h_all, x_all, logits, comb, stage_up, stage_down, stage_in, load_expert,
                  exp_bias, out)


def attn_stage(nc, passed, sem, bank, h_all, x_all, logits, ident, made, loaded, loaded_more, load_expert, frames, dft, mel2,
               dct, w_mfcc, b_tok, w_pack, b_qk_col, b_v, b_gate_col, ln_b_col, ln_g_col, b_proj, head_main,
               head_rest):
    with ExitStack() as ctx:
        def sb(name, shape, dt=F32):
            return ctx.enter_context(nc.sbuf_tensor(name, shape, dt))

        pack_raw = sb("pack_raw", [P, 2, N_PACK])
        pack_hi = sb("pack_hi", [P, 2, N_PACK], F32R)
        pack_lo = sb("pack_lo", [P, 2, N_PACK], F32R)
        ln_b = sb("ln_b", [P, 2])
        ln_g = sb("ln_g", [P, 2])
        ln_b_wide = sb("ln_b_wide", [P, 2, BLK])
        bqk = sb("bqk", [P, 4])
        bgate = sb("bgate", [P, 2])
        bgate_half = sb("bgate_half", [P, 2])
        bv_bc = sb("bv_bc", [BLK, D])
        bproj_bc = sb("bproj_bc", [BLK, D])
        causal = sb("causal", [BLK, BLK])
        hm_main = sb("hm_main", [P, HEADS_MAIN])
        hm_rest = sb("hm_rest", [REST, HEADS - HEADS_MAIN])
        minus_half = sb("minus_half", [BLK, N_BLK])
        ln_eps_tile = sb("log_eps", [P, 1])

        stats = sb("stats", [BLK, N_BLK, 6])
        moments = sb("moments", [BLK, N_BLK, 2])
        var_eps = sb("var_eps", [BLK, N_BLK])
        rstd = sb("rstd", [BLK, N_BLK])
        hn = sb("hn", [BLK, N_BLK, D])
        z = sb("z", [BLK, N_BLK, D])
        x2 = sb("x2", [BLK, N_BLK, D])
        hb = sb("hb", [BLK, N_BLK, D])
        hn_t = sb("hn_t", [P, 3, N_TOK], F32R)
        z_t = sb("z_t", [P, 3, N_TOK], F32R)
        a_t = sb("a_t", [P, 3, N_TOK], F32R)
        x_t = a_t
        gate = sb("gate", [P, 2, N_TOK])
        kg = sb("kg", [P, 2, N_TOK])
        k_exp = sb("k_exp", [P, 2, N_TOK])
        k_pos = sb("k_pos", [P, 2, N_TOK])
        kf = sb("kf", [P, 2, N_TOK])
        kh = sb("kh", [P, HEADS, N_TOK])
        q_exp, q_pos = k_exp, k_pos
        qf = sb("qf", [P, 2, N_TOK])
        v_aug = sb("v_aug", [BLK, N_BLK, HEADS, VA])
        k_tok = sb("k_tok", [BLK, N_BLK - 1, D])
        state = sb("state", [P, N_BLK, HEADS_MAIN * VA])
        state_r = sb("state_r", [P, N_BLK, (HEADS - HEADS_MAIN) * VA])
        probs = pack_raw[0:BLK, :, :].rearrange("p a c -> p (a c)")[:, 0:3 * GRP * BLK].rearrange(
            "p (r c) -> p r c", r=3)
        den = sb("den", [BLK, HEADS])
        rden = sb("rden", [BLK, HEADS])
        attn = sb("attn", [BLK, N_BLK, D])

        with ExitStack() as tok_ctx:
            def tok_sb(name, shape, dt=F32):
                return tok_ctx.enter_context(nc.sbuf_tensor(name, shape, dt))

            fr = kh[0:FRAME, 0:N_SEQ, :]
            dft_sb = tok_sb("dft_sb", [FRAME, 2 * N_BINS])
            mel_sb = tok_sb("mel_sb", [2 * N_BINS, N_MEL])
            dct_sb = tok_sb("dct_sb", [N_MFCC, N_MEL])
            wm_sb = tok_sb("wm_sb", [N_MFCC, D])
            to_h = tok_sb("to_h", [N_MEL + 1, D])
            squares = tok_sb("squares", [2 * N_BINS, N_TOK])
            logmel = tok_sb("logmel", [N_MEL + 1, N_TOK])
            wts_in, pack_in, frames_in = sem("wts_in"), sem("pack_in"), sem("frames_in")
            spectrum, squared, melled, logged = sem("spectrum"), sem("squared"), sem("melled"), sem("logged")
            token_mm, token_out, fused, fused_out = sem("token_mm"), sem("token_out"), sem("fused"), sem("fused_out")
            bias_mm, bias_out, split_hi, split_lo = sem("bias_mm"), sem("bias_out"), sem("split_hi"), sem("split_lo")
            scaled, wide_b = sem("scaled"), sem("wide_b")
            N_SMALL = 16

            with nc.Block() as block:
                @block.sync
                def _(sp):
                    sp.dma_start(dft_sb[:], dft).then_inc(frames_in, 16)
                    sp.dma_start(fr, frames).then_inc(frames_in, 16)
                    sp.dma_start(mel_sb[:], mel2).then_inc(frames_in, 16)
                    sp.dma_start(dct_sb[:], dct).then_inc(wts_in, 16)
                    sp.dma_start(wm_sb[:], w_mfcc).then_inc(wts_in, 16)
                    sp.dma_start(to_h[N_MEL:N_MEL + 1, :], b_tok).then_inc(wts_in, 16)
                    sp.dma_start(pack_raw[:, 0, :], w_pack[0:P, :]).then_inc(pack_in, 16)
                    sp.dma_start(pack_raw[0:REST, 1, :], w_pack[P:D, :]).then_inc(pack_in, 16)
                    sp.dma_start(pack_raw[REST:P, 1, :], w_pack[P:D, :]).then_inc(pack_in, 16)
                    for half in range(2):
                        lo, n = half * P, (P, REST)[half]
                        sp.dma_start(bqk[0:n, half:half + 1], b_qk_col[lo:lo + n, :]).then_inc(wts_in, 16)
                        sp.dma_start(bqk[0:n, 2 + half:3 + half], b_qk_col[D + lo:D + lo + n, :]).then_inc(wts_in, 16)
                        sp.dma_start(bgate[0:n, half:half + 1], b_gate_col[lo:lo + n, :]).then_inc(wts_in, 16)
                        sp.dma_start(ln_b[0:n, half:half + 1], ln_b_col[lo:lo + n, :]).then_inc(wts_in, 16)
                    sp.dma_start(ln_g[:, 0:1], ln_g_col[0:P, :]).then_inc(wts_in, 16)
                    sp.dma_start(ln_g[0:REST, 1:2], ln_g_col[P:D, :]).then_inc(wts_in, 16)
                    sp.dma_start(ln_g[REST:P, 1:2], ln_g_col[P:D, :]).then_inc(wts_in, 16)
                    sp.dma_start(bv_bc[:], b_v.partition_broadcast(BLK)).then_inc(wts_in, 16)
                    sp.dma_start(bproj_bc[:], b_proj.partition_broadcast(BLK)).then_inc(wts_in, 16)
                    sp.dma_start(hm_main[:], head_main).then_inc(loaded, 16)
                    sp.dma_start(hm_rest[:], head_rest).then_inc(loaded, 16)
                    load_expert(sp, 0)

                @block.gpsimd
                def _(pool):
                    nc.gpsimd.memset(ident[:], 0.0).then_inc(made, 1)
                    nc.gpsimd.memset(causal[:], 1.0).then_inc(made, 1)
                    nc.gpsimd.memset(ln_eps_tile[:], 1e-6).then_inc(made, 1)
                    nc.gpsimd.memset(logmel[:], 1.0).then_inc(made, 1)
                    nc.gpsimd.memset(minus_half[:], -0.5).then_inc(made, 1)
                    pool.wait_ge(made, 5)
                    nc.gpsimd.affine_select(out=ident[:], in_=ident[:], compare_op=ALU.not_equal, fill=1.0, base=0,
                                            pattern=[[-1, P]], channel_multiplier=1).then_inc(made, 1)
                    nc.gpsimd.affine_select(out=causal[:], in_=causal[:], compare_op=ALU.is_ge, fill=0.0, base=0,
                                            pattern=[[1, BLK]], channel_multiplier=-1).then_inc(made, 1)
                    nc.gpsimd.memset(v_aug[:], 1.0).then_inc(made, 1)
                    nc.gpsimd.memset(state[:, 0, :], 0.0).then_inc(made, 1)
                    nc.gpsimd.memset(state_r[:], 0.0).then_inc(made, 1)
                    pool.wait_ge(made, 10)
                    nc.gpsimd.memset(qf[REST:P, 1, :], 0.0).then_inc(made, 1)
                    nc.gpsimd.memset(kh[REST:P, HEADS_MAIN:HEADS, :], 0.0).then_inc(made, 1)
                    pool.wait_ge(made, 12)
                    pool.wait_ge(wts_in, 16 * N_SMALL)
                    nc.gpsimd.memset(ln_b_wide[:], 0.0).then_inc(wide_b, 1)
                    pool.wait_ge(wide_b, 1)
                    nc.gpsimd.tensor_scalar(ln_b_wide[:, 0, :], ln_b_wide[:, 0, :], ln_b[:, 0:1], None,
                                            ALU.add).then_inc(wide_b, 1)
                    nc.gpsimd.tensor_scalar(ln_b_wide[0:REST, 1, :], ln_b_wide[0:REST, 1, :], ln_b[0:REST, 1:2], None,
                                            ALU.add).then_inc(wide_b, 1)

                @block.tensor
                def _(pe):
                    pe.wait_ge(wts_in, 16 * N_SMALL)
                    nc.tensor.matmul(bank[3][0:N_MEL, 0:D], dct_sb[:], wm_sb[:], start=True, stop=True).then_inc(fused, 1)
                    pe.wait_ge(pack_in, 48)
                    pe.wait_ge(wide_b, 3)
                    for n, (lo, m) in enumerate([(COL_Q, P), (COL_Q + P, REST), (COL_K, P), (COL_K + P, REST)]):
                        nc.tensor.matmul(bank[2][0:m, n:n + 1], pack_raw[:, 0, lo:lo + m], ln_b[:, 0:1],
                                         start=(n == 0), stop=False, skip_group_check=True)
                        nc.tensor.matmul(bank[2][0:m, n:n + 1], pack_raw[0:REST, 1, lo:lo + m], ln_b[0:REST, 1:2],
                                         start=False, stop=True, skip_group_check=True)
                    nc.tensor.matmul(bank[1][0:BLK, 0:D], ln_b_wide[:, 0, :], pack_raw[:, 0, COL_V:COL_V + D],
                                     start=True, stop=False)
                    nc.tensor.matmul(bank[1][0:BLK, 0:D], ln_b_wide[0:REST, 1, :], pack_raw[0:REST, 1, COL_V:COL_V + D],
                                     start=False, stop=True).then_inc(bias_mm, 1)
                    pe.wait_ge(frames_in, 48)
                    pe.wait_ge(fused_out, 1)
                    pe.wait_ge(bias_out, 5)

                    def spectrum_of(n):
                        nc.tensor.matmul(bank[0][0:2 * N_BINS, 0:N_TOK], dft_sb[:], fr[:, n, :],
                                         start=True, stop=True).then_inc(spectrum, 1)

                    def tokens_of(n, first):
                        pe.wait_ge(squared, n + 1)
                        if not first:
                            pe.wait_ge(logged, n)
                        nc.tensor.matmul(bank[2][0:N_MEL, 0:N_TOK], mel_sb[:], squares[:],
                                         start=True, stop=True).then_inc(melled, 1)

                    def features_of(n, first):
                        pe.wait_ge(logged, n + 1)
                        if not first:
                            pe.wait_ge(token_out, 2 * n)
                        for t in range(N_BLK):
                            mm = nc.tensor.matmul(bank[4 + t // 2][0:BLK, (t % 2) * D:(t % 2 + 1) * D],
                                                  logmel[:, t * BLK:(t + 1) * BLK], to_h[:],
                                                  start=(t % 2 == 0), stop=(t % 2 == 1), skip_group_check=True)
                            if t % 2:
                                mm.then_inc(token_mm, 1)

                    pe.wait_ge(made, 4)
                    spectrum_of(0)
                    tokens_of(0, True)
                    spectrum_of(1)
                    features_of(0, True)
                    with pe.Fori(1, N_SEQ - 1) as n:
                        tokens_of(n, False)
                        spectrum_of(n + 1)
                        features_of(n, False)
                    tokens_of(N_SEQ - 1, False)
                    features_of(N_SEQ - 1, False)

                @block.scalar
                def _(act):
                    def square_of(n, first):
                        act.wait_ge(spectrum, n + 1)
                        if not first:
                            act.wait_ge(melled, n)
                        nc.scalar.activation(squares[:], bank[0][0:2 * N_BINS, 0:N_TOK], ACT.Square).then_inc(squared, 1)

                    def log_of(n, first):
                        act.wait_ge(melled, n + 1)
                        if not first:
                            act.wait_ge(token_mm, 2 * n)
                        nc.scalar.activation(logmel[0:N_MEL, :], bank[2][0:N_MEL, 0:N_TOK], ACT.Ln,
                                             bias=ln_eps_tile[0:N_MEL, :]).then_inc(logged, 1)

                    act.wait_ge(made, 4)
                    square_of(0, True)
                    log_of(0, True)
                    with act.Fori(1, N_SEQ) as n:
                        square_of(n, False)
                        log_of(n, False)
                    act.wait_ge(scaled, 2)
                    nc.scalar.copy(pack_hi[:, 0, :], pack_raw[:, 0, :]).then_inc(split_hi, 1)
                    nc.scalar.copy(pack_hi[:, 1, :], pack_raw[:, 1, :]).then_inc(split_hi, 1)
                    nc.scalar.mul(bgate_half[:, 0:1], bgate[:, 0:1], 0.5)
                    nc.scalar.mul(bgate_half[0:REST, 1:2], bgate[0:REST, 1:2], 0.5).then_inc(split_hi, 1)

                @block.vector
                def _(dve):
                    dve.wait_ge(wts_in, 16 * N_SMALL)
                    dve.wait_ge(fused, 1)
                    nc.vector.tensor_copy(to_h[0:N_MEL, :], bank[3][0:N_MEL, 0:D]).then_inc(fused_out, 1)
                    dve.wait_ge(bias_mm, 1)
                    for n, m in enumerate([P, REST, P, REST]):
                        nc.vector.tensor_tensor(bqk[0:m, n:n + 1], bank[2][0:m, n:n + 1], bqk[0:m, n:n + 1],
                                                ALU.add).then_inc(bias_out, 1)
                    nc.vector.tensor_tensor(bv_bc[:], bank[1][0:BLK, 0:D], bv_bc[:], ALU.add).then_inc(bias_out, 1)
                    for part in range(2):
                        nc.vector.tensor_scalar(pack_raw[:, part, 0:3 * D], pack_raw[:, part, 0:3 * D],
                                                ln_g[:, part:part + 1], None, ALU.mult).then_inc(scaled, 1)
                    with dve.Fori(0, N_SEQ) as n:
                        for pair in range(2):
                            dve.wait_ge(token_mm, 2 * n + pair + 1)
                            nc.vector.tensor_copy(h_all[:, n, 2 * pair:2 * pair + 2, :],
                                                  bank[4 + pair][0:BLK, 0:2 * D].rearrange("p (t d) -> p t d", t=2)
                                                  ).then_inc(token_out, 1)
                    for part in range(2):
                        dve.wait_ge(split_hi, part + 1)
                        nc.vector.tensor_tensor(pack_lo[:, part, :], pack_raw[:, part, :],
                                                pack_hi[:, part, :].bitcast(F32), ALU.subtract).then_inc(split_lo, 1)

        centred = sem("centred")
        rooted = sem("rooted")
        chain = sem("chain")
        hn_done, z_done, x2_done = sem("hn_done"), sem("z_done"), sem("x2_done")
        t_hn, t_z, t_a, t_x = sem("t_hn"), sem("t_z"), sem("t_a"), sem("t_x")
        hi_hn, hi_z, hi_a, hi_x = sem("hi_hn"), sem("hi_z"), sem("hi_a"), sem("hi_x")
        lo_hn, lo_z, lo_a, lo_x = sem("lo_hn"), sem("lo_z"), sem("lo_a"), sem("lo_x")
        mm_gk, mm_q, mm_v = sem("mm_gk"), sem("mm_q"), sem("mm_v")
        tanh_done, gate_done = sem("tanh_done"), sem("gate_done")
        kg_done, kexp_done, kpos_done, kf_done = sem("kg_done"), sem("kexp_done"), sem("kpos_done"), sem("kf_done")
        kh_dve, kh_act = sem("kh_dve"), sem("kh_act")
        qexp_done, qpos_done, qf_done = sem("qexp_done"), sem("qpos_done"), sem("qf_done")
        v_done, t_k, ktok_done, mm_kv, state_done = (sem("v_done"), sem("t_k"), sem("ktok_done"), sem("mm_kv"),
                                                     sem("state_done"))
        scores_done, probs_dve, probs_act, probs_pool = (sem("scores_done"), sem("probs_dve"), sem("probs_act"),
                                                         sem("probs_pool"))
        pv_done, den_done, rden_done, attn_done = sem("pv_done"), sem("den_done"), sem("rden_done"), sem("attn_done")
        hb_done, mm_proj, h_done, mm_rt, logits_done = (sem("hb_done"), sem("mm_proj"), sem("h_done"), sem("mm_rt"),
                                                        sem("logits_done"))
        x_copied = sem("x_copied")
        masked = sem("masked")
        N_SC = N_BLK * N_GRP

        def halves(t3):
            return [(t3[:, 0, :], P), (t3[0:REST, 1, :], REST)]

        with nc.Block() as block:
            @block.sync
            def _(sp):
                with sp.Fori(0, N_SEQ) as n:
                    sp.wait_ge(lo_x, 2 * n + 2)
                    stand(sp, passed)
                    sp.dma_start(x_all[:, n, :, :].bitcast(F32), x_t[:].bitcast(F32)).then_inc(x_copied, 16)
                    sp.wait_ge(x_copied, 16 * n + 16)
                    stand(sp, passed)

            @block.tensor
            def _(pe):
                def transpose_blocks(src, n_done, dst_main, dst_rest, signal, wait_main, wait_rest):
                    wait_main()
                    for t in range(N_BLK):
                        mm = nc.tensor.transpose(dst_main[:, t * BLK:(t + 1) * BLK], src[:, t, 0:P], ident[0:BLK, 0:BLK])
                    mm.then_inc(signal, 1)
                    wait_rest()
                    for t in range(N_BLK):
                        mm = nc.tensor.transpose(dst_rest[0:REST, t * BLK:(t + 1) * BLK], src[:, t, P:D],
                                                 ident[0:BLK, 0:BLK])
                    mm.then_inc(signal, 1)

                def project(dst, m, col, x):
                    o = dst[0:m, 0:N_TOK]
                    c = slice(col, col + m)
                    nc.tensor.matmul(o, pack_hi[:, 0, c], x[:, 0, :], start=True, stop=False)
                    nc.tensor.matmul(o, pack_hi[:, 0, c], x[:, 1, :], start=False, stop=False)
                    nc.tensor.matmul(o, pack_lo[:, 0, c], x[:, 0, :], start=False, stop=False)
                    nc.tensor.matmul(o, pack_hi[:, 1, c], x[:, 2, :], start=False, stop=False)
                    return nc.tensor.matmul(o, pack_lo[:, 1, c], x[:, 2, :], start=False, stop=True)

                def project_block(o, x, t, c, first=True, last=True):
                    b = slice(t * BLK, (t + 1) * BLK)
                    nc.tensor.matmul(o, x[:, 0, b], pack_hi[:, 0, c], start=first, stop=False, skip_group_check=True)
                    nc.tensor.matmul(o, x[:, 0, b], pack_lo[:, 0, c], start=False, stop=False, skip_group_check=True)
                    nc.tensor.matmul(o, x[:, 1, b], pack_hi[:, 0, c], start=False, stop=False, skip_group_check=True)
                    nc.tensor.matmul(o, x[:, 2, b], pack_hi[:, 1, c], start=False, stop=False, skip_group_check=True)
                    return nc.tensor.matmul(o, x[:, 2, b], pack_lo[:, 1, c], start=False, stop=last,
                                            skip_group_check=True)

                def front_transpose(n):
                    pe.wait_ge(hn_done, n + 1)
                    transpose_blocks(hn, None, bank[0], bank[1], t_hn,
                                     lambda: at_least(pe, ktok_done, n), lambda: None)
                    pe.wait_ge(z_done, n + 1)
                    transpose_blocks(z, None, bank[2], bank[3], t_z,
                                     lambda: at_least(pe, state_done, 2 * n), lambda: None)

                def front_gate(n):
                    pe.wait_ge(lo_hn, 2 * n + 2)
                    project(bank[0], P, COL_G, hn_t).then_inc(mm_gk, 1)
                    project(bank[1], REST, COL_G + P, hn_t).then_inc(mm_gk, 1)

                def front_k(n):
                    pe.wait_ge(lo_z, 2 * n + 2)
                    project(bank[2], P, COL_K, z_t).then_inc(mm_gk, 1)
                    project(bank[3], REST, COL_K + P, z_t).then_inc(mm_gk, 1)

                def front_q(n):
                    pe.wait_ge(tanh_done, 2 * n + 1)
                    project(bank[0], P, COL_Q, z_t).then_inc(mm_q, 1)
                    pe.wait_ge(tanh_done, 2 * n + 2)
                    project(bank[1], REST, COL_Q + P, z_t).then_inc(mm_q, 1)
                    for pair in range(2):
                        pe.wait_ge(kg_done, 2 * n + pair + 1)
                        for t in (2 * pair, 2 * pair + 1):
                            o = bank[2 + pair][0:BLK, (t % 2) * D:(t % 2 + 1) * D]
                            mm = project_block(o, z_t, t, slice(COL_V, COL_V + D), first=(t % 2 == 0))
                        mm.then_inc(mm_v, 1)

                def front_state(n):
                    pe.wait_ge(kf_done, 2 * n + 2)
                    pe.wait_ge(qf_done, 2 * n + 2)
                    for t in range(N_BLK - 1):
                        b = slice(t * BLK, (t + 1) * BLK)
                        dst = bank[t // 2][0:BLK, (t % 2) * D:(t % 2 + 1) * D]
                        nc.tensor.transpose(dst[:, 0:P], kf[:, 0, b], ident[:])
                        mm = nc.tensor.transpose(dst[:, P:D], kf[0:REST, 1, b], ident[0:REST, 0:REST])
                    mm.then_inc(t_k, 1)
                    pe.wait_ge(v_done, 2 * n + 2)
                    pe.wait_ge(ktok_done, n + 1)
                    nm, nr = HEADS_MAIN * VA, (HEADS - HEADS_MAIN) * VA
                    for t in range(N_BLK - 1):
                        mm = nc.tensor.matmul(bank[2][:, t * nm:(t + 1) * nm], k_tok[:, t, 0:P],
                                              v_aug[:, t, 0:HEADS_MAIN, :], start=True, stop=True,
                                              skip_group_check=True)
                    mm.then_inc(mm_kv, 1)
                    for t in range(N_BLK - 1):
                        mm = nc.tensor.matmul(bank[3][0:REST, t * nr:(t + 1) * nr], k_tok[:, t, P:D],
                                              v_aug[:, t, HEADS_MAIN:HEADS, :], start=True, stop=True,
                                              skip_group_check=True)
                    mm.then_inc(mm_kv, 1)

                def scores(n, g):
                    t, grp = divmod(g, N_GRP)
                    b = slice(t * BLK, (t + 1) * BLK)
                    if g >= 2:
                        wait_probs(n, g - 2)
                    if g == 0:
                        pe.wait_ge(kh_dve, n + 1)
                    if g in (1, 2):
                        pe.wait_ge(kh_act, 2 * n + g)
                    for j in range(GRP):
                        h = grp * GRP + j
                        mm = nc.tensor.matmul(bank[4 + g % 2][0:BLK, j * BLK:(j + 1) * BLK], kh[:, h, b],
                                              qf[:, h // HEADS_MAIN, b], start=True, stop=True, skip_group_check=True)
                    mm.then_inc(scores_done, 1)

                def wait_probs(n, g):
                    if g % 2 == 0:
                        pe.wait_ge(probs_dve, n * (N_SC // 2) + g // 2 + 1)
                    else:
                        pe.wait_ge(probs_pool, n * (N_SC // 2) + g // 2 + 1)

                def attention(n):
                    pe.wait_ge(qf_done, 2 * n + 2)
                    scores(n, 0)
                    scores(n, 1)
                    pe.wait_ge(state_done, 2 * n + 2)
                    for t in range(N_BLK):
                        o = bank[6 + t % 2]
                        b = slice(t * BLK, (t + 1) * BLK)
                        nm = HEADS_MAIN * VA
                        if t >= 2:
                            pe.wait_ge(attn_done, n * N_BLK + t - 1)
                        nc.tensor.matmul(o[0:BLK, 0:nm], qf[:, 0, b], state[:, t, :], start=True, stop=False,
                                         skip_group_check=True)
                        nc.tensor.matmul(o[0:BLK, nm:HEADS * VA], qf[:, 1, b], state_r[:, t, :], start=False, stop=False,
                                         skip_group_check=True)
                        for grp in range(N_GRP):
                            g = t * N_GRP + grp
                            if g + 2 < N_SC:
                                scores(n, g + 2)
                            wait_probs(n, g)
                            for j in range(GRP):
                                h = grp * GRP + j
                                mm = nc.tensor.matmul(o[0:BLK, h * VA:(h + 1) * VA],
                                                      probs[:, g % 3, j * BLK:(j + 1) * BLK], v_aug[:, t, h, :],
                                                      start=False, stop=True, skip_group_check=True)
                        mm.then_inc(pv_done, 1)

                def attention_transpose(n):
                    pe.wait_ge(attn_done, N_BLK * n + N_BLK)
                    transpose_blocks(attn, None, bank[4], bank[5], t_a, lambda: None, lambda: None)

                def attention_project(n):
                    pe.wait_ge(lo_a, 2 * n + 2)
                    for t in range(N_BLK):
                        mm = project_block(bank[6 + t // 2][0:BLK, (t % 2) * D:(t % 2 + 1) * D], a_t, t,
                                           slice(COL_P, COL_P + D), first=(t % 2 == 0))
                        if t % 2:
                            mm.then_inc(mm_proj, 1)

                def tail_x(n):
                    pe.wait_ge(x2_done, n + 1)
                    transpose_blocks(x2, None, bank[4], bank[5], t_x, lambda: None, lambda: None)

                def tail_router(n):
                    pe.wait_ge(lo_x, 2 * n + 2)
                    for t in range(N_BLK):
                        mm = project_block(bank[6][0:BLK, t * N_EXP:(t + 1) * N_EXP], x_t, t,
                                           slice(COL_R, COL_R + N_EXP), first=(t == 0))
                    mm.then_inc(mm_rt, 1)

                def turn(n, nxt):
                    if n is not None:
                        attention(n)
                    if nxt is not None:
                        front_transpose(nxt)
                    if n is not None:
                        attention_transpose(n)
                    if nxt is not None:
                        front_gate(nxt)
                    if n is not None:
                        attention_project(n)
                    if nxt is not None:
                        front_k(nxt)
                    if n is not None:
                        tail_x(n)
                    if nxt is not None:
                        front_q(nxt)
                    if n is not None:
                        tail_router(n)
                    if nxt is not None:
                        front_state(nxt)
                    if n is not None:
                        pe.wait_ge(logits_done, n + 1)

                pe.wait_ge(loaded, 32)
                turn(None, 0)
                with pe.Fori(0, N_SEQ - 1) as n:
                    turn(n, n + 1)
                turn(N_SEQ - 1, None)

            @block.scalar
            def _(act):
                def hi_parts(src_main, src_rest, dst, ready, n, signal):
                    act.wait_ge(ready, 2 * n + 1)
                    nc.scalar.copy(dst[:, 0, :], src_main[:, 0:N_TOK]).then_inc(signal, 1)
                    act.wait_ge(ready, 2 * n + 2)
                    nc.scalar.copy(dst[0:REST, 2, :], src_rest[0:REST, 0:N_TOK]).then_inc(signal, 1)

                def attention(n):
                    for g in range(1, N_SC, 2):
                        act.wait_ge(scores_done, n * N_SC + g + 1)
                        nc.scalar.copy(probs[:, g % 3, :], bank[5][0:BLK, 0:GRP * BLK]).then_inc(probs_act, 1)

                def front_hi(n):
                    hi_parts(bank[0], bank[1], hn_t, t_hn, n, hi_hn)
                    hi_parts(bank[2], bank[3], z_t, t_z, n, hi_z)

                def front(n):
                    for half, (dst, m) in enumerate(halves(gate)):
                        act.wait_ge(mm_gk, 4 * n + half + 1)
                        nc.scalar.activation(dst, bank[half][0:m, 0:N_TOK], ACT.Tanh, bias=bgate_half[0:m, half:half + 1],
                                             scale=0.5).then_inc(tanh_done, 1)
                    for half, (dst, m) in enumerate(halves(k_exp)):
                        act.wait_ge(kg_done, 2 * n + half + 1)
                        nc.scalar.activation(dst, kg[0:m, half, :], ACT.Exp).then_inc(kexp_done, 1)

                def front_q(n):
                    for half, (dst, m) in enumerate(halves(q_exp)):
                        act.wait_ge(mm_q, 2 * n + half + 1)
                        act.wait_ge(kf_done, 2 * n + half + 1)
                        nc.scalar.activation(dst, bank[half][0:m, 0:N_TOK], ACT.Exp,
                                             bias=bqk[0:m, half:half + 1]).then_inc(qexp_done, 1)

                def head_rows(n, grp):
                    act.wait_ge(kf_done, 2 * n + (1 if grp == 1 else 2))
                    for h in range(grp * GRP, (grp + 1) * GRP):
                        half, m = (0, P) if h < HEADS_MAIN else (1, REST)
                        mask = (hm_main, hm_rest)[half]
                        j = h - half * HEADS_MAIN
                        ins = nc.scalar.activation(kh[0:m, h, :], kf[0:m, half, :], ACT.Copy, scale=mask[:, j:j + 1])
                    ins.then_inc(kh_act, 1)

                def front_state(n):
                    act.wait_ge(t_k, n + 1)
                    nc.scalar.copy(k_tok[:, 0:2, :], bank[0][0:BLK, 0:2 * D].rearrange("p (t d) -> p t d", t=2))
                    nc.scalar.copy(k_tok[:, 2, :], bank[1][0:BLK, 0:D]).then_inc(ktok_done, 1)

                def turn(n, nxt):
                    if n is not None:
                        attention(n)
                    if nxt is not None:
                        front_hi(nxt)
                    if n is not None:
                        hi_parts(bank[4], bank[5], a_t, t_a, n, hi_a)
                    if nxt is not None:
                        front(nxt)
                    if n is not None:
                        hi_parts(bank[4], bank[5], x_t, t_x, n, hi_x)
                    if nxt is not None:
                        head_rows(nxt, 1)
                        front_q(nxt)
                        front_state(nxt)
                        head_rows(nxt, 2)
                    if n is not None:
                        act.wait_ge(x_copied, 16 * n + 16)

                turn(None, 0)
                with act.Fori(0, N_SEQ - 1) as n:
                    turn(n, n + 1)
                turn(N_SEQ - 1, None)

            @block.vector
            def _(dve):
                LN_STEPS = 3
                LN_PER_SEQ = 3

                def norm_stats(src, which):
                    for t in range(N_BLK):
                        ins = nc.vector.bn_stats(stats[:, t, :], src(t))
                    ins.then_inc(chain, 1)
                    dve.wait_ge(chain, which * LN_STEPS + 1)
                    stand(dve, passed)
                    for t in range(N_BLK):
                        ins = nc.vector.bn_aggr(moments[:, t, :], stats[:, t, :])
                    ins.then_inc(chain, 1)
                    dve.wait_ge(chain, which * LN_STEPS + 2)
                    stand(dve, passed)
                    nc.vector.tensor_scalar(var_eps[:], moments[:, :, 1], LN_EPS, None, ALU.add).then_inc(centred, 1)

                def norm_apply(src, dst, which, signal):
                    dve.wait_ge(rooted, which + 1)
                    for t in range(N_BLK):
                        ins = nc.vector.tensor_scalar(dst[:, t, :], src(t), moments[:, t, 0:1], rstd[:, t:t + 1],
                                                      ALU.subtract, ALU.mult)
                        if t == N_BLK - 2:
                            ins.then_inc(chain, 1)
                    ins.then_inc(signal, 1)

                def lo_parts(src_main, src_rest, dst, hi_ready, n, signal):
                    dve.wait_ge(hi_ready, 2 * n + 1)
                    nc.vector.tensor_tensor(dst[:, 1, :], src_main[:, 0:N_TOK], dst[:, 0, :].bitcast(F32),
                                            ALU.subtract).then_inc(signal, 1)
                    dve.wait_ge(hi_ready, 2 * n + 2)
                    nc.vector.tensor_tensor(dst[REST:P, 2, :], src_rest[0:REST, 0:N_TOK], dst[0:REST, 2, :].bitcast(F32),
                                            ALU.subtract).then_inc(signal, 1)

                def norm_h_stats(n, which):
                    norm_stats(lambda t: h_all[:, n, t, :], which)

                def norm_h_apply(n, which):
                    at_least(dve, t_hn, 2 * n)
                    norm_apply(lambda t: h_all[:, n, t, :], hn, which, hn_done)

                def norm_hn_stats(n, which):
                    dve.wait_ge(hn_done, n + 1)
                    stand(dve, passed)
                    norm_stats(lambda t: hn[:, t, :], which + 1)

                def norm_hn_apply(n, which):
                    at_least(dve, t_z, 2 * n)
                    norm_apply(lambda t: hn[:, t, :], z, which + 1, z_done)

                pieces = [norm_h_stats, norm_h_apply, norm_hn_stats, norm_hn_apply]

                def normalize(n, t):
                    o = bank[6 + t % 2][0:BLK, 0:HEADS * VA].rearrange("p (h e) -> p h e", e=VA)
                    dve.wait_ge(pv_done, N_BLK * n + t + 1)
                    nc.vector.tensor_scalar(den[:], o[:, :, DH], 1e-6, None, ALU.add).then_inc(den_done, 1)
                    dve.wait_ge(den_done, N_BLK * n + t + 1)
                    nc.vector.reciprocal(rden[:], den[:]).then_inc(rden_done, 1)
                    dve.wait_ge(rden_done, N_BLK * n + t + 1)
                    nc.vector.tensor_tensor(attn[:, t, :].rearrange("p (h e) -> p h e", e=DH), o[:, :, 0:DH],
                                            rden[:].unsqueeze(2).broadcast_to((BLK, HEADS, DH)),
                                            ALU.mult).then_inc(attn_done, 1)

                def attention(n, nxt, which):
                    for g in range(N_SC):
                        if g % 2 == 0:
                            dve.wait_ge(scores_done, n * N_SC + g + 1)
                            nc.vector.tensor_tensor(probs[:, g % 3, :].rearrange("p (j l) -> p j l", j=GRP),
                                                    bank[4][0:BLK, 0:GRP * BLK].rearrange("p (j l) -> p j l", j=GRP),
                                                    causal[:].unsqueeze(1).broadcast_to((BLK, GRP, BLK)),
                                                    ALU.mult).then_inc(probs_dve, 1)
                        if g % N_GRP == 1 and g > N_GRP:
                            normalize(n, g // N_GRP - 1)
                        if g in (2, 4, 6, 8) and nxt is not None:
                            pieces[g // 2 - 1](nxt, which)
                    normalize(n, N_BLK - 1)

                def attention_out(n):
                    lo_parts(bank[4], bank[5], a_t, hi_a, n, lo_a)
                    dve.wait_ge(hb_done, n + 1)
                    for pair in range(2):
                        dve.wait_ge(mm_proj, 2 * n + pair + 1)
                        ts = slice(2 * pair, 2 * pair + 2)
                        nc.vector.tensor_tensor(h_all[:, n, ts, :],
                                                bank[6 + pair][0:BLK, 0:2 * D].rearrange("p (t d) -> p t d", t=2),
                                                hb[:, ts, :], ALU.add).then_inc(h_done, 1)

                def front(n):
                    lo_parts(bank[0], bank[1], hn_t, hi_hn, n, lo_hn)
                    lo_parts(bank[2], bank[3], z_t, hi_z, n, lo_z)

                def front_k(n):
                    for half, (dst, m) in enumerate(halves(gate)):
                        dve.wait_ge(tanh_done, 2 * n + half + 1)
                        nc.vector.tensor_scalar(dst, dst, 0.5, 0.5, ALU.mult, ALU.add).then_inc(gate_done, 1)
                    for half, (dst, m) in enumerate(halves(kg)):
                        dve.wait_ge(gate_done, 2 * n + half + 1)
                        dve.wait_ge(mm_gk, 4 * n + half + 3)
                        nc.vector.scalar_tensor_tensor(dst, bank[2 + half][0:m, 0:N_TOK], bqk[0:m, 2 + half:3 + half],
                                                       gate[0:m, half, :], ALU.add, ALU.mult).then_inc(kg_done, 1)
                    for half, (dst, m) in enumerate(halves(k_pos)):
                        dve.wait_ge(kg_done, 2 * n + half + 1)
                        nc.vector.tensor_scalar(dst, kg[0:m, half, :], 0.0, None, ALU.max).then_inc(kpos_done, 1)
                    for half, (dst, m) in enumerate(halves(kf)):
                        dve.wait_ge(kexp_done, 2 * n + half + 1)
                        dve.wait_ge(kpos_done, 2 * n + half + 1)
                        nc.vector.scalar_tensor_tensor(dst, k_exp[0:m, half, :], 1.0, k_pos[0:m, half, :],
                                                       ALU.min, ALU.add).then_inc(kf_done, 1)
                    dve.wait_ge(kf_done, 2 * n + 1)
                    for h in range(GRP):
                        ins = nc.vector.tensor_scalar(kh[:, h, :], kf[:, 0, :], hm_main[:, h:h + 1], None, ALU.mult)
                    ins.then_inc(kh_dve, 1)

                def front_q(n):
                    for half, (dst, m) in enumerate(halves(q_pos)):
                        dve.wait_ge(qexp_done, 2 * n + half + 1)
                        nc.vector.tensor_scalar(dst, bank[half][0:m, 0:N_TOK], bqk[0:m, half:half + 1], 0.0,
                                                ALU.add, ALU.max).then_inc(qpos_done, 1)
                        dve.wait_ge(qpos_done, 2 * n + half + 1)
                        nc.vector.scalar_tensor_tensor(qf[0:m, half, :], q_exp[0:m, half, :], 1.0, dst, ALU.min,
                                                       ALU.add).then_inc(qf_done, 1)
                    for pair in range(2):
                        dve.wait_ge(mm_v, 2 * n + pair + 1)
                        for t in (2 * pair, 2 * pair + 1):
                            ins = nc.vector.tensor_tensor(
                                v_aug[:, t, :, 0:DH],
                                bank[2 + pair][0:BLK, (t % 2) * D:(t % 2 + 1) * D].rearrange("p (h e) -> p h e", e=DH),
                                bv_bc[:].rearrange("p (h e) -> p h e", e=DH), ALU.add)
                        ins.then_inc(v_done, 1)

                def front_state(n):
                    for half, (dst, heads, mask, m) in enumerate([
                            (state, HEADS_MAIN, hm_main, P), (state_r, HEADS - HEADS_MAIN, hm_rest, REST)]):
                        dve.wait_ge(mm_kv, 2 * n + half + 1)
                        for t in range(N_BLK - 1):
                            ins = nc.vector.tensor_tensor(
                                dst[0:m, t + 1, :].rearrange("p (h e) -> p h e", e=VA),
                                bank[2 + half][0:m, t * heads * VA:(t + 1) * heads * VA].rearrange(
                                    "p (h e) -> p h e", e=VA),
                                mask[:].unsqueeze(2).broadcast_to((m, heads, VA)), ALU.mult)
                        ins.then_inc(masked, 1)
                    for t in range(1, N_BLK - 1):
                        dve.wait_ge(masked, 4 * n + 2 * t)
                        ins = nc.vector.tensor_tensor(state[:, t + 1, :], state[:, t + 1, :], state[:, t, :], ALU.add)
                        if t == 1:
                            ins.then_inc(masked, 1)
                        ins2 = nc.vector.tensor_tensor(state_r[0:REST, t + 1, :], state_r[0:REST, t + 1, :],
                                                       state_r[0:REST, t, :], ALU.add)
                        if t == 1:
                            ins2.then_inc(masked, 1)
                    ins.then_inc(state_done, 1)
                    ins2.then_inc(state_done, 1)

                def turn(n, nxt):
                    if n is None:
                        for piece in pieces:
                            piece(nxt, 0)
                    else:
                        attention(n, nxt, LN_PER_SEQ * n + 2)
                    if nxt is not None:
                        front(nxt)
                    if n is not None:
                        attention_out(n)
                        dve.wait_ge(h_done, 2 * n + 2)
                        stand(dve, passed)
                        which = LN_PER_SEQ * n + (4 if nxt is not None else 2)
                        norm_stats(lambda t: h_all[:, n, t, :], which)
                        norm_apply(lambda t: h_all[:, n, t, :], x2, which, x2_done)
                    if nxt is not None:
                        front_k(nxt)
                    if n is not None:
                        lo_parts(bank[4], bank[5], x_t, hi_x, n, lo_x)
                    if nxt is not None:
                        front_q(nxt)
                    if n is not None:
                        dve.wait_ge(mm_rt, n + 1)
                        nc.vector.tensor_copy(logits[:, bass.ds(n * N_BLK, N_BLK), :],
                                              bank[6][0:BLK, 0:N_BLK * N_EXP].rearrange("p (t e) -> p t e", e=N_EXP)
                                              ).then_inc(logits_done, 1)
                    if nxt is not None:
                        front_state(nxt)

                dve.wait_ge(loaded, 32)
                turn(None, 0)
                with dve.Fori(0, N_SEQ - 1) as n:
                    turn(n, n + 1)
                turn(N_SEQ - 1, None)

            @block.gpsimd
            def _(pool):
                def root(which):
                    pool.wait_ge(centred, which + 1)
                    nc.gpsimd.tensor_tensor(rstd[:], var_eps[:], minus_half[:], ALU.pow).then_inc(rooted, 1)

                def attention(n, nxt):
                    for g in range(1, N_SC, 2):
                        if g in (5, 9) and nxt is not None:
                            root(3 * n + (2 if g == 5 else 3))
                        pool.wait_ge(probs_act, n * (N_SC // 2) + g // 2 + 1)
                        p3 = probs[:, g % 3, :].rearrange("p (j l) -> p j l", j=GRP)
                        nc.gpsimd.tensor_tensor(p3, p3, causal[:].unsqueeze(1).broadcast_to((BLK, GRP, BLK)),
                                                ALU.mult).then_inc(probs_pool, 1)

                def residual(n):
                    at_least(pool, h_done, 2 * n)
                    nc.gpsimd.tensor_tensor(hb[:], h_all[:, n, :, :],
                                            bproj_bc[:].unsqueeze(1).broadcast_to((BLK, N_BLK, D)),
                                            ALU.add).then_inc(hb_done, 1)

                def turn(n, nxt):
                    if n is None:
                        root(0)
                        root(1)
                    else:
                        attention(n, nxt)
                        root(3 * n + (4 if nxt is not None else 2))
                    if nxt is not None:
                        residual(nxt)

                pool.wait_ge(loaded, 32)
                turn(None, 0)
                with pool.Fori(0, N_SEQ - 1) as n:
                    turn(n, n + 1)
                turn(N_SEQ - 1, None)


def moe_stage(nc, passed, sem, bank, h_all, x_all, logits, comb, stage_up, stage_down, stage_in, load_expert,
              exp_bias, out):
    N_ROW = N_SEQ * N_BLK
    with ExitStack() as ctx:
        def sb(name, shape, dt=F32):
            return ctx.enter_context(nc.sbuf_tensor(name, shape, dt))

        up_hi = sb("up_hi", [P, 2, 2, 2 * F], F32R)
        up_lo = sb("up_lo", [P, 2, 2, 2 * F], F32R)
        down_hi = sb("down_hi", [P, 2, N_CHUNK, D], F32R)
        down_lo = sb("down_lo", [P, 2, N_CHUNK, D], F32R)
        silu = sb("silu", [P, 2, N_TOK])
        prod = sb("prod", [P, 2, N_TOK])
        hid_hi = sb("hid_hi", [P, 2, N_CHUNK, N_TOK], F32R)
        hid_lo = sb("hid_lo", [P, 2, N_CHUNK, N_TOK], F32R)
        bias_bc = sb("bias_bc", [BLK, N_EXP])
        earlier = sb("earlier", [BLK, N_EXP, N_EXP])
        row = sb("row", [BLK, N_ROW])
        row2 = sb("row2", [BLK, N_ROW])
        expd = sb("expd", [BLK, N_ROW, N_EXP])
        picks = sb("picks", [BLK, N_ROW, N_EXP])
        above = sb("above", [BLK, N_SEQ, N_BLK * N_EXP * N_EXP])
        equal = sb("equal", [BLK, N_SEQ, N_BLK * N_EXP * N_EXP])

        bias_in, tri_made, split_hi, split_lo = sem("bias_in"), sem("tri_made"), sem("e_split_hi"), sem("e_split_lo")
        mm_up, silu_done, prod_done, hid_hi_done, hid_lo_done = (sem("mm_up"), sem("silu_done"), sem("prod_done"),
                                                                 sem("hid_hi_done"), sem("hid_lo_done"))
        mm_down, added, stored, soft_in, soft_exp, order = (sem("mm_down"), sem("added"), sem("stored"), sem("soft_in"),
                                                            sem("soft_exp"), sem("order"))
        N_STEP = (N_EXP + 1) * N_SEQ

        def over_steps(engine, step, split, last):
            def expert(e, par):
                m = e * N_SEQ
                step(m, e, 0, par, par ^ 1, isinstance(e, int) and e == 0)
                step(m + 1, e, 1, par, par, False)
                split(e, par)
                with engine.Fori(1, N_SEQ // 2) as i:
                    step(m + 2 * i, e, 2 * i, par, par, False, par_s=0)
                    step(m + 2 * i + 1, e, 2 * i + 1, par, par, False, par_s=1)

            expert(0, 0)
            with engine.Fori(0, N_EXP // 2) as i:
                expert(2 * i + 1, 1)
                expert(2 * i + 2, 0)
            last()

        with nc.Block() as block:
            @block.sync
            def _(sp):
                sp.dma_start(bias_bc[:], exp_bias.partition_broadcast(BLK)).then_inc(bias_in, 16)
                with sp.Fori(1, N_EXP + 1) as e:
                    sp.wait_ge(split_lo, e)
                    stand(sp, passed)
                    load_expert(sp, e)
                with sp.Fori(0, N_SEQ) as s:
                    sp.wait_ge(added, N_EXP * N_SEQ + s + 1)
                    stand(sp, passed)
                    sp.dma_start(out[s].rearrange("(t p) d -> p t d", p=BLK), h_all[:, s, :, :]).then_inc(stored, 16)
                sp.wait_ge(stored, 16 * N_SEQ)

            @block.gpsimd
            def _(pool):
                nc.gpsimd.memset(earlier[:], 1.0).then_inc(tri_made, 1)
                pool.wait_ge(tri_made, 1)
                nc.gpsimd.affine_select(out=earlier[:], in_=earlier[:], compare_op=ALU.is_ge, fill=0.0, base=-1,
                                        pattern=[[1, N_EXP], [-1, N_EXP]], channel_multiplier=0).then_inc(tri_made, 1)

            @block.tensor
            def _(pe):
                def gate_up(m, f, par, s, first):
                    at_least(pe, prod_done, m * N_CHUNK + f - N_CHUNK + 1)
                    x = [x_all[:, s, i, :] for i in range(3)]
                    for which in range(2):
                        o = bank[2 * f + which][:, 0:N_TOK]
                        c = slice(which * F + f * P, which * F + (f + 1) * P)
                        nc.tensor.matmul(o, up_hi[:, par, 0, c], x[0], start=True, stop=False)
                        nc.tensor.matmul(o, up_hi[:, par, 0, c], x[1], start=False, stop=False)
                        nc.tensor.matmul(o, up_lo[:, par, 0, c], x[0], start=False, stop=False)
                        nc.tensor.matmul(o, up_hi[:, par, 1, c], x[2], start=False, stop=False)
                        mm = nc.tensor.matmul(o, up_lo[:, par, 1, c], x[2], start=False, stop=True)
                    mm.then_inc(mm_up, 1)

                def down(m, hp, par):
                    at_least(pe, added, m)
                    pe.wait_ge(hid_lo_done, N_CHUNK * m + N_CHUNK)
                    for t in range(N_BLK):
                        o = bank[6 + t // 2][0:BLK, (t % 2) * D:(t % 2 + 1) * D]
                        b = slice(t * BLK, (t + 1) * BLK)
                        for f in range(N_CHUNK):
                            nc.tensor.matmul(o, hid_hi[:, hp, f, b], down_hi[:, par, f, :],
                                             start=(f == 0 and t % 2 == 0), stop=False, skip_group_check=True)
                            nc.tensor.matmul(o, hid_hi[:, hp, f, b], down_lo[:, par, f, :], start=False, stop=False,
                                             skip_group_check=True)
                            mm = nc.tensor.matmul(o, hid_lo[:, hp, f, b], down_hi[:, par, f, :], start=False,
                                                  stop=(f == N_CHUNK - 1), skip_group_check=True)
                    mm.then_inc(mm_down, 1)

                def step(m, e, s, par, prev_par, first, par_s=None):
                    ps = s % 2 if par_s is None else par_s
                    if par_s is None and ps == 0:
                        pe.wait_ge(split_lo, e + 1)
                    gate_up(m, 0, par, s, first)
                    gate_up(m, 1, par, s, first)
                    if not first:
                        down(m - 1, ps ^ 1, prev_par)
                    gate_up(m, 2, par, s, first)

                over_steps(pe, step, lambda e, par: None, lambda: down(N_STEP - 1, 1, 0))

            @block.scalar
            def _(act):
                def split(e, par):
                    if isinstance(e, int) or par == 1:
                        split_one(e + 1, par ^ 1)
                    else:
                        with act.If(e < N_EXP):
                            split_one(e + 1, par ^ 1)

                def split_one(e, par):
                    act.wait_ge(stage_in, 64 * e + 64)
                    if not (isinstance(e, int) and e < 2):
                        act.wait_ge(mm_down, (e - 1) * N_SEQ)
                    nc.scalar.copy(up_hi[:, par, 0, :], stage_up[:, 0, :])
                    nc.scalar.copy(up_hi[:, par, 1, :], stage_up[:, 1, :])
                    nc.scalar.copy(down_hi[:, par, :, :], stage_down[:]).then_inc(split_hi, 1)

                def step(m, e, s, par, prev_par, first, par_s=None):
                    ps = s % 2 if par_s is None else par_s
                    for f in range(N_CHUNK):
                        g = N_CHUNK * ps + f
                        c = m * N_CHUNK + f
                        act.wait_ge(mm_up, c + 1)
                        at_least(act, prod_done, c - 1)
                        nc.scalar.activation(silu[:, g % 2, :], bank[2 * f][:, 0:N_TOK], ACT.Silu).then_inc(silu_done, 1)
                        if f == 0 and m_zero(m):
                            continue
                        hi(c - 1, (g - 1) % 2, (ps if f else ps ^ 1), (f - 1) % N_CHUNK)

                def m_zero(m):
                    return isinstance(m, int) and m == 0

                def hi(c, ring, hp, f):
                    act.wait_ge(prod_done, c + 1)
                    if not (isinstance(c, int) and c < 2 * N_CHUNK):
                        act.wait_ge(mm_down, c_step(c, f) - 1)
                    nc.scalar.copy(hid_hi[:, hp, f, :], prod[:, ring, :]).then_inc(hid_hi_done, 1)

                def c_step(c, f):
                    return step_of[0] if f != N_CHUNK - 1 else step_of[0] - 1

                step_of = [0]

                def counted(m, *a, **k):
                    step_of[0] = m
                    step(m, *a, **k)

                split_one(0, 0)
                act.wait_ge(soft_in, 1)
                nc.scalar.activation(expd[:], expd[:], ACT.Exp).then_inc(soft_exp, 1)

                def last():
                    step_of[0] = N_STEP
                    hi(N_STEP * N_CHUNK - 1, 1, 1, N_CHUNK - 1)

                over_steps(act, counted, split, last)

            @block.vector
            def _(dve):
                done = [0]

                def then(ins):
                    done[0] += 1
                    ins.then_inc(order, 1)
                    dve.wait_ge(order, done[0])

                def split(e, par):
                    if isinstance(e, int) or par == 1:
                        split_one(e + 1, par ^ 1)
                    else:
                        with dve.If(e < N_EXP):
                            split_one(e + 1, par ^ 1)

                def split_one(e, par):
                    dve.wait_ge(split_hi, e + 1)
                    nc.vector.tensor_tensor(up_lo[:, par, 0, :], stage_up[:, 0, :], up_hi[:, par, 0, :].bitcast(F32),
                                            ALU.subtract)
                    nc.vector.tensor_tensor(up_lo[:, par, 1, :], stage_up[:, 1, :], up_hi[:, par, 1, :].bitcast(F32),
                                            ALU.subtract)
                    nc.vector.tensor_tensor(down_lo[:, par, :, :], stage_down[:], down_hi[:, par, :, :].bitcast(F32),
                                            ALU.subtract).then_inc(split_lo, 1)

                split_one(0, 0)
                wide = lambda r: r[:].unsqueeze(2).broadcast_to((BLK, N_ROW, N_EXP))
                then(nc.vector.tensor_reduce(row[:], logits[:], axis=AX.X, op=ALU.max))
                nc.vector.tensor_tensor(expd[:], logits[:], wide(row), ALU.subtract).then_inc(soft_in, 1)
                dve.wait_ge(soft_exp, 1)
                then(nc.vector.tensor_reduce(row[:], expd[:], axis=AX.X, op=ALU.add))
                then(nc.vector.reciprocal(row2[:], row[:]))
                then(nc.vector.tensor_tensor(expd[:], expd[:], wide(row2), ALU.mult))
                dve.wait_ge(bias_in, 16)
                then(nc.vector.tensor_tensor(picks[:], expd[:], bias_bc[:].unsqueeze(1).broadcast_to(
                    (BLK, N_ROW, N_EXP)), ALU.add))
                dve.wait_ge(tri_made, 2)
                for r in range(N_ROW):
                    b, t = divmod(r, N_BLK)
                    c = slice(t * N_EXP * N_EXP, (t + 1) * N_EXP * N_EXP)
                    mine = picks[:, r, :].unsqueeze(2).broadcast_to((BLK, N_EXP, N_EXP))
                    other = picks[:, r, :].unsqueeze(1).broadcast_to((BLK, N_EXP, N_EXP))
                    nc.vector.tensor_tensor(above[:, b, c].rearrange("p (e j) -> p e j", e=N_EXP), other, mine, ALU.is_gt)
                    ins = nc.vector.tensor_tensor(equal[:, b, c].rearrange("p (e j) -> p e j", e=N_EXP), other, mine,
                                                  ALU.is_equal)
                then(ins)
                eq4 = equal[:].rearrange("p b (t x) -> p (b t) x", t=N_BLK)
                ab4 = above[:].rearrange("p b (t x) -> p (b t) x", t=N_BLK)
                then(nc.vector.tensor_tensor(eq4, eq4, earlier[:].rearrange("p e j -> p (e j)").unsqueeze(1).broadcast_to(
                    (BLK, N_ROW, N_EXP * N_EXP)), ALU.mult))
                then(nc.vector.tensor_tensor(ab4, ab4, eq4, ALU.add))
                then(nc.vector.tensor_reduce(picks[:], above[:].rearrange("p b (t e j) -> p (b t) e j", t=N_BLK, e=N_EXP),
                                             axis=AX.X, op=ALU.add))
                then(nc.vector.tensor_scalar(picks[:], picks[:], 1.5, None, ALU.is_lt))
                then(nc.vector.tensor_tensor(picks[:], picks[:], expd[:], ALU.mult))
                then(nc.vector.tensor_reduce(row[:], picks[:], axis=AX.X, op=ALU.add))
                then(nc.vector.tensor_scalar(row[:], row[:], 1e-9, None, ALU.add))
                then(nc.vector.reciprocal(row2[:], row[:]))
                nc.vector.memset(comb[:, 0, :], 1.0)
                then(nc.vector.tensor_tensor(comb[:, 1:1 + N_EXP, :].rearrange("p e r -> p r e"), picks[:], wide(row2),
                                             ALU.mult))

                def lo(c, ring, hp, f):
                    dve.wait_ge(hid_hi_done, c + 1)
                    nc.vector.tensor_tensor(hid_lo[:, hp, f, :], prod[:, ring, :], hid_hi[:, hp, f, :].bitcast(F32),
                                            ALU.subtract).then_inc(hid_lo_done, 1)

                def add_output(m, s, e):
                    dve.wait_ge(mm_down, m + 1)
                    for t in range(N_BLK):
                        y = bank[6 + t // 2][0:BLK, (t % 2) * D:(t % 2 + 1) * D]
                        h = h_all[:, s, t, :]
                        ins = nc.vector.scalar_tensor_tensor(h, y, comb[:, e, bass.ds(s * N_BLK + t, 1)], h,
                                                             ALU.mult, ALU.add)
                    ins.then_inc(added, 1)

                def step(m, e, s, par, prev_par, first, par_s=None):
                    ps = s % 2 if par_s is None else par_s
                    for f in range(N_CHUNK):
                        g = N_CHUNK * ps + f
                        c = m * N_CHUNK + f
                        dve.wait_ge(silu_done, c + 1)
                        at_least(dve, hid_lo_done, c - 1)
                        nc.vector.tensor_tensor(prod[:, g % 2, :], silu[:, g % 2, :], bank[2 * f + 1][:, 0:N_TOK],
                                                ALU.mult).then_inc(prod_done, 1)
                        if not (first and f == 0):
                            lo(c - 1, (g - 1) % 2, (ps if f else ps ^ 1), (f - 1) % N_CHUNK)
                        if f == 1 and not first:
                            if par_s is None and ps == 0:
                                add_output(m - 1, N_SEQ - 1, e - 1)
                            else:
                                add_output(m - 1, s - 1, e)

                def last():
                    c = N_STEP * N_CHUNK - 1
                    lo(c, 1, 1, N_CHUNK - 1)
                    add_output(N_STEP - 1, N_SEQ - 1, N_EXP)

                over_steps(dve, step, split, last)


_IN_ORDER = ["frames", "dft", "mel2", "dct", "w_mfcc", "b_tok", "w_pack", "b_qk_col", "b_v", "b_gate_col", "ln_b_col",
             "ln_g_col", "b_proj", "head_main", "head_rest", "exp_bias", "w_up", "w_down"]


def lay_out(x, L0_tok_mel_filters, L0_tok_dct, L0_tok_w_proj, L0_tok_b_proj, L0_attn_W_qkv, L0_attn_b_qkv,
            L0_attn_W_gate, L0_attn_b_gate, L0_attn_W_proj, L0_attn_b_proj, L0_attn_ln_g, L0_attn_ln_b,
            L0_ffn_w_router, L0_ffn_expert_bias, L0_ffn_Wg, L0_ffn_Wu, L0_ffn_Wd, L0_ffn_sg, L0_ffn_su, L0_ffn_sd):
    k = np.arange(N_BINS)[None, :]
    j = np.arange(FRAME)[:, None]
    window = (0.54 - 0.46 * np.cos(2.0 * np.pi * j / (FRAME - 1)))
    angle = 2.0 * np.pi * ((j * k) % FRAME) / FRAME
    dft = np.concatenate([window * np.cos(angle), -window * np.sin(angle)], axis=1).astype(np.float32)
    head_of = np.arange(P)[:, None] // DH
    return {
        "frames": x.reshape(N_SEQ, N_TOK, STEP)[:, :, :FRAME].transpose(2, 0, 1),
        "dft": dft,
        "mel2": np.concatenate([L0_tok_mel_filters.T, L0_tok_mel_filters.T], axis=0),
        "dct": L0_tok_dct,
        "w_mfcc": L0_tok_w_proj,
        "b_tok": L0_tok_b_proj.reshape(1, D),
        "w_pack": np.concatenate([L0_attn_W_qkv, L0_attn_W_gate, L0_attn_W_proj, L0_ffn_w_router.T], axis=1),
        "b_qk_col": L0_attn_b_qkv[:2 * D].reshape(2 * D, 1),
        "b_v": L0_attn_b_qkv[2 * D:],
        "b_gate_col": L0_attn_b_gate.reshape(D, 1),
        "ln_b_col": L0_attn_ln_b.reshape(D, 1),
        "ln_g_col": L0_attn_ln_g.reshape(D, 1),
        "b_proj": L0_attn_b_proj,
        "head_main": (head_of == np.arange(HEADS_MAIN)[None, :]).astype(np.float32),
        "head_rest": (head_of[:REST] == np.arange(HEADS - HEADS_MAIN)[None, :]).astype(np.float32),
        "exp_bias": L0_ffn_expert_bias,
        "w_up": np.concatenate([
            np.concatenate([L0_ffn_sg[None], L0_ffn_Wg], axis=0).transpose(0, 2, 1),
            np.concatenate([L0_ffn_su[None], L0_ffn_Wu], axis=0).transpose(0, 2, 1)], axis=2),
        "w_down": np.concatenate([L0_ffn_sd[None], L0_ffn_Wd], axis=0).transpose(0, 2, 1).reshape(
            N_EXP + 1, N_CHUNK, P, D).transpose(0, 2, 1, 3),
    }


def kernel(**inputs):
    import concourse.bacc as bacc
    from concourse.bass_utils import run_bass_kernel_spmd

    nc = bacc.Bacc("TRN2", target_bir_lowering=False, num_devices=1)
    laid = lay_out(**{name: np.asarray(a) for name, a in inputs.items()})
    arrays, args = {}, []
    for name in _IN_ORDER:
        a = np.ascontiguousarray(laid[name])
        arrays[f"in_{name}"] = a
        args.append(nc.dram_tensor(f"in_{name}", a.shape, mybir.dt.from_np(a.dtype), kind="ExternalInput").ap())
    out = nc.dram_tensor("out_dram", (N_SEQ, N_TOK, D), F32, kind="ExternalOutput").ap()
    build(nc, *args, out)
    got = run_bass_kernel_spmd(nc, [arrays], core_ids=[0])
    return got.results[0]["out_dram"]
```

```python
from contextlib import ExitStack

import numpy as np

import concourse.bass as bass
from concourse import mybir

F32 = mybir.dt.float32
F32R = mybir.dt.float32r
I32 = mybir.dt.int32
ACT = mybir.ActivationFunctionType
ALU = mybir.AluOpType
AX = mybir.AxisListType

P = 128
N_SEQ = 8
FRAME = 100
STEP = 160
N_TOK = 500
N_BLK = 4
BLK = N_TOK // N_BLK
D = 192
REST = D - P
HEADS = 12
DH = D // HEADS
HEADS_MAIN = P // DH
N_MEL = 40
N_BINS = FRAME // 2 + 1
N_MFCC = 13
N_EXP = 8
F = 384
N_CHUNK = F // P
LN_EPS = 1e-5
VA = DH + 1
GRP = 4
N_GRP = HEADS // GRP
COL_Q, COL_K, COL_V, COL_G, COL_P, COL_R = 0, D, 2 * D, 3 * D, 4 * D, 5 * D
N_PACK = 5 * D + N_EXP
TOP = 2
N_ROW = N_SEQ * N_BLK
N_ALL = N_SEQ * N_TOK
N_TILE = (TOP * N_ALL + N_EXP * (P - 1)) // P
N_META = 2
NOWHERE = 1 << 29


def at_least(engine, semaphore, value):
    if not isinstance(value, int) or value > 0:
        engine.wait_ge(semaphore, value)


def stand(engine, passed):
    engine.sem_inc(passed, 1)


def build(nc, frames, dft, mel2, dct, w_mfcc, b_tok, w_pack, b_qk_col, b_v, b_gate_col, ln_b_col, ln_g_col,
          b_proj, head_main, head_rest, exp_bias, w_up, w_down, out):
    with ExitStack() as ctx:
        def sb(name, shape, dt=F32):
            return ctx.enter_context(nc.sbuf_tensor(name, shape, dt))

        def sem(name):
            return ctx.enter_context(nc.semaphore(name))

        bank = [ctx.enter_context(nc.psum_tensor(f"bank{i}", [P, 512], F32)) for i in range(8)]

        h_all = sb("h_all", [BLK, N_SEQ, N_BLK, D])
        logits = sb("logits", [BLK, N_ROW, N_EXP])
        ident = sb("ident", [P, P])
        stage_up = sb("stage_up", [P, 2, 2 * F])
        stage_down = sb("stage_down", [P, N_CHUNK, D])
        stage_in = sem("stage_in")
        x_dram = nc.dram_tensor("x_dram", (N_ALL, D), F32).ap()
        slots_dram = nc.dram_tensor("slots_dram", (N_TILE * P, D + N_META), F32).ap()
        y_dram = nc.dram_tensor("y_dram", (N_ALL * TOP, D), F32).ap()
        passed = sem("passed")
        loaded = sem("loaded")
        made = sem("made")

        def load_expert(sp, e):
            sp.dma_start(stage_up[:, 0, :], w_up[e, 0:P, :]).then_inc(stage_in, 16)
            sp.dma_start(stage_up[0:REST, 1, :], w_up[e, P:D, :]).then_inc(stage_in, 16)
            sp.dma_start(stage_up[REST:P, 1, :], w_up[e, P:D, :]).then_inc(stage_in, 16)
            sp.dma_start(stage_down[:], w_down[e]).then_inc(stage_in, 16)

        attn_stage(nc, passed, sem, bank, h_all, x_dram, slots_dram, logits, ident, made, loaded, load_expert,
                   frames, dft, mel2, dct, w_mfcc, b_tok, w_pack, b_qk_col, b_v, b_gate_col, ln_b_col, ln_g_col,
                   b_proj, head_main, head_rest)
        moe_stage(nc, passed, sem, bank, h_all, x_dram, slots_dram, y_dram, logits, ident, stage_up, stage_down,
                  stage_in, load_expert, exp_bias)
        final_stage(nc, sem, h_all, y_dram, out)


def attn_stage(nc, passed, sem, bank, h_all, x_dram, slots_dram, logits, ident, made, loaded, load_expert,
               frames, dft, mel2, dct, w_mfcc, b_tok, w_pack, b_qk_col, b_v, b_gate_col, ln_b_col, ln_g_col, b_proj, head_main,
               head_rest):
    with ExitStack() as ctx:
        def sb(name, shape, dt=F32):
            return ctx.enter_context(nc.sbuf_tensor(name, shape, dt))

        pack_raw = sb("pack_raw", [P, 2, N_PACK])
        pack_hi = sb("pack_hi", [P, 2, N_PACK], F32R)
        pack_lo = sb("pack_lo", [P, 2, N_PACK], F32R)
        ln_b = sb("ln_b", [P, 2])
        ln_g = sb("ln_g", [P, 2])
        ln_b_wide = sb("ln_b_wide", [P, 2, BLK])
        bqk = sb("bqk", [P, 4])
        bgate = sb("bgate", [P, 2])
        bgate_half = sb("bgate_half", [P, 2])
        bv_bc = sb("bv_bc", [BLK, D])
        bproj_bc = sb("bproj_bc", [BLK, D])
        causal = sb("causal", [BLK, BLK])
        hm_main = sb("hm_main", [P, HEADS_MAIN])
        hm_rest = sb("hm_rest", [REST, HEADS - HEADS_MAIN])
        minus_half = sb("minus_half", [BLK, N_BLK])
        empty_slot = sb("empty_slot", [P, D + N_META])
        ln_eps_tile = sb("log_eps", [P, 1])

        stats = sb("stats", [BLK, N_BLK, 6])
        moments = sb("moments", [BLK, N_BLK, 2])
        var_eps = sb("var_eps", [BLK, N_BLK])
        rstd = sb("rstd", [BLK, N_BLK])
        hn = sb("hn", [BLK, N_BLK, D])
        z = sb("z", [BLK, N_BLK, D])
        x2 = sb("x2", [BLK, N_BLK, D])
        hb = sb("hb", [BLK, N_BLK, D])
        hn_t = sb("hn_t", [P, 3, N_TOK], F32R)
        z_t = sb("z_t", [P, 3, N_TOK], F32R)
        a_t = sb("a_t", [P, 3, N_TOK], F32R)
        x_t = a_t
        gate = sb("gate", [P, 2, N_TOK])
        kg = sb("kg", [P, 2, N_TOK])
        k_exp = sb("k_exp", [P, 2, N_TOK])
        k_pos = sb("k_pos", [P, 2, N_TOK])
        kf = sb("kf", [P, 2, N_TOK])
        kh = sb("kh", [P, HEADS, N_TOK])
        q_exp, q_pos = k_exp, k_pos
        qf = sb("qf", [P, 2, N_TOK])
        v_aug = sb("v_aug", [BLK, N_BLK, HEADS, VA])
        k_tok = sb("k_tok", [BLK, N_BLK - 1, D])
        state = sb("state", [P, N_BLK, HEADS_MAIN * VA])
        state_r = sb("state_r", [P, N_BLK, (HEADS - HEADS_MAIN) * VA])
        probs = pack_raw[0:BLK, :, :].rearrange("p a c -> p (a c)")[:, 0:3 * GRP * BLK].rearrange(
            "p (r c) -> p r c", r=3)
        den = sb("den", [BLK, HEADS])
        rden = sb("rden", [BLK, HEADS])
        attn = sb("attn", [BLK, N_BLK, D])

        with ExitStack() as tok_ctx:
            def tok_sb(name, shape, dt=F32):
                return tok_ctx.enter_context(nc.sbuf_tensor(name, shape, dt))

            fr = kh[0:FRAME, 0:N_SEQ, :]
            dft_sb = tok_sb("dft_sb", [FRAME, 2 * N_BINS])
            mel_sb = tok_sb("mel_sb", [2 * N_BINS, N_MEL])
            dct_sb = tok_sb("dct_sb", [N_MFCC, N_MEL])
            wm_sb = tok_sb("wm_sb", [N_MFCC, D])
            to_h = tok_sb("to_h", [N_MEL + 1, D])
            squares = tok_sb("squares", [2 * N_BINS, N_TOK])
            logmel = tok_sb("logmel", [N_MEL + 1, N_TOK])
            wts_in, pack_in, frames_in = sem("wts_in"), sem("pack_in"), sem("frames_in")
            spectrum, squared, melled, logged = sem("spectrum"), sem("squared"), sem("melled"), sem("logged")
            token_mm, token_out, fused, fused_out = sem("token_mm"), sem("token_out"), sem("fused"), sem("fused_out")
            bias_mm, bias_out, split_hi, split_lo = sem("bias_mm"), sem("bias_out"), sem("split_hi"), sem("split_lo")
            scaled, wide_b = sem("scaled"), sem("wide_b")
            N_SMALL = 16

            with nc.Block() as block:
                @block.sync
                def _(sp):
                    sp.dma_start(dft_sb[:], dft).then_inc(frames_in, 16)
                    sp.dma_start(fr, frames).then_inc(frames_in, 16)
                    sp.dma_start(mel_sb[:], mel2).then_inc(frames_in, 16)
                    sp.dma_start(dct_sb[:], dct).then_inc(wts_in, 16)
                    sp.dma_start(wm_sb[:], w_mfcc).then_inc(wts_in, 16)
                    sp.dma_start(to_h[N_MEL:N_MEL + 1, :], b_tok).then_inc(wts_in, 16)
                    sp.dma_start(pack_raw[:, 0, :], w_pack[0:P, :]).then_inc(pack_in, 16)
                    sp.dma_start(pack_raw[0:REST, 1, :], w_pack[P:D, :]).then_inc(pack_in, 16)
                    sp.dma_start(pack_raw[REST:P, 1, :], w_pack[P:D, :]).then_inc(pack_in, 16)
                    for half in range(2):
                        lo, n = half * P, (P, REST)[half]
                        sp.dma_start(bqk[0:n, half:half + 1], b_qk_col[lo:lo + n, :]).then_inc(wts_in, 16)
                        sp.dma_start(bqk[0:n, 2 + half:3 + half], b_qk_col[D + lo:D + lo + n, :]).then_inc(wts_in, 16)
                        sp.dma_start(bgate[0:n, half:half + 1], b_gate_col[lo:lo + n, :]).then_inc(wts_in, 16)
                        sp.dma_start(ln_b[0:n, half:half + 1], ln_b_col[lo:lo + n, :]).then_inc(wts_in, 16)
                    sp.dma_start(ln_g[:, 0:1], ln_g_col[0:P, :]).then_inc(wts_in, 16)
                    sp.dma_start(ln_g[0:REST, 1:2], ln_g_col[P:D, :]).then_inc(wts_in, 16)
                    sp.dma_start(ln_g[REST:P, 1:2], ln_g_col[P:D, :]).then_inc(wts_in, 16)
                    sp.dma_start(bv_bc[:], b_v.partition_broadcast(BLK)).then_inc(wts_in, 16)
                    sp.dma_start(bproj_bc[:], b_proj.partition_broadcast(BLK)).then_inc(wts_in, 16)
                    sp.dma_start(hm_main[:], head_main).then_inc(loaded, 16)
                    sp.dma_start(hm_rest[:], head_rest).then_inc(loaded, 16)
                    load_expert(sp, N_EXP)

                @block.gpsimd
                def _(pool):
                    nc.gpsimd.memset(ident[:], 0.0).then_inc(made, 1)
                    nc.gpsimd.memset(causal[:], 1.0).then_inc(made, 1)
                    nc.gpsimd.memset(ln_eps_tile[:], 1e-6).then_inc(made, 1)
                    nc.gpsimd.memset(logmel[:], 1.0).then_inc(made, 1)
                    nc.gpsimd.memset(minus_half[:], -0.5).then_inc(made, 1)
                    pool.wait_ge(made, 5)
                    nc.gpsimd.affine_select(out=ident[:], in_=ident[:], compare_op=ALU.not_equal, fill=1.0, base=0,
                                            pattern=[[-1, P]], channel_multiplier=1).then_inc(made, 1)
                    nc.gpsimd.affine_select(out=causal[:], in_=causal[:], compare_op=ALU.is_ge, fill=0.0, base=0,
                                            pattern=[[1, BLK]], channel_multiplier=-1).then_inc(made, 1)
                    nc.gpsimd.memset(v_aug[:], 1.0).then_inc(made, 1)
                    nc.gpsimd.memset(state[:, 0, :], 0.0).then_inc(made, 1)
                    nc.gpsimd.memset(state_r[:], 0.0).then_inc(made, 1)
                    pool.wait_ge(made, 10)
                    nc.gpsimd.memset(qf[REST:P, 1, :], 0.0).then_inc(made, 1)
                    nc.gpsimd.memset(kh[REST:P, HEADS_MAIN:HEADS, :], 0.0).then_inc(made, 1)
                    pool.wait_ge(made, 12)
                    nc.gpsimd.memset(empty_slot[:], 0.0).then_inc(made, 1)
                    pool.wait_ge(made, 13)
                    nc.gpsimd.memset(empty_slot[:, D:D + 1].bitcast(I32), NOWHERE).then_inc(made, 1)
                    pool.wait_ge(wts_in, 16 * N_SMALL)
                    nc.gpsimd.memset(ln_b_wide[:], 0.0).then_inc(wide_b, 1)
                    pool.wait_ge(wide_b, 1)
                    nc.gpsimd.tensor_scalar(ln_b_wide[:, 0, :], ln_b_wide[:, 0, :], ln_b[:, 0:1], None,
                                            ALU.add).then_inc(wide_b, 1)
                    nc.gpsimd.tensor_scalar(ln_b_wide[0:REST, 1, :], ln_b_wide[0:REST, 1, :], ln_b[0:REST, 1:2], None,
                                            ALU.add).then_inc(wide_b, 1)

                @block.tensor
                def _(pe):
                    pe.wait_ge(wts_in, 16 * N_SMALL)
                    nc.tensor.matmul(bank[3][0:N_MEL, 0:D], dct_sb[:], wm_sb[:], start=True, stop=True).then_inc(fused, 1)
                    pe.wait_ge(pack_in, 48)
                    pe.wait_ge(wide_b, 3)
                    for n, (lo, m) in enumerate([(COL_Q, P), (COL_Q + P, REST), (COL_K, P), (COL_K + P, REST)]):
                        nc.tensor.matmul(bank[2][0:m, n:n + 1], pack_raw[:, 0, lo:lo + m], ln_b[:, 0:1],
                                         start=(n == 0), stop=False, skip_group_check=True)
                        nc.tensor.matmul(bank[2][0:m, n:n + 1], pack_raw[0:REST, 1, lo:lo + m], ln_b[0:REST, 1:2],
                                         start=False, stop=True, skip_group_check=True)
                    nc.tensor.matmul(bank[1][0:BLK, 0:D], ln_b_wide[:, 0, :], pack_raw[:, 0, COL_V:COL_V + D],
                                     start=True, stop=False)
                    nc.tensor.matmul(bank[1][0:BLK, 0:D], ln_b_wide[0:REST, 1, :], pack_raw[0:REST, 1, COL_V:COL_V + D],
                                     start=False, stop=True).then_inc(bias_mm, 1)
                    pe.wait_ge(frames_in, 48)
                    pe.wait_ge(fused_out, 1)
                    pe.wait_ge(bias_out, 5)

                    def spectrum_of(n):
                        nc.tensor.matmul(bank[0][0:2 * N_BINS, 0:N_TOK], dft_sb[:], fr[:, n, :],
                                         start=True, stop=True).then_inc(spectrum, 1)

                    def tokens_of(n, first):
                        pe.wait_ge(squared, n + 1)
                        if not first:
                            pe.wait_ge(logged, n)
                        nc.tensor.matmul(bank[2][0:N_MEL, 0:N_TOK], mel_sb[:], squares[:],
                                         start=True, stop=True).then_inc(melled, 1)

                    def features_of(n, first):
                        pe.wait_ge(logged, n + 1)
                        if not first:
                            pe.wait_ge(token_out, 2 * n)
                        for t in range(N_BLK):
                            mm = nc.tensor.matmul(bank[4 + t // 2][0:BLK, (t % 2) * D:(t % 2 + 1) * D],
                                                  logmel[:, t * BLK:(t + 1) * BLK], to_h[:],
                                                  start=(t % 2 == 0), stop=(t % 2 == 1), skip_group_check=True)
                            if t % 2:
                                mm.then_inc(token_mm, 1)

                    pe.wait_ge(made, 4)
                    spectrum_of(0)
                    tokens_of(0, True)
                    spectrum_of(1)
                    features_of(0, True)
                    with pe.Fori(1, N_SEQ - 1) as n:
                        tokens_of(n, False)
                        spectrum_of(n + 1)
                        features_of(n, False)
                    tokens_of(N_SEQ - 1, False)
                    features_of(N_SEQ - 1, False)

                @block.scalar
                def _(act):
                    def square_of(n, first):
                        act.wait_ge(spectrum, n + 1)
                        if not first:
                            act.wait_ge(melled, n)
                        nc.scalar.activation(squares[:], bank[0][0:2 * N_BINS, 0:N_TOK], ACT.Square).then_inc(squared, 1)

                    def log_of(n, first):
                        act.wait_ge(melled, n + 1)
                        if not first:
                            act.wait_ge(token_mm, 2 * n)
                        nc.scalar.activation(logmel[0:N_MEL, :], bank[2][0:N_MEL, 0:N_TOK], ACT.Ln,
                                             bias=ln_eps_tile[0:N_MEL, :]).then_inc(logged, 1)

                    act.wait_ge(made, 4)
                    square_of(0, True)
                    log_of(0, True)
                    with act.Fori(1, N_SEQ) as n:
                        square_of(n, False)
                        log_of(n, False)
                    act.wait_ge(scaled, 2)
                    nc.scalar.copy(pack_hi[:, 0, :], pack_raw[:, 0, :]).then_inc(split_hi, 1)
                    nc.scalar.copy(pack_hi[:, 1, :], pack_raw[:, 1, :]).then_inc(split_hi, 1)
                    nc.scalar.mul(bgate_half[:, 0:1], bgate[:, 0:1], 0.5)
                    nc.scalar.mul(bgate_half[0:REST, 1:2], bgate[0:REST, 1:2], 0.5).then_inc(split_hi, 1)

                @block.vector
                def _(dve):
                    dve.wait_ge(wts_in, 16 * N_SMALL)
                    dve.wait_ge(fused, 1)
                    nc.vector.tensor_copy(to_h[0:N_MEL, :], bank[3][0:N_MEL, 0:D]).then_inc(fused_out, 1)
                    dve.wait_ge(bias_mm, 1)
                    for n, m in enumerate([P, REST, P, REST]):
                        nc.vector.tensor_tensor(bqk[0:m, n:n + 1], bank[2][0:m, n:n + 1], bqk[0:m, n:n + 1],
                                                ALU.add).then_inc(bias_out, 1)
                    nc.vector.tensor_tensor(bv_bc[:], bank[1][0:BLK, 0:D], bv_bc[:], ALU.add).then_inc(bias_out, 1)
                    for part in range(2):
                        nc.vector.tensor_scalar(pack_raw[:, part, 0:3 * D], pack_raw[:, part, 0:3 * D],
                                                ln_g[:, part:part + 1], None, ALU.mult).then_inc(scaled, 1)
                    with dve.Fori(0, N_SEQ) as n:
                        for pair in range(2):
                            dve.wait_ge(token_mm, 2 * n + pair + 1)
                            nc.vector.tensor_copy(h_all[:, n, 2 * pair:2 * pair + 2, :],
                                                  bank[4 + pair][0:BLK, 0:2 * D].rearrange("p (t d) -> p t d", t=2)
                                                  ).then_inc(token_out, 1)
                    for part in range(2):
                        dve.wait_ge(split_hi, part + 1)
                        nc.vector.tensor_tensor(pack_lo[:, part, :], pack_raw[:, part, :],
                                                pack_hi[:, part, :].bitcast(F32), ALU.subtract).then_inc(split_lo, 1)

        centred = sem("centred")
        rooted = sem("rooted")
        chain = sem("chain")
        hn_done, z_done, x2_done = sem("hn_done"), sem("z_done"), sem("x2_done")
        t_hn, t_z, t_a, t_x = sem("t_hn"), sem("t_z"), sem("t_a"), sem("t_x")
        hi_hn, hi_z, hi_a, hi_x = sem("hi_hn"), sem("hi_z"), sem("hi_a"), sem("hi_x")
        lo_hn, lo_z, lo_a, lo_x = sem("lo_hn"), sem("lo_z"), sem("lo_a"), sem("lo_x")
        mm_gk, mm_q, mm_v = sem("mm_gk"), sem("mm_q"), sem("mm_v")
        tanh_done, gate_done = sem("tanh_done"), sem("gate_done")
        kg_done, kexp_done, kpos_done, kf_done = sem("kg_done"), sem("kexp_done"), sem("kpos_done"), sem("kf_done")
        kh_dve, kh_act = sem("kh_dve"), sem("kh_act")
        qexp_done, qpos_done, qf_done = sem("qexp_done"), sem("qpos_done"), sem("qf_done")
        v_done, t_k, ktok_done, mm_kv, state_done = (sem("v_done"), sem("t_k"), sem("ktok_done"), sem("mm_kv"),
                                                     sem("state_done"))
        scores_done, probs_dve, probs_act, probs_pool = (sem("scores_done"), sem("probs_dve"), sem("probs_act"),
                                                         sem("probs_pool"))
        pv_done, den_done, rden_done, attn_done = sem("pv_done"), sem("den_done"), sem("rden_done"), sem("attn_done")
        hb_done, mm_proj, h_done, mm_rt, logits_done = (sem("hb_done"), sem("mm_proj"), sem("h_done"), sem("mm_rt"),
                                                        sem("logits_done"))
        x_stored, emptied = sem("x_stored"), sem("emptied")
        masked = sem("masked")
        N_SC = N_BLK * N_GRP

        def halves(t3):
            return [(t3[:, 0, :], P), (t3[0:REST, 1, :], REST)]

        with nc.Block() as block:
            @block.sync
            def _(sp):
                sp.sem_inc(x_stored, 16)
                sp.dma_start(slots_dram.rearrange("(t p) c -> p t c", p=P),
                             empty_slot[:].unsqueeze(1).broadcast_to((P, N_TILE, D + N_META))).then_inc(emptied, 16)
                with sp.Fori(0, N_SEQ) as n:
                    sp.wait_ge(x2_done, n + 1)
                    stand(sp, passed)
                    sp.dma_start(x_dram[bass.ds(n * N_TOK, N_TOK), :].rearrange("(t p) d -> p t d", p=BLK),
                                 x2[:]).then_inc(x_stored, 16)
                    sp.wait_ge(x_stored, 16 * n + 32)
                    stand(sp, passed)
                sp.wait_ge(emptied, 16)

            @block.tensor
            def _(pe):
                def transpose_blocks(src, n_done, dst_main, dst_rest, signal, wait_main, wait_rest):
                    wait_main()
                    for t in range(N_BLK):
                        mm = nc.tensor.transpose(dst_main[:, t * BLK:(t + 1) * BLK], src[:, t, 0:P], ident[0:BLK, 0:BLK])
                    mm.then_inc(signal, 1)
                    wait_rest()
                    for t in range(N_BLK):
                        mm = nc.tensor.transpose(dst_rest[0:REST, t * BLK:(t + 1) * BLK], src[:, t, P:D],
                                                 ident[0:BLK, 0:BLK])
                    mm.then_inc(signal, 1)

                def project(dst, m, col, x):
                    o = dst[0:m, 0:N_TOK]
                    c = slice(col, col + m)
                    nc.tensor.matmul(o, pack_hi[:, 0, c], x[:, 0, :], start=True, stop=False)
                    nc.tensor.matmul(o, pack_hi[:, 0, c], x[:, 1, :], start=False, stop=False)
                    nc.tensor.matmul(o, pack_lo[:, 0, c], x[:, 0, :], start=False, stop=False)
                    nc.tensor.matmul(o, pack_hi[:, 1, c], x[:, 2, :], start=False, stop=False)
                    return nc.tensor.matmul(o, pack_lo[:, 1, c], x[:, 2, :], start=False, stop=True)

                def project_block(o, x, t, c, first=True, last=True):
                    b = slice(t * BLK, (t + 1) * BLK)
                    nc.tensor.matmul(o, x[:, 0, b], pack_hi[:, 0, c], start=first, stop=False, skip_group_check=True)
                    nc.tensor.matmul(o, x[:, 0, b], pack_lo[:, 0, c], start=False, stop=False, skip_group_check=True)
                    nc.tensor.matmul(o, x[:, 1, b], pack_hi[:, 0, c], start=False, stop=False, skip_group_check=True)
                    nc.tensor.matmul(o, x[:, 2, b], pack_hi[:, 1, c], start=False, stop=False, skip_group_check=True)
                    return nc.tensor.matmul(o, x[:, 2, b], pack_lo[:, 1, c], start=False, stop=last,
                                            skip_group_check=True)

                def front_transpose(n):
                    pe.wait_ge(hn_done, n + 1)
                    transpose_blocks(hn, None, bank[0], bank[1], t_hn,
                                     lambda: at_least(pe, ktok_done, n), lambda: None)
                    pe.wait_ge(z_done, n + 1)
                    transpose_blocks(z, None, bank[2], bank[3], t_z,
                                     lambda: at_least(pe, state_done, 2 * n), lambda: None)

                def front_gate(n):
                    pe.wait_ge(lo_hn, 2 * n + 2)
                    project(bank[0], P, COL_G, hn_t).then_inc(mm_gk, 1)
                    project(bank[1], REST, COL_G + P, hn_t).then_inc(mm_gk, 1)

                def front_k(n):
                    pe.wait_ge(lo_z, 2 * n + 2)
                    project(bank[2], P, COL_K, z_t).then_inc(mm_gk, 1)
                    project(bank[3], REST, COL_K + P, z_t).then_inc(mm_gk, 1)

                def front_q(n):
                    pe.wait_ge(tanh_done, 2 * n + 1)
                    project(bank[0], P, COL_Q, z_t).then_inc(mm_q, 1)
                    pe.wait_ge(tanh_done, 2 * n + 2)
                    project(bank[1], REST, COL_Q + P, z_t).then_inc(mm_q, 1)
                    for pair in range(2):
                        pe.wait_ge(kg_done, 2 * n + pair + 1)
                        for t in (2 * pair, 2 * pair + 1):
                            o = bank[2 + pair][0:BLK, (t % 2) * D:(t % 2 + 1) * D]
                            mm = project_block(o, z_t, t, slice(COL_V, COL_V + D), first=(t % 2 == 0))
                        mm.then_inc(mm_v, 1)

                def front_state(n):
                    pe.wait_ge(kf_done, 2 * n + 2)
                    pe.wait_ge(qf_done, 2 * n + 2)
                    for t in range(N_BLK - 1):
                        b = slice(t * BLK, (t + 1) * BLK)
                        dst = bank[t // 2][0:BLK, (t % 2) * D:(t % 2 + 1) * D]
                        nc.tensor.transpose(dst[:, 0:P], kf[:, 0, b], ident[:])
                        mm = nc.tensor.transpose(dst[:, P:D], kf[0:REST, 1, b], ident[0:REST, 0:REST])
                    mm.then_inc(t_k, 1)
                    pe.wait_ge(v_done, 2 * n + 2)
                    pe.wait_ge(ktok_done, n + 1)
                    nm, nr = HEADS_MAIN * VA, (HEADS - HEADS_MAIN) * VA
                    for t in range(N_BLK - 1):
                        mm = nc.tensor.matmul(bank[2][:, t * nm:(t + 1) * nm], k_tok[:, t, 0:P],
                                              v_aug[:, t, 0:HEADS_MAIN, :], start=True, stop=True,
                                              skip_group_check=True)
                    mm.then_inc(mm_kv, 1)
                    for t in range(N_BLK - 1):
                        mm = nc.tensor.matmul(bank[3][0:REST, t * nr:(t + 1) * nr], k_tok[:, t, P:D],
                                              v_aug[:, t, HEADS_MAIN:HEADS, :], start=True, stop=True,
                                              skip_group_check=True)
                    mm.then_inc(mm_kv, 1)

                def scores(n, g):
                    t, grp = divmod(g, N_GRP)
                    b = slice(t * BLK, (t + 1) * BLK)
                    if g >= 2:
                        wait_probs(n, g - 2)
                    if g == 0:
                        pe.wait_ge(kh_dve, n + 1)
                    if g in (1, 2):
                        pe.wait_ge(kh_act, 2 * n + g)
                    for j in range(GRP):
                        h = grp * GRP + j
                        mm = nc.tensor.matmul(bank[4 + g % 2][0:BLK, j * BLK:(j + 1) * BLK], kh[:, h, b],
                                              qf[:, h // HEADS_MAIN, b], start=True, stop=True, skip_group_check=True)
                    mm.then_inc(scores_done, 1)

                def wait_probs(n, g):
                    if g % 2 == 0:
                        pe.wait_ge(probs_dve, n * (N_SC // 2) + g // 2 + 1)
                    else:
                        pe.wait_ge(probs_pool, n * (N_SC // 2) + g // 2 + 1)

                def attention(n):
                    pe.wait_ge(qf_done, 2 * n + 2)
                    scores(n, 0)
                    scores(n, 1)
                    pe.wait_ge(state_done, 2 * n + 2)
                    for t in range(N_BLK):
                        o = bank[6 + t % 2]
                        b = slice(t * BLK, (t + 1) * BLK)
                        nm = HEADS_MAIN * VA
                        if t >= 2:
                            pe.wait_ge(attn_done, n * N_BLK + t - 1)
                        nc.tensor.matmul(o[0:BLK, 0:nm], qf[:, 0, b], state[:, t, :], start=True, stop=False,
                                         skip_group_check=True)
                        nc.tensor.matmul(o[0:BLK, nm:HEADS * VA], qf[:, 1, b], state_r[:, t, :], start=False, stop=False,
                                         skip_group_check=True)
                        for grp in range(N_GRP):
                            g = t * N_GRP + grp
                            if g + 2 < N_SC:
                                scores(n, g + 2)
                            wait_probs(n, g)
                            for j in range(GRP):
                                h = grp * GRP + j
                                mm = nc.tensor.matmul(o[0:BLK, h * VA:(h + 1) * VA],
                                                      probs[:, g % 3, j * BLK:(j + 1) * BLK], v_aug[:, t, h, :],
                                                      start=False, stop=True, skip_group_check=True)
                        mm.then_inc(pv_done, 1)

                def attention_transpose(n):
                    pe.wait_ge(attn_done, N_BLK * n + N_BLK)
                    transpose_blocks(attn, None, bank[4], bank[5], t_a, lambda: None, lambda: None)

                def attention_project(n):
                    pe.wait_ge(lo_a, 2 * n + 2)
                    for t in range(N_BLK):
                        mm = project_block(bank[6 + t // 2][0:BLK, (t % 2) * D:(t % 2 + 1) * D], a_t, t,
                                           slice(COL_P, COL_P + D), first=(t % 2 == 0))
                        if t % 2:
                            mm.then_inc(mm_proj, 1)

                def tail_x(n):
                    pe.wait_ge(x2_done, n + 1)
                    transpose_blocks(x2, None, bank[4], bank[5], t_x, lambda: None, lambda: None)

                def tail_router(n):
                    pe.wait_ge(lo_x, 2 * n + 2)
                    for t in range(N_BLK):
                        mm = project_block(bank[6][0:BLK, t * N_EXP:(t + 1) * N_EXP], x_t, t,
                                           slice(COL_R, COL_R + N_EXP), first=(t == 0))
                    mm.then_inc(mm_rt, 1)

                def turn(n, nxt):
                    if n is not None:
                        attention(n)
                    if nxt is not None:
                        front_transpose(nxt)
                    if n is not None:
                        attention_transpose(n)
                    if nxt is not None:
                        front_gate(nxt)
                    if n is not None:
                        attention_project(n)
                    if nxt is not None:
                        front_k(nxt)
                    if n is not None:
                        tail_x(n)
                    if nxt is not None:
                        front_q(nxt)
                    if n is not None:
                        tail_router(n)
                    if nxt is not None:
                        front_state(nxt)
                    if n is not None:
                        pe.wait_ge(logits_done, n + 1)

                pe.wait_ge(loaded, 32)
                turn(None, 0)
                with pe.Fori(0, N_SEQ - 1) as n:
                    turn(n, n + 1)
                turn(N_SEQ - 1, None)

            @block.scalar
            def _(act):
                def hi_parts(src_main, src_rest, dst, ready, n, signal):
                    act.wait_ge(ready, 2 * n + 1)
                    nc.scalar.copy(dst[:, 0, :], src_main[:, 0:N_TOK]).then_inc(signal, 1)
                    act.wait_ge(ready, 2 * n + 2)
                    nc.scalar.copy(dst[0:REST, 2, :], src_rest[0:REST, 0:N_TOK]).then_inc(signal, 1)

                def attention(n):
                    for g in range(1, N_SC, 2):
                        act.wait_ge(scores_done, n * N_SC + g + 1)
                        nc.scalar.copy(probs[:, g % 3, :], bank[5][0:BLK, 0:GRP * BLK]).then_inc(probs_act, 1)

                def front_hi(n):
                    hi_parts(bank[0], bank[1], hn_t, t_hn, n, hi_hn)
                    hi_parts(bank[2], bank[3], z_t, t_z, n, hi_z)

                def front(n):
                    for half, (dst, m) in enumerate(halves(gate)):
                        act.wait_ge(mm_gk, 4 * n + half + 1)
                        nc.scalar.activation(dst, bank[half][0:m, 0:N_TOK], ACT.Tanh, bias=bgate_half[0:m, half:half + 1],
                                             scale=0.5).then_inc(tanh_done, 1)
                    for half, (dst, m) in enumerate(halves(k_exp)):
                        act.wait_ge(kg_done, 2 * n + half + 1)
                        nc.scalar.activation(dst, kg[0:m, half, :], ACT.Exp).then_inc(kexp_done, 1)

                def front_q(n):
                    for half, (dst, m) in enumerate(halves(q_exp)):
                        act.wait_ge(mm_q, 2 * n + half + 1)
                        act.wait_ge(kf_done, 2 * n + half + 1)
                        nc.scalar.activation(dst, bank[half][0:m, 0:N_TOK], ACT.Exp,
                                             bias=bqk[0:m, half:half + 1]).then_inc(qexp_done, 1)

                def head_rows(n, grp):
                    act.wait_ge(kf_done, 2 * n + (1 if grp == 1 else 2))
                    for h in range(grp * GRP, (grp + 1) * GRP):
                        half, m = (0, P) if h < HEADS_MAIN else (1, REST)
                        mask = (hm_main, hm_rest)[half]
                        j = h - half * HEADS_MAIN
                        ins = nc.scalar.activation(kh[0:m, h, :], kf[0:m, half, :], ACT.Copy, scale=mask[:, j:j + 1])
                    ins.then_inc(kh_act, 1)

                def front_state(n):
                    act.wait_ge(t_k, n + 1)
                    nc.scalar.copy(k_tok[:, 0:2, :], bank[0][0:BLK, 0:2 * D].rearrange("p (t d) -> p t d", t=2))
                    nc.scalar.copy(k_tok[:, 2, :], bank[1][0:BLK, 0:D]).then_inc(ktok_done, 1)

                def turn(n, nxt):
                    if n is not None:
                        attention(n)
                    if nxt is not None:
                        front_hi(nxt)
                    if n is not None:
                        hi_parts(bank[4], bank[5], a_t, t_a, n, hi_a)
                    if nxt is not None:
                        front(nxt)
                    if n is not None:
                        hi_parts(bank[4], bank[5], x_t, t_x, n, hi_x)
                    if nxt is not None:
                        head_rows(nxt, 1)
                        front_q(nxt)
                        front_state(nxt)
                        head_rows(nxt, 2)

                turn(None, 0)
                with act.Fori(0, N_SEQ - 1) as n:
                    turn(n, n + 1)
                turn(N_SEQ - 1, None)

            @block.vector
            def _(dve):
                LN_STEPS = 3
                LN_PER_SEQ = 3

                def norm_stats(src, which):
                    for t in range(N_BLK):
                        ins = nc.vector.bn_stats(stats[:, t, :], src(t))
                    ins.then_inc(chain, 1)
                    dve.wait_ge(chain, which * LN_STEPS + 1)
                    stand(dve, passed)
                    for t in range(N_BLK):
                        ins = nc.vector.bn_aggr(moments[:, t, :], stats[:, t, :])
                    ins.then_inc(chain, 1)
                    dve.wait_ge(chain, which * LN_STEPS + 2)
                    stand(dve, passed)
                    nc.vector.tensor_scalar(var_eps[:], moments[:, :, 1], LN_EPS, None, ALU.add).then_inc(centred, 1)

                def norm_apply(src, dst, which, signal):
                    dve.wait_ge(rooted, which + 1)
                    for t in range(N_BLK):
                        ins = nc.vector.tensor_scalar(dst[:, t, :], src(t), moments[:, t, 0:1], rstd[:, t:t + 1],
                                                      ALU.subtract, ALU.mult)
                        if t == N_BLK - 2:
                            ins.then_inc(chain, 1)
                    ins.then_inc(signal, 1)

                def lo_parts(src_main, src_rest, dst, hi_ready, n, signal):
                    dve.wait_ge(hi_ready, 2 * n + 1)
                    nc.vector.tensor_tensor(dst[:, 1, :], src_main[:, 0:N_TOK], dst[:, 0, :].bitcast(F32),
                                            ALU.subtract).then_inc(signal, 1)
                    dve.wait_ge(hi_ready, 2 * n + 2)
                    nc.vector.tensor_tensor(dst[REST:P, 2, :], src_rest[0:REST, 0:N_TOK], dst[0:REST, 2, :].bitcast(F32),
                                            ALU.subtract).then_inc(signal, 1)

                def norm_h_stats(n, which):
                    norm_stats(lambda t: h_all[:, n, t, :], which)

                def norm_h_apply(n, which):
                    at_least(dve, t_hn, 2 * n)
                    norm_apply(lambda t: h_all[:, n, t, :], hn, which, hn_done)

                def norm_hn_stats(n, which):
                    dve.wait_ge(hn_done, n + 1)
                    stand(dve, passed)
                    norm_stats(lambda t: hn[:, t, :], which + 1)

                def norm_hn_apply(n, which):
                    at_least(dve, t_z, 2 * n)
                    norm_apply(lambda t: hn[:, t, :], z, which + 1, z_done)

                pieces = [norm_h_stats, norm_h_apply, norm_hn_stats, norm_hn_apply]

                def normalize(n, t):
                    o = bank[6 + t % 2][0:BLK, 0:HEADS * VA].rearrange("p (h e) -> p h e", e=VA)
                    dve.wait_ge(pv_done, N_BLK * n + t + 1)
                    nc.vector.tensor_scalar(den[:], o[:, :, DH], 1e-6, None, ALU.add).then_inc(den_done, 1)
                    dve.wait_ge(den_done, N_BLK * n + t + 1)
                    nc.vector.reciprocal(rden[:], den[:]).then_inc(rden_done, 1)
                    dve.wait_ge(rden_done, N_BLK * n + t + 1)
                    nc.vector.tensor_tensor(attn[:, t, :].rearrange("p (h e) -> p h e", e=DH), o[:, :, 0:DH],
                                            rden[:].unsqueeze(2).broadcast_to((BLK, HEADS, DH)),
                                            ALU.mult).then_inc(attn_done, 1)

                def attention(n, nxt, which):
                    for g in range(N_SC):
                        if g % 2 == 0:
                            dve.wait_ge(scores_done, n * N_SC + g + 1)
                            nc.vector.tensor_tensor(probs[:, g % 3, :].rearrange("p (j l) -> p j l", j=GRP),
                                                    bank[4][0:BLK, 0:GRP * BLK].rearrange("p (j l) -> p j l", j=GRP),
                                                    causal[:].unsqueeze(1).broadcast_to((BLK, GRP, BLK)),
                                                    ALU.mult).then_inc(probs_dve, 1)
                        if g % N_GRP == 1 and g > N_GRP:
                            normalize(n, g // N_GRP - 1)
                        if g in (2, 4, 6, 8) and nxt is not None:
                            pieces[g // 2 - 1](nxt, which)
                    normalize(n, N_BLK - 1)

                def attention_out(n):
                    lo_parts(bank[4], bank[5], a_t, hi_a, n, lo_a)
                    dve.wait_ge(hb_done, n + 1)
                    for pair in range(2):
                        dve.wait_ge(mm_proj, 2 * n + pair + 1)
                        ts = slice(2 * pair, 2 * pair + 2)
                        nc.vector.tensor_tensor(h_all[:, n, ts, :],
                                                bank[6 + pair][0:BLK, 0:2 * D].rearrange("p (t d) -> p t d", t=2),
                                                hb[:, ts, :], ALU.add).then_inc(h_done, 1)

                def front(n):
                    lo_parts(bank[0], bank[1], hn_t, hi_hn, n, lo_hn)
                    lo_parts(bank[2], bank[3], z_t, hi_z, n, lo_z)

                def front_k(n):
                    for half, (dst, m) in enumerate(halves(gate)):
                        dve.wait_ge(tanh_done, 2 * n + half + 1)
                        nc.vector.tensor_scalar(dst, dst, 0.5, 0.5, ALU.mult, ALU.add).then_inc(gate_done, 1)
                    for half, (dst, m) in enumerate(halves(kg)):
                        dve.wait_ge(gate_done, 2 * n + half + 1)
                        dve.wait_ge(mm_gk, 4 * n + half + 3)
                        nc.vector.scalar_tensor_tensor(dst, bank[2 + half][0:m, 0:N_TOK], bqk[0:m, 2 + half:3 + half],
                                                       gate[0:m, half, :], ALU.add, ALU.mult).then_inc(kg_done, 1)
                    for half, (dst, m) in enumerate(halves(k_pos)):
                        dve.wait_ge(kg_done, 2 * n + half + 1)
                        nc.vector.tensor_scalar(dst, kg[0:m, half, :], 0.0, None, ALU.max).then_inc(kpos_done, 1)
                    for half, (dst, m) in enumerate(halves(kf)):
                        dve.wait_ge(kexp_done, 2 * n + half + 1)
                        dve.wait_ge(kpos_done, 2 * n + half + 1)
                        nc.vector.scalar_tensor_tensor(dst, k_exp[0:m, half, :], 1.0, k_pos[0:m, half, :],
                                                       ALU.min, ALU.add).then_inc(kf_done, 1)
                    dve.wait_ge(kf_done, 2 * n + 1)
                    for h in range(GRP):
                        ins = nc.vector.tensor_scalar(kh[:, h, :], kf[:, 0, :], hm_main[:, h:h + 1], None, ALU.mult)
                    ins.then_inc(kh_dve, 1)

                def front_q(n):
                    for half, (dst, m) in enumerate(halves(q_pos)):
                        dve.wait_ge(qexp_done, 2 * n + half + 1)
                        nc.vector.tensor_scalar(dst, bank[half][0:m, 0:N_TOK], bqk[0:m, half:half + 1], 0.0,
                                                ALU.add, ALU.max).then_inc(qpos_done, 1)
                        dve.wait_ge(qpos_done, 2 * n + half + 1)
                        nc.vector.scalar_tensor_tensor(qf[0:m, half, :], q_exp[0:m, half, :], 1.0, dst, ALU.min,
                                                       ALU.add).then_inc(qf_done, 1)
                    for pair in range(2):
                        dve.wait_ge(mm_v, 2 * n + pair + 1)
                        for t in (2 * pair, 2 * pair + 1):
                            ins = nc.vector.tensor_tensor(
                                v_aug[:, t, :, 0:DH],
                                bank[2 + pair][0:BLK, (t % 2) * D:(t % 2 + 1) * D].rearrange("p (h e) -> p h e", e=DH),
                                bv_bc[:].rearrange("p (h e) -> p h e", e=DH), ALU.add)
                        ins.then_inc(v_done, 1)

                def front_state(n):
                    for half, (dst, heads, mask, m) in enumerate([
                            (state, HEADS_MAIN, hm_main, P), (state_r, HEADS - HEADS_MAIN, hm_rest, REST)]):
                        dve.wait_ge(mm_kv, 2 * n + half + 1)
                        for t in range(N_BLK - 1):
                            ins = nc.vector.tensor_tensor(
                                dst[0:m, t + 1, :].rearrange("p (h e) -> p h e", e=VA),
                                bank[2 + half][0:m, t * heads * VA:(t + 1) * heads * VA].rearrange(
                                    "p (h e) -> p h e", e=VA),
                                mask[:].unsqueeze(2).broadcast_to((m, heads, VA)), ALU.mult)
                        ins.then_inc(masked, 1)
                    for t in range(1, N_BLK - 1):
                        dve.wait_ge(masked, 4 * n + 2 * t)
                        ins = nc.vector.tensor_tensor(state[:, t + 1, :], state[:, t + 1, :], state[:, t, :], ALU.add)
                        if t == 1:
                            ins.then_inc(masked, 1)
                        ins2 = nc.vector.tensor_tensor(state_r[0:REST, t + 1, :], state_r[0:REST, t + 1, :],
                                                       state_r[0:REST, t, :], ALU.add)
                        if t == 1:
                            ins2.then_inc(masked, 1)
                    ins.then_inc(state_done, 1)
                    ins2.then_inc(state_done, 1)

                def turn(n, nxt):
                    if n is None:
                        for piece in pieces:
                            piece(nxt, 0)
                    else:
                        attention(n, nxt, LN_PER_SEQ * n + 2)
                    if nxt is not None:
                        front(nxt)
                    if n is not None:
                        attention_out(n)
                        dve.wait_ge(h_done, 2 * n + 2)
                        stand(dve, passed)
                        which = LN_PER_SEQ * n + (4 if nxt is not None else 2)
                        norm_stats(lambda t: h_all[:, n, t, :], which)
                        dve.wait_ge(x_stored, 16 * n + 16)
                        norm_apply(lambda t: h_all[:, n, t, :], x2, which, x2_done)
                    if nxt is not None:
                        front_k(nxt)
                    if n is not None:
                        lo_parts(bank[4], bank[5], x_t, hi_x, n, lo_x)
                    if nxt is not None:
                        front_q(nxt)
                    if n is not None:
                        dve.wait_ge(mm_rt, n + 1)
                        nc.vector.tensor_copy(logits[:, bass.ds(n * N_BLK, N_BLK), :],
                                              bank[6][0:BLK, 0:N_BLK * N_EXP].rearrange("p (t e) -> p t e", e=N_EXP)
                                              ).then_inc(logits_done, 1)
                    if nxt is not None:
                        front_state(nxt)

                dve.wait_ge(loaded, 32)
                turn(None, 0)
                with dve.Fori(0, N_SEQ - 1) as n:
                    turn(n, n + 1)
                turn(N_SEQ - 1, None)

            @block.gpsimd
            def _(pool):
                def root(which):
                    pool.wait_ge(centred, which + 1)
                    nc.gpsimd.tensor_tensor(rstd[:], var_eps[:], minus_half[:], ALU.pow).then_inc(rooted, 1)

                def attention(n, nxt):
                    for g in range(1, N_SC, 2):
                        if g in (5, 9) and nxt is not None:
                            root(3 * n + (2 if g == 5 else 3))
                        pool.wait_ge(probs_act, n * (N_SC // 2) + g // 2 + 1)
                        p3 = probs[:, g % 3, :].rearrange("p (j l) -> p j l", j=GRP)
                        nc.gpsimd.tensor_tensor(p3, p3, causal[:].unsqueeze(1).broadcast_to((BLK, GRP, BLK)),
                                                ALU.mult).then_inc(probs_pool, 1)

                def residual(n):
                    at_least(pool, h_done, 2 * n)
                    nc.gpsimd.tensor_tensor(hb[:], h_all[:, n, :, :],
                                            bproj_bc[:].unsqueeze(1).broadcast_to((BLK, N_BLK, D)),
                                            ALU.add).then_inc(hb_done, 1)

                def turn(n, nxt):
                    if n is None:
                        root(0)
                        root(1)
                    else:
                        attention(n, nxt)
                        root(3 * n + (4 if nxt is not None else 2))
                    if nxt is not None:
                        residual(nxt)

                pool.wait_ge(loaded, 32)
                turn(None, 0)
                with pool.Fori(0, N_SEQ - 1) as n:
                    turn(n, n + 1)
                turn(N_SEQ - 1, None)


def moe_stage(nc, passed, sem, bank, h_all, x_dram, slots_dram, y_dram, logits, ident, stage_up, stage_down,
              stage_in, load_expert, exp_bias):
    SHARED = N_EXP
    CARRY = N_ROW
    ALL_TILES = N_ROW + N_TILE
    X, H, Y, G, U = 0, 1, (2, 3), (4, 5), (6, 7)
    with ExitStack() as ctx:
        def sb(name, shape, dt=F32):
            return ctx.enter_context(nc.sbuf_tensor(name, shape, dt))

        up_hi = sb("up_hi", [P, N_EXP + 1, 2, 2 * F], F32R)
        up_lo = sb("up_lo", [P, N_EXP + 1, 2, 2 * F], F32R)
        down_hi = sb("down_hi", [P, N_EXP + 1, N_CHUNK, D], F32R)
        down_lo = sb("down_lo", [P, N_EXP + 1, N_CHUNK, D], F32R)
        x_in = sb("x_in", [P, 2, D])
        x_t = sb("xm_t", [P, 2, 3, P], F32R)
        silu = sb("silu", [P, F])
        prod = sb("prod", [P, F])
        hid_hi = sb("hid_hi", [P, N_CHUNK, P], F32R)
        hid_lo = sb("hid_lo", [P, N_CHUNK, P], F32R)
        y_out = sb("y_out", [P, 2, D])
        slot_meta = sb("slot_meta", [P, N_TILE, N_META])
        y_row = sb("y_row", [P, 2], I32)
        send = sb("send", [BLK, 2, TOP, D + N_META])
        send_to = sb("send_to", [BLK, 2, TOP], I32)
        bias_bc = sb("bias_bc", [BLK, N_EXP])
        earlier = sb("earlier", [BLK, N_EXP, N_EXP])
        before = sb("before", [BLK, BLK])
        ones = sb("ones", [BLK, BLK])
        tile_start = sb("tile_start", [BLK, N_ROW])
        tile_no = sb("tile_no", [1, N_TILE])
        row = sb("row", [BLK, N_ROW])
        row2 = sb("row2", [BLK, N_ROW])
        scores = sb("scores", [BLK, N_ROW, N_EXP])
        picks = sb("picks", [BLK, N_ROW, N_EXP])
        chosen = sb("chosen", [BLK, N_ROW, N_EXP])
        work = sb("work", [BLK, N_TILE * N_EXP])
        prefix = work[:, 0:2 * N_ROW * N_EXP].rearrange("p (a r e) -> p a r e", a=2, e=N_EXP)
        filled = work[:, 0:N_EXP * N_ROW].rearrange("p (e r) -> p e r", e=N_EXP)
        over = work[0:1, :].rearrange("p (t e) -> p t e", e=N_EXP)
        RANK = 4
        above = silu[0:BLK, 0:RANK * N_EXP * N_EXP].rearrange("p (r e j) -> p r e j", r=RANK, e=N_EXP)
        equal = prod[0:BLK, 0:RANK * N_EXP * N_EXP].rearrange("p (r e j) -> p r e j", r=RANK, e=N_EXP)
        n_tiles = sb("n_tiles", [BLK, N_EXP])
        first_tile = sb("first_tile", [BLK, N_EXP])
        last_tile = sb("last_tile", [BLK, N_EXP])
        tile_expert_f = sb("tile_expert_f", [1, N_TILE])
        tile_expert = sb("tile_expert", [1, N_TILE], I32)
        slot = sb("slot", [BLK, TOP, N_ROW])
        meta = sb("meta", [BLK, N_ROW, TOP, N_META])

        bias_in, consts = sem("bias_in"), sem("consts")
        split_hi, split_lo = sem("e_split_hi"), sem("e_split_lo")
        soft_in, soft_exp, counts_in, counted, order, routed = (sem("soft_in"), sem("soft_exp"), sem("counts_in"),
                                                                sem("counted"), sem("order"), sem("routed"))
        x_loaded = [sem("x_loaded0"), sem("x_loaded1")]
        t_x, hi_x, lo_x, mm_g, mm_u = sem("m_t_x"), sem("m_hi_x"), sem("m_lo_x"), sem("mm_g"), sem("mm_u")
        silu_done, prod_done, t_h, hi_h, lo_h, mm_y = (sem("silu_done"), sem("prod_done"), sem("t_h"), sem("hi_h"),
                                                       sem("lo_h"), sem("mm_y"))
        added = sem("added")
        y_ready = sem("y_ready")
        y_sent = [sem("y_sent0"), sem("y_sent1")]                
        send_in = [sem("send_in0"), sem("send_in1")]
        rows_set = sem("rows_set")
        marked = sem("marked")
        x_sent = [sem("x_sent0"), sem("x_sent1")]

        def at(weights, e):
            return weights[:, bass.ds(e, 1), :, :].rearrange("p o a c -> p (o a) c")

        def over_tiles(engine, step, each_expert=None, before_routed=None, after_change=None):
            S, R = "shared", "routed"
            step(0, 0, 0, S, None, S)
            step(1, 0, 1, S, S, S)
            step(2, 1, 0, S, S, S)
            with engine.Fori(1, N_EXP + 1) as q:
                if each_expert:
                    each_expert(q - 1)
                step(2 * q + 1, q, 1, S, S, S)
                step(2 * q + 2, q + 1, 0, S, S, S)
            with engine.Fori(N_EXP + 1, CARRY // 2 - 1) as q:
                step(2 * q + 1, q, 1, S, S, S)
                step(2 * q + 2, q + 1, 0, S, S, S)
            step(CARRY - 1, CARRY // 2 - 1, 1, S, S, R)
            if before_routed:
                before_routed()
            step(CARRY, CARRY // 2, 0, R, S, R)
            if after_change:
                after_change()
            step(CARRY + 1, CARRY // 2, 1, R, R, R)
            step(CARRY + 2, CARRY // 2 + 1, 0, R, R, R)
            with engine.Fori(CARRY // 2 + 1, ALL_TILES // 2 - 1) as q:
                step(2 * q + 1, q, 1, R, R, R)
                step(2 * q + 2, q + 1, 0, R, R, R)
            step(ALL_TILES - 1, ALL_TILES // 2 - 1, 1, R, R, None)

        with nc.Block() as block:
            @block.sync
            def _(sp):
                sp.dma_start(bias_bc[:], exp_bias.partition_broadcast(BLK)).then_inc(bias_in, 16)

                def load_x(i, par, shared, k):
                    at_least(sp, t_x, i - 1)
                    stand(sp, passed)
                    if shared:
                        sp.dma_start(x_in[0:BLK, par, :], x_dram[bass.ds(i * BLK, BLK), :]).then_inc(x_loaded[par], 16)
                    else:
                        sp.dma_start(x_in[:, par, :], slots_dram[bass.ds(k * P, P), 0:D]).then_inc(x_loaded[par], 16)

                def load_send(j, half, par):
                    at_least(sp, x_sent[par], 32 * half)
                    stand(sp, passed)
                    for pick in range(TOP):
                        sp.dma_start(send[:, par, pick, 0:D], x_dram[bass.ds(j * BLK, BLK), :]).then_inc(
                            send_in[par], 16)

                def load_slots(k, par):
                    load_x(CARRY + k, par, False, k)
                    sp.dma_start(slot_meta[:, bass.ds(k, 1), :],
                                 slots_dram[bass.ds(k * P, P), D:D + N_META].unsqueeze(1)).then_inc(x_loaded[par], 16)

                sp.wait_ge(consts, 1)
                load_x(0, 0, True, 0)
                load_x(1, 1, True, 1)
                load_send(0, 0, 0)
                load_send(1, 0, 1)
                sp.wait_ge(split_lo, 1)
                load_expert(sp, 0)
                with sp.Fori(1, N_EXP + 1) as q:
                    load_x(2 * q, 0, True, 0)
                    load_x(2 * q + 1, 1, True, 0)
                    load_send(2 * q, q, 0)
                    load_send(2 * q + 1, q, 1)
                    sp.wait_ge(split_lo, q + 1)
                    stand(sp, passed)
                    load_expert(sp, q)
                with sp.Fori(N_EXP + 1, N_ROW // 2) as q:
                    load_x(2 * q, 0, True, 0)
                    load_x(2 * q + 1, 1, True, 0)
                    load_send(2 * q, q, 0)
                    load_send(2 * q + 1, q, 1)
                for par in range(2):
                    sp.wait_ge(x_sent[par], 32 * (N_ROW // 2))
                load_slots(0, 0)
                load_slots(1, 1)
                with sp.Fori(1, N_TILE // 2) as q:
                    load_slots(2 * q, 0)
                    load_slots(2 * q + 1, 1)
                for par in range(2):
                    sp.wait_ge(y_sent[par], 16 * (N_TILE // 2))
                sp.wait_ge(stage_in, 64 * (N_EXP + 2))

            @block.gpsimd
            def _(pool):
                nc.gpsimd.memset(x_in[:], 0.0).then_inc(consts, 1)
                nc.gpsimd.memset(earlier[:], 1.0).then_inc(consts, 1)
                nc.gpsimd.memset(before[:], 1.0).then_inc(consts, 1)
                nc.gpsimd.memset(ones[:], 1.0).then_inc(consts, 1)
                nc.gpsimd.iota(tile_start[:], pattern=[[P, N_ROW]], base=0, channel_multiplier=0,
                               allow_small_or_imprecise_dtypes=True).then_inc(consts, 1)
                nc.gpsimd.iota(tile_no[:], pattern=[[1, N_TILE]], base=0, channel_multiplier=0,
                               allow_small_or_imprecise_dtypes=True).then_inc(consts, 1)
                nc.gpsimd.iota(meta[:, :, :, 0].bitcast(I32), pattern=[[TOP * BLK, N_ROW], [1, TOP]], base=0,
                               channel_multiplier=TOP).then_inc(consts, 1)
                pool.wait_ge(consts, 7)
                nc.gpsimd.affine_select(out=earlier[:], in_=earlier[:], compare_op=ALU.is_ge, fill=0.0, base=-1,
                                        pattern=[[1, N_EXP], [-1, N_EXP]], channel_multiplier=0).then_inc(consts, 1)
                nc.gpsimd.affine_select(out=before[:], in_=before[:], compare_op=ALU.is_ge, fill=0.0, base=-1,
                                        pattern=[[1, BLK]], channel_multiplier=-1).then_inc(consts, 1)

                def send_block(j, half, par):
                    at_least(pool, x_sent[par], 32 * half)
                    stand(pool, passed)
                    nc.gpsimd.tensor_copy(send_to[:, par, :], slot[:, :, j]).then_inc(marked, 1)
                    pool.wait_ge(send_in[par], 32 * half + 32)
                    stand(pool, passed)
                    nc.gpsimd.tensor_copy(send[:, par, :, D:D + N_META].bitcast(I32),
                                          meta[:, j, :, :].bitcast(I32)).then_inc(marked, 1)
                    pool.wait_ge(marked, 2 * j + 2)
                    stand(pool, passed)
                    for pick in range(TOP):
                        nc.gpsimd.indirect_dma_start(
                            out=slots_dram, out_offset=bass.IndirectOffsetOnAxis(ap=send_to[:, par, pick:pick + 1], axis=0),
                            in_=send[:, par, pick, :], in_offset=None, bounds_check=N_TILE * P - 1,
                            oob_is_err=False).then_inc(x_sent[par], 16)

                pool.wait_ge(routed, 1)
                send_block(0, 0, 0)
                send_block(1, 0, 1)
                with pool.Fori(1, N_ROW // 2) as q:
                    send_block(2 * q, q, 0)
                    send_block(2 * q + 1, q, 1)

                def send_y(k, half, par):
                    pool.wait_ge(t_x, CARRY + k + 1)
                    at_least(pool, y_sent[par], 16 * half)
                    stand(pool, passed)
                    nc.gpsimd.tensor_copy(y_row[:, par:par + 1], slot_meta[:, bass.ds(k, 1), 0].bitcast(I32)
                                          ).then_inc(rows_set, 1)
                    pool.wait_ge(rows_set, k + 1)
                    pool.wait_ge(y_ready, k + 3)
                    stand(pool, passed)
                    nc.gpsimd.indirect_dma_start(
                        out=y_dram, out_offset=bass.IndirectOffsetOnAxis(ap=y_row[:, par:par + 1], axis=0),
                        in_=y_out[:, par, :], in_offset=None, bounds_check=N_ALL * TOP - 1,
                        oob_is_err=False).then_inc(y_sent[par], 16)

                send_y(0, 0, 0)
                send_y(1, 0, 1)
                with pool.Fori(1, N_TILE // 2) as q:
                    send_y(2 * q, q, 0)
                    send_y(2 * q + 1, q, 1)

            @block.tensor
            def _(pe):
                def transpose_x(i, half, par, kind):
                    if kind == "shared":
                        pe.wait_ge(x_loaded[par], 16 * half + 16)
                    else:
                        pe.wait_ge(x_loaded[par], 32 * (half - CARRY // 2) + 32 + 16 * (CARRY // 2))
                    at_least(pe, lo_x, i)
                    nc.tensor.transpose(bank[X][:, 0:P], x_in[:, par, 0:P], ident[:])
                    nc.tensor.transpose(bank[X][0:REST, P:2 * P], x_in[:, par, P:D], ident[:]).then_inc(t_x, 1)

                def gate_up(i, par, e):
                    pe.wait_ge(lo_x, i + 1)
                    at_least(pe, prod_done, i - 1)
                    for which, (b, signal) in enumerate([(G, mm_g), (U, mm_u)]):
                        c = slice(which * F, (which + 1) * F)
                        o = bank[b[par]][:, 0:F]
                        nc.tensor.matmul(o, x_t[:, par, 0, :], up_hi[:, e, 0, c], start=True, stop=False)
                        nc.tensor.matmul(o, x_t[:, par, 0, :], up_lo[:, e, 0, c], start=False, stop=False)
                        nc.tensor.matmul(o, x_t[:, par, 1, :], up_hi[:, e, 0, c], start=False, stop=False)
                        nc.tensor.matmul(o, x_t[:, par, 2, :], up_hi[:, e, 1, c], start=False, stop=False)
                        nc.tensor.matmul(o, x_t[:, par, 2, :], up_lo[:, e, 1, c], start=False, stop=True
                                         ).then_inc(signal, 1)

                def transpose_h(i):
                    at_least(pe, lo_h, i)
                    pe.wait_ge(prod_done, i + 1)
                    for f in range(N_CHUNK):
                        mm = nc.tensor.transpose(bank[H][:, f * P:(f + 1) * P], prod[:, f * P:(f + 1) * P], ident[:])
                    mm.then_inc(t_h, 1)

                def down(i, par, e, shared):
                    pe.wait_ge(lo_h, i + 1)
                    if shared:
                        at_least(pe, added, i - 1)
                    else:
                        pe.wait_ge(y_ready, i - CARRY + 1)
                    o = bank[Y[par]][:, 0:D]
                    for f in range(N_CHUNK):
                        nc.tensor.matmul(o, hid_hi[:, f, :], down_hi[:, e, f, :], start=(f == 0), stop=False)
                        nc.tensor.matmul(o, hid_hi[:, f, :], down_lo[:, e, f, :], start=False, stop=False)
                        mm = nc.tensor.matmul(o, hid_lo[:, f, :], down_hi[:, e, f, :], start=False,
                                              stop=(f == N_CHUNK - 1))
                    mm.then_inc(mm_y, 1)

                def expert_of(i, kind):
                    if kind == "shared":
                        return SHARED
                    return pe.value_load(tile_expert[0:1, bass.ds(i - CARRY, 1)], min_val=0, max_val=N_EXP - 1)

                def step(i, half, par, kind, prev, following):
                    if prev:
                        transpose_h(i - 1)
                    if following:
                        transpose_x(i + 1, half + par, par ^ 1, following)
                    gate_up(i, par, expert_of(i, kind))
                    if prev:
                        down(i - 1, par ^ 1, expert_of(i - 1, prev), prev == "shared")

                pe.wait_ge(consts, 9)
                pe.wait_ge(counts_in, 1)
                flat = lambda a: a.rearrange("p r e -> p (r e)")
                nc.tensor.matmul(bank[X][0:BLK, 0:N_ROW * N_EXP], before[:], flat(chosen[:]), start=True, stop=False,
                                 skip_group_check=True)
                nc.tensor.matmul(bank[X][0:BLK, 0:N_ROW * N_EXP], ones[:], flat(prefix[:, 1]), start=False, stop=True,
                                 skip_group_check=True)
                nc.tensor.matmul(bank[H][0:BLK, 0:N_EXP], ones[:], prefix[:, 1, N_ROW - 1, :], start=True, stop=False)
                nc.tensor.matmul(bank[H][0:BLK, 0:N_EXP], ones[:], chosen[:, N_ROW - 1, :], start=False, stop=True
                                 ).then_inc(counted, 1)
                pe.wait_ge(split_lo, 1)
                pe.wait_ge(routed, 1)
                transpose_x(0, 0, 0, "shared")

                def before_routed():
                    pe.wait_ge(split_lo, N_EXP + 1)

                def after_change():
                    pe.wait_ge(added, CARRY)

                over_tiles(pe, step, before_routed=before_routed, after_change=after_change)
                transpose_h(ALL_TILES - 1)
                down(ALL_TILES - 1, 1, expert_of(ALL_TILES - 1, "routed"), False)

            @block.scalar
            def _(act):
                def split_hi_of(e, arrived):
                    act.wait_ge(stage_in, arrived)
                    stand(act, passed)
                    nc.scalar.copy(at(up_hi, e), stage_up[:])
                    nc.scalar.copy(at(down_hi, e), stage_down[:]).then_inc(split_hi, 1)

                def hi_of_x(i, par):
                    at_least(act, mm_u, i - 1)
                    act.wait_ge(t_x, i + 1)
                    nc.scalar.copy(x_t[:, par, 0, :], bank[X][:, 0:P])
                    nc.scalar.copy(x_t[0:REST, par, 2, :], bank[X][0:REST, P:2 * P]).then_inc(hi_x, 1)

                def step(i, half, par, kind, prev, following):
                    if prev:
                        act.wait_ge(t_h, i)
                        at_least(act, mm_y, i - 1)
                        nc.scalar.copy(hid_hi[:], bank[H][:, 0:F].rearrange("p (f t) -> p f t", f=N_CHUNK)
                                       ).then_inc(hi_h, 1)
                    if following:
                        hi_of_x(i + 1, par ^ 1)
                    act.wait_ge(mm_g, i + 1)
                    at_least(act, prod_done, i)
                    nc.scalar.activation(silu[:], bank[G[par]][:, 0:F], ACT.Silu).then_inc(silu_done, 1)
                    if prev == "routed":
                        output(i - 1, half - 1 + par - CARRY // 2, par ^ 1)

                def output(i, pair, par):
                    at_least(act, y_sent[par], 16 * pair)
                    act.wait_ge(mm_y, i + 1)
                    stand(act, passed)
                    nc.scalar.activation(y_out[:, par, :], bank[Y[par]][:, 0:D], ACT.Copy,
                                         scale=slot_meta[:, bass.ds(i - CARRY, 1), 1]).then_inc(y_ready, 1)

                act.sem_inc(y_ready, 2)
                act.wait_ge(soft_in, 1)
                nc.scalar.activation(scores[:], scores[:], ACT.Exp).then_inc(soft_exp, 1)
                split_hi_of(SHARED, 64)
                hi_of_x(0, 0)
                over_tiles(act, step, each_expert=lambda e: split_hi_of(e, 64 * e + 128))
                act.wait_ge(t_h, ALL_TILES)
                act.wait_ge(mm_y, ALL_TILES - 1)
                nc.scalar.copy(hid_hi[:], bank[H][:, 0:F].rearrange("p (f t) -> p f t", f=N_CHUNK)).then_inc(hi_h, 1)
                output(ALL_TILES - 1, N_TILE // 2 - 1, 1)

            @block.vector
            def _(dve):
                done = [0]

                def then(ins):
                    done[0] += 1
                    ins.then_inc(order, 1)
                    dve.wait_ge(order, done[0])

                def split_lo_of(e, n):
                    dve.wait_ge(split_hi, n)
                    stand(dve, passed)
                    nc.vector.tensor_tensor(at(up_lo, e), stage_up[:], at(up_hi, e).bitcast(F32),
                                            ALU.subtract)
                    nc.vector.tensor_tensor(at(down_lo, e), stage_down[:],
                                            at(down_hi, e).bitcast(F32), ALU.subtract).then_inc(split_lo, 1)

                wide = lambda r: r.unsqueeze(2).broadcast_to((BLK, N_ROW, N_EXP))
                per_row = lambda a: a.unsqueeze(1).broadcast_to((BLK, N_ROW, N_EXP))
                then(nc.vector.tensor_reduce(row[:], logits[:], axis=AX.X, op=ALU.max))
                nc.vector.tensor_tensor(scores[:], logits[:], wide(row[:]), ALU.subtract).then_inc(soft_in, 1)
                dve.wait_ge(soft_exp, 1)
                then(nc.vector.tensor_reduce(row[:], scores[:], axis=AX.X, op=ALU.add))
                then(nc.vector.reciprocal(row2[:], row[:]))
                then(nc.vector.tensor_tensor(scores[:], scores[:], wide(row2[:]), ALU.mult))
                dve.wait_ge(bias_in, 16)
                then(nc.vector.tensor_tensor(picks[:], scores[:], per_row(bias_bc[:]), ALU.add))
                dve.wait_ge(consts, 9)
                for c in range(N_ROW // RANK):
                    rows = slice(c * RANK, (c + 1) * RANK)
                    for r in range(RANK):
                        mine = picks[:, c * RANK + r, :].unsqueeze(2).broadcast_to((BLK, N_EXP, N_EXP))
                        other = picks[:, c * RANK + r, :].unsqueeze(1).broadcast_to((BLK, N_EXP, N_EXP))
                        nc.vector.tensor_tensor(above[:, r], other, mine, ALU.is_gt)
                        ins = nc.vector.tensor_tensor(equal[:, r], other, mine, ALU.is_equal)
                    then(ins)
                    pair3 = lambda a: a.rearrange("p r e j -> p r (e j)")
                    then(nc.vector.tensor_tensor(pair3(equal), pair3(equal), earlier[:].rearrange(
                        "p e j -> p (e j)").unsqueeze(1).broadcast_to((BLK, RANK, N_EXP * N_EXP)), ALU.mult))
                    then(nc.vector.tensor_tensor(pair3(above), pair3(above), pair3(equal), ALU.add))
                    then(nc.vector.tensor_reduce(chosen[:, rows, :], above, axis=AX.X, op=ALU.add))
                then(nc.vector.tensor_scalar(chosen[:], chosen[:], TOP - 0.5, None, ALU.is_lt))
                nc.vector.memset(prefix[:, :, 0, :], 0.0)
                then(nc.vector.tensor_copy(prefix[:, 0, 1:N_ROW, :], chosen[:, 0:N_ROW - 1, :]))
                now, dist = 0, 1
                while dist < N_ROW:
                    nc.vector.tensor_copy(prefix[:, 1 - now, 0:dist, :], prefix[:, now, 0:dist, :])
                    then(nc.vector.tensor_tensor(prefix[:, 1 - now, dist:N_ROW, :], prefix[:, now, dist:N_ROW, :],
                                                 prefix[:, now, 0:N_ROW - dist, :], ALU.add))
                    now, dist = 1 - now, 2 * dist
                assert now == 1
                nc.vector.tensor_copy(row[:, 0:1], row[:, 0:1]).then_inc(counts_in, 1)
                then(nc.vector.tensor_tensor(picks[:], chosen[:], scores[:], ALU.mult))
                then(nc.vector.tensor_reduce(row[:], picks[:], axis=AX.X, op=ALU.add))
                then(nc.vector.tensor_scalar(row[:], row[:], 1e-9, None, ALU.add))
                then(nc.vector.reciprocal(row2[:], row[:]))
                then(nc.vector.tensor_tensor(picks[:], picks[:], wide(row2[:]), ALU.mult))
                dve.wait_ge(counted, 1)
                then(nc.vector.tensor_copy(last_tile[:], bank[H][0:BLK, 0:N_EXP]))
                then(nc.vector.tensor_tensor(filled, last_tile[:].unsqueeze(2).broadcast_to((BLK, N_EXP, N_ROW)),
                                             tile_start[:].unsqueeze(1).broadcast_to((BLK, N_EXP, N_ROW)), ALU.is_gt))
                then(nc.vector.tensor_reduce(n_tiles[:], filled, axis=AX.X, op=ALU.add))
                then(nc.vector.tensor_tensor(above[:, 0], earlier[:],
                                             n_tiles[:].unsqueeze(1).broadcast_to((BLK, N_EXP, N_EXP)), ALU.mult))
                then(nc.vector.tensor_reduce(first_tile[:], above[:, 0], axis=AX.X, op=ALU.add))
                then(nc.vector.tensor_tensor(last_tile[:], first_tile[:], n_tiles[:], ALU.add))
                then(nc.vector.tensor_tensor(over, tile_no[:].unsqueeze(2).broadcast_to((1, N_TILE, N_EXP)),
                                             last_tile[0:1, :].unsqueeze(1).broadcast_to((1, N_TILE, N_EXP)), ALU.is_ge))
                then(nc.vector.tensor_reduce(tile_expert_f[:], over, axis=AX.X, op=ALU.add))
                then(nc.vector.tensor_scalar(tile_expert[:], tile_expert_f[:], float(N_EXP - 1), None, ALU.min))
                then(nc.vector.tensor_scalar(first_tile[:], first_tile[:], float(P), None, ALU.mult))
                then(nc.vector.tensor_tensor(scores[:], bank[X][0:BLK, 0:N_ROW * N_EXP].rearrange(
                    "p (r e) -> p r e", e=N_EXP), per_row(first_tile[:]), ALU.add))
                then(nc.vector.tensor_tensor(chosen[:], scores[:], chosen[:], ALU.mult))
                then(nc.vector.tensor_reduce(slot[:, 1, :], chosen[:], axis=AX.X, op=ALU.max))
                then(nc.vector.tensor_reduce(row[:], chosen[:], axis=AX.X, op=ALU.add))
                then(nc.vector.tensor_tensor(slot[:, 0, :], row[:], slot[:, 1, :], ALU.subtract))
                then(nc.vector.tensor_tensor(scores[:], scores[:], wide(slot[:, 1, :]), ALU.is_equal))
                then(nc.vector.tensor_tensor(scores[:], scores[:], picks[:], ALU.mult))
                then(nc.vector.tensor_tensor(picks[:], picks[:], scores[:], ALU.subtract))
                nc.vector.tensor_reduce(meta[:, :, 0, 1], picks[:], axis=AX.X, op=ALU.add)
                nc.vector.tensor_reduce(meta[:, :, 1, 1], scores[:], axis=AX.X, op=ALU.add).then_inc(routed, 1)

                def lo_of_x(i, par):
                    dve.wait_ge(hi_x, i + 1)
                    nc.vector.tensor_tensor(x_t[:, par, 1, :], bank[X][:, 0:P], x_t[:, par, 0, :].bitcast(F32),
                                            ALU.subtract)
                    nc.vector.tensor_tensor(x_t[REST:P, par, 2, :], bank[X][0:REST, P:2 * P],
                                            x_t[0:REST, par, 2, :].bitcast(F32), ALU.subtract).then_inc(lo_x, 1)

                def lo_of_h(i):
                    dve.wait_ge(hi_h, i + 1)
                    nc.vector.tensor_tensor(hid_lo[:], bank[H][:, 0:F].rearrange("p (f t) -> p f t", f=N_CHUNK),
                                            hid_hi[:].bitcast(F32), ALU.subtract).then_inc(lo_h, 1)

                h_rows = h_all[:].rearrange("p s t d -> p (s t) d")

                def step(i, half, par, kind, prev, following):
                    if prev:
                        lo_of_h(i - 1)
                    if following:
                        lo_of_x(i + 1, par ^ 1)
                    dve.wait_ge(silu_done, i + 1)
                    dve.wait_ge(mm_u, i + 1)
                    at_least(dve, t_h, i)
                    nc.vector.tensor_tensor(prod[:], silu[:], bank[U[par]][:, 0:F], ALU.mult).then_inc(prod_done, 1)
                    if prev == "shared":
                        dve.wait_ge(mm_y, i)
                        h = h_rows[:, i - 1, :]
                        nc.vector.tensor_tensor(h, bank[Y[par ^ 1]][0:BLK, 0:D], h, ALU.add).then_inc(added, 1)

                split_lo_of(SHARED, 1)
                lo_of_x(0, 0)
                over_tiles(dve, step, each_expert=lambda e: split_lo_of(e, e + 2))
                lo_of_h(ALL_TILES - 1)


def final_stage(nc, sem, h_all, y_dram, out):
    with ExitStack() as ctx:
        y = ctx.enter_context(nc.sbuf_tensor("y_picks", [BLK, N_SEQ, N_BLK, TOP, D], F32))
        y_in = [sem(f"y_in{s}") for s in range(N_SEQ)]
        half_sum, summed, stored = sem("half_sum"), sem("summed"), sem("stored")
        with nc.Block() as block:
            @block.sync
            def _(sp):
                for s in range(N_SEQ):
                    rows = y_dram[s * N_TOK * TOP:(s + 1) * N_TOK * TOP, :]
                    sp.dma_start(y[:, s], rows.rearrange("(t p w) d -> p t w d", p=BLK, w=TOP)).then_inc(y_in[s], 16)
                for s in range(N_SEQ):
                    sp.wait_ge(summed, s + 1)
                    sp.dma_start(out[s].rearrange("(t p) d -> p t d", p=BLK), h_all[:, s, :, :]).then_inc(stored, 16)
                sp.wait_ge(stored, 16 * N_SEQ)

            @block.vector
            def _(dve):
                for s in range(N_SEQ):
                    h = h_all[:, s, :, :]
                    dve.wait_ge(y_in[s], 16)
                    nc.vector.tensor_tensor(h, h, y[:, s, :, 0, :], ALU.add).then_inc(half_sum, 1)
                    dve.wait_ge(half_sum, s + 1)
                    nc.vector.tensor_tensor(h, h, y[:, s, :, 1, :], ALU.add).then_inc(summed, 1)


_IN_ORDER = ["frames", "dft", "mel2", "dct", "w_mfcc", "b_tok", "w_pack", "b_qk_col", "b_v", "b_gate_col", "ln_b_col",
             "ln_g_col", "b_proj", "head_main", "head_rest", "exp_bias", "w_up", "w_down"]


def lay_out(x, L0_tok_mel_filters, L0_tok_dct, L0_tok_w_proj, L0_tok_b_proj, L0_attn_W_qkv, L0_attn_b_qkv,
            L0_attn_W_gate, L0_attn_b_gate, L0_attn_W_proj, L0_attn_b_proj, L0_attn_ln_g, L0_attn_ln_b,
            L0_ffn_w_router, L0_ffn_expert_bias, L0_ffn_Wg, L0_ffn_Wu, L0_ffn_Wd, L0_ffn_sg, L0_ffn_su, L0_ffn_sd):
    k = np.arange(N_BINS)[None, :]
    j = np.arange(FRAME)[:, None]
    window = (0.54 - 0.46 * np.cos(2.0 * np.pi * j / (FRAME - 1)))
    angle = 2.0 * np.pi * ((j * k) % FRAME) / FRAME
    dft = np.concatenate([window * np.cos(angle), -window * np.sin(angle)], axis=1).astype(np.float32)
    head_of = np.arange(P)[:, None] // DH
    return {
        "frames": x.reshape(N_SEQ, N_TOK, STEP)[:, :, :FRAME].transpose(2, 0, 1),
        "dft": dft,
        "mel2": np.concatenate([L0_tok_mel_filters.T, L0_tok_mel_filters.T], axis=0),
        "dct": L0_tok_dct,
        "w_mfcc": L0_tok_w_proj,
        "b_tok": L0_tok_b_proj.reshape(1, D),
        "w_pack": np.concatenate([L0_attn_W_qkv, L0_attn_W_gate, L0_attn_W_proj, L0_ffn_w_router.T], axis=1),
        "b_qk_col": L0_attn_b_qkv[:2 * D].reshape(2 * D, 1),
        "b_v": L0_attn_b_qkv[2 * D:],
        "b_gate_col": L0_attn_b_gate.reshape(D, 1),
        "ln_b_col": L0_attn_ln_b.reshape(D, 1),
        "ln_g_col": L0_attn_ln_g.reshape(D, 1),
        "b_proj": L0_attn_b_proj,
        "head_main": (head_of == np.arange(HEADS_MAIN)[None, :]).astype(np.float32),
        "head_rest": (head_of[:REST] == np.arange(HEADS - HEADS_MAIN)[None, :]).astype(np.float32),
        "exp_bias": L0_ffn_expert_bias,
        "w_up": np.concatenate([
            np.concatenate([L0_ffn_Wg, L0_ffn_sg[None]], axis=0).transpose(0, 2, 1),
            np.concatenate([L0_ffn_Wu, L0_ffn_su[None]], axis=0).transpose(0, 2, 1)], axis=2),
        "w_down": np.concatenate([L0_ffn_Wd, L0_ffn_sd[None]], axis=0).transpose(0, 2, 1).reshape(
            N_EXP + 1, N_CHUNK, P, D).transpose(0, 2, 1, 3),
    }


def kernel(**inputs):
    import concourse.bacc as bacc
    from concourse.bass_utils import run_bass_kernel_spmd

    nc = bacc.Bacc("TRN2", target_bir_lowering=False, num_devices=1)
    laid = lay_out(**{name: np.asarray(a) for name, a in inputs.items()})
    arrays, args = {}, []
    for name in _IN_ORDER:
        a = np.ascontiguousarray(laid[name])
        arrays[f"in_{name}"] = a
        args.append(nc.dram_tensor(f"in_{name}", a.shape, mybir.dt.from_np(a.dtype), kind="ExternalInput").ap())
    out = nc.dram_tensor("out_dram", (N_SEQ, N_TOK, D), F32, kind="ExternalOutput").ap()
    build(nc, *args, out)
    got = run_bass_kernel_spmd(nc, [arrays], core_ids=[0])
    return got.results[0]["out_dram"]
```

```python
from contextlib import ExitStack

import numpy as np

import concourse.bass as bass
from concourse import mybir

F32 = mybir.dt.float32
F32R = mybir.dt.float32r
I32 = mybir.dt.int32
ACT = mybir.ActivationFunctionType
ALU = mybir.AluOpType
AX = mybir.AxisListType

P = 128
N_SEQ = 8
FRAME = 100
STEP = 160
N_TOK = 500
N_BLK = 4
BLK = N_TOK // N_BLK
D = 192
REST = D - P
HEADS = 12
DH = D // HEADS
HEADS_MAIN = P // DH
N_MEL = 40
N_BINS = FRAME // 2 + 1
N_MFCC = 13
N_EXP = 8
F = 384
N_CHUNK = F // P
LN_EPS = 1e-5
VA = DH + 1
GRP = 4
N_GRP = HEADS // GRP
POOL_HEADS = 3
COL_Q, COL_K, COL_V, COL_G, COL_P, COL_R = 0, D, 2 * D, 3 * D, 4 * D, 5 * D
N_PACK = 5 * D + N_EXP
TOP = 2
N_ROW = N_SEQ * N_BLK
N_ALL = N_SEQ * N_TOK
N_TILE = (TOP * N_ALL + N_EXP * (P - 1)) // P
N_META = 2
BEATEN = 3e38
NOWHERE = 1 << 29


def at_least(engine, semaphore, value):
    if not isinstance(value, int) or value > 0:
        engine.wait_ge(semaphore, value)


def stand(engine, passed):
    engine.sem_inc(passed, 1)


def build(nc, frames, dft, mel2, dct, w_mfcc, b_tok, w_pack, b_qk_col, b_v, b_gate_col, ln_b_col, ln_g_col,
          b_proj, head_main, head_rest, exp_bias, w_up, w_down, out):
    with ExitStack() as ctx:
        def sb(name, shape, dt=F32):
            return ctx.enter_context(nc.sbuf_tensor(name, shape, dt))

        def sem(name):
            return ctx.enter_context(nc.semaphore(name))

        bank = [ctx.enter_context(nc.psum_tensor(f"bank{i}", [P, 512], F32)) for i in range(8)]

        h_all = sb("h_all", [BLK, N_SEQ, N_BLK, D])
        logits = sb("logits", [BLK, N_ROW, N_EXP])
        ident = sb("ident", [P, P])
        stage_up = sb("stage_up", [P, 2, 2 * F])
        stage_down = sb("stage_down", [P, N_CHUNK, D])
        stage_in = [sem("stage_in0"), sem("stage_in1")]
        x_dram = nc.dram_tensor("x_dram", (N_ALL, D), F32).ap()
        slots_dram = nc.dram_tensor("slots_dram", (N_TILE * P, D + N_META), F32).ap()
        y_dram = nc.dram_tensor("y_dram", (N_ALL * TOP, D), F32).ap()
        passed = sem("passed")
        loaded = sem("loaded")
        made = sem("made")

        def load_expert(sp, e, piece):
            if piece == 0:
                sp.dma_start(stage_up[:, 0, :], w_up[e, 0:P, :]).then_inc(stage_in[0], 16)
            else:
                sp.dma_start(stage_up[0:REST, 1, :], w_up[e, P:D, :]).then_inc(stage_in[1], 16)
                sp.dma_start(stage_up[REST:P, 1, :], w_up[e, P:D, :]).then_inc(stage_in[1], 16)
                sp.dma_start(stage_down[:], w_down[e]).then_inc(stage_in[1], 16)

        attn_stage(nc, passed, sem, bank, h_all, x_dram, slots_dram, logits, ident, made, loaded, load_expert,
                   frames, dft, mel2, dct, w_mfcc, b_tok, w_pack, b_qk_col, b_v, b_gate_col, ln_b_col, ln_g_col,
                   b_proj, head_main, head_rest)
        moe_stage(nc, passed, sem, bank, h_all, x_dram, slots_dram, y_dram, logits, ident, stage_up, stage_down,
                  stage_in, load_expert, exp_bias, out)


def attn_stage(nc, passed, sem, bank, h_all, x_dram, slots_dram, logits, ident, made, loaded, load_expert,
               frames, dft, mel2, dct, w_mfcc, b_tok, w_pack, b_qk_col, b_v, b_gate_col, ln_b_col, ln_g_col, b_proj, head_main,
               head_rest):
    with ExitStack() as ctx:
        def sb(name, shape, dt=F32):
            return ctx.enter_context(nc.sbuf_tensor(name, shape, dt))

        pack_raw = sb("pack_raw", [P, 2, N_PACK])
        pack_hi = sb("pack_hi", [P, 2, N_PACK], F32R)
        pack_lo = sb("pack_lo", [P, 2, N_PACK], F32R)
        w_router = sb("w_router_sb", [P, 2, N_EXP])
        ln_b = sb("ln_b", [P, 2])
        ln_g = sb("ln_g", [P, 2])
        ln_b_wide = sb("ln_b_wide", [P, 2, BLK])
        bqk = sb("bqk", [P, 4])
        bgate = sb("bgate", [P, 2])
        bgate_half = sb("bgate_half", [P, 2])
        bv_bc = sb("bv_bc", [BLK, D])
        bproj_bc = sb("bproj_bc", [BLK, D])
        causal = sb("causal", [BLK, BLK])
        hm_main = sb("hm_main", [P, HEADS_MAIN])
        hm_rest = sb("hm_rest", [REST, HEADS - HEADS_MAIN])
        minus_half = sb("minus_half", [BLK, N_BLK])
        empty_slot = sb("empty_slot", [P, D + N_META])
        ln_eps_tile = sb("log_eps", [P, 1])

        stats = sb("stats", [BLK, N_BLK, 6])
        moments = sb("moments", [BLK, N_BLK, 2])
        var_eps = sb("var_eps", [BLK, N_BLK])
        rstd = sb("rstd", [BLK, N_BLK])
        hn = sb("hn", [BLK, N_BLK, D])
        z = sb("z", [BLK, N_BLK, D])
        x2 = sb("x2", [BLK, N_BLK, D])
        hb = sb("hb", [BLK, N_BLK, D])
        hn_t = sb("hn_t", [P, 3, N_TOK], F32R)
        z_t = sb("z_t", [P, 3, N_TOK], F32R)
        a_t = sb("a_t", [P, 3, N_TOK], F32R)
        gate = sb("gate", [P, 2, N_TOK])
        kg = sb("kg", [P, 2, N_TOK])
        x_t = kg
        k_exp = sb("k_exp", [P, 2, N_TOK])
        k_pos = sb("k_pos", [P, 2, N_TOK])
        kf = sb("kf", [P, 2, N_TOK])
        kh = sb("kh", [P, HEADS, N_TOK])
        logits_t = k_exp[0:N_EXP, 0, :]
        q_exp, q_pos = k_exp, k_pos
        qf = sb("qf", [P, 2, N_TOK])
        v_aug = sb("v_aug", [BLK, N_BLK, HEADS, VA])
        k_tok = sb("k_tok", [BLK, N_BLK - 1, D])
        state = sb("state", [P, N_BLK, HEADS_MAIN * VA])
        state_r = sb("state_r", [P, N_BLK, (HEADS - HEADS_MAIN) * VA])
        probs = pack_raw[0:BLK, :, :].rearrange("p a c -> p (a c)")[:, 0:3 * GRP * BLK].rearrange(
            "p (r c) -> p r c", r=3)
        den = sb("den", [BLK, HEADS])
        rden = sb("rden", [BLK, HEADS])
        attn = sb("attn", [BLK, N_BLK, D])

        centred = sem("centred")
        rooted = sem("rooted")
        chain = sem("chain")
        hn_done, z_done, x2_done = sem("hn_done"), sem("z_done"), sem("x2_done")
        t_hn, t_z, t_a, t_x = sem("t_hn"), sem("t_z"), sem("t_a"), sem("t_x")
        LN_STEPS = 3
        LN_PER_SEQ = 3

        def norm_stats(dve, src, which):
            for t in range(N_BLK):
                ins = nc.vector.bn_stats(stats[:, t, :], src(t))
            ins.then_inc(chain, 1)
            dve.wait_ge(chain, which * LN_STEPS + 1)
            stand(dve, passed)
            for t in range(N_BLK):
                ins = nc.vector.bn_aggr(moments[:, t, :], stats[:, t, :])
            ins.then_inc(chain, 1)
            dve.wait_ge(chain, which * LN_STEPS + 2)
            stand(dve, passed)
            nc.vector.tensor_scalar(var_eps[:], moments[:, :, 1], LN_EPS, None, ALU.add).then_inc(centred, 1)

        def norm_apply(dve, src, dst, which, signal):
            dve.wait_ge(rooted, which + 1)
            for t in range(N_BLK):
                ins = nc.vector.tensor_scalar(dst[:, t, :], src(t), moments[:, t, 0:1], rstd[:, t:t + 1],
                                              ALU.subtract, ALU.mult)
                if t == N_BLK - 2:
                    ins.then_inc(chain, 1)
            ins.then_inc(signal, 1)

        def norm_h_stats(dve, n, which):
            norm_stats(dve, lambda t: h_all[:, n, t, :], which)

        def norm_h_apply(dve, n, which):
            at_least(dve, t_hn, 2 * n)
            norm_apply(dve, lambda t: h_all[:, n, t, :], hn, which, hn_done)

        def norm_hn_stats(dve, n, which):
            dve.wait_ge(hn_done, n + 1)
            stand(dve, passed)
            norm_stats(dve, lambda t: hn[:, t, :], which + 1)

        def norm_hn_apply(dve, n, which):
            at_least(dve, t_z, 2 * n)
            norm_apply(dve, lambda t: hn[:, t, :], z, which + 1, z_done)

        def root(pool, which):
            pool.wait_ge(centred, which + 1)
            nc.gpsimd.tensor_tensor(rstd[:], var_eps[:], minus_half[:], ALU.pow).then_inc(rooted, 1)

        with ExitStack() as tok_ctx:
            def tok_sb(name, shape, dt=F32):
                return tok_ctx.enter_context(nc.sbuf_tensor(name, shape, dt))

            fr = kh[0:FRAME, 0:N_SEQ, :]
            dft_sb = tok_sb("dft_sb", [FRAME, 2 * N_BINS])
            mel_sb = tok_sb("mel_sb", [2 * N_BINS, N_MEL])
            dct_sb = tok_sb("dct_sb", [N_MFCC, N_MEL])
            wm_sb = tok_sb("wm_sb", [N_MFCC, D])
            to_h = tok_sb("to_h", [N_MEL + 1, D])
            squares = tok_sb("squares", [2 * N_BINS, N_TOK])
            logmel = tok_sb("logmel", [N_MEL + 1, N_TOK])
            wts_in, pack_in, frames_in = sem("wts_in"), sem("pack_in"), sem("frames_in")
            spectrum, squared, melled, logged = sem("spectrum"), sem("squared"), sem("melled"), sem("logged")
            token_mm, token_out, fused, fused_out = sem("token_mm"), sem("token_out"), sem("fused"), sem("fused_out")
            bias_mm, bias_out, split_hi, split_lo = sem("bias_mm"), sem("bias_out"), sem("split_hi"), sem("split_lo")
            scaled, wide_b = sem("scaled"), sem("wide_b")
            N_SMALL = 16

            with nc.Block() as block:
                @block.sync
                def _(sp):
                    sp.dma_start(dft_sb[:], dft).then_inc(frames_in, 16)
                    sp.dma_start(fr, frames).then_inc(frames_in, 16)
                    sp.dma_start(mel_sb[:], mel2).then_inc(frames_in, 16)
                    sp.dma_start(dct_sb[:], dct).then_inc(wts_in, 16)
                    sp.dma_start(wm_sb[:], w_mfcc).then_inc(wts_in, 16)
                    sp.dma_start(to_h[N_MEL:N_MEL + 1, :], b_tok).then_inc(wts_in, 16)
                    sp.dma_start(pack_raw[:, 0, :], w_pack[0:P, :]).then_inc(pack_in, 16)
                    sp.dma_start(pack_raw[0:REST, 1, :], w_pack[P:D, :]).then_inc(pack_in, 16)
                    sp.dma_start(pack_raw[REST:P, 1, :], w_pack[P:D, :]).then_inc(pack_in, 16)
                    for half in range(2):
                        lo, n = half * P, (P, REST)[half]
                        sp.dma_start(bqk[0:n, half:half + 1], b_qk_col[lo:lo + n, :]).then_inc(wts_in, 16)
                        sp.dma_start(bqk[0:n, 2 + half:3 + half], b_qk_col[D + lo:D + lo + n, :]).then_inc(wts_in, 16)
                        sp.dma_start(bgate[0:n, half:half + 1], b_gate_col[lo:lo + n, :]).then_inc(wts_in, 16)
                        sp.dma_start(ln_b[0:n, half:half + 1], ln_b_col[lo:lo + n, :]).then_inc(wts_in, 16)
                    sp.dma_start(ln_g[:, 0:1], ln_g_col[0:P, :]).then_inc(wts_in, 16)
                    sp.dma_start(ln_g[0:REST, 1:2], ln_g_col[P:D, :]).then_inc(wts_in, 16)
                    sp.dma_start(ln_g[REST:P, 1:2], ln_g_col[P:D, :]).then_inc(wts_in, 16)
                    sp.dma_start(bv_bc[:], b_v.partition_broadcast(BLK)).then_inc(wts_in, 16)
                    sp.dma_start(bproj_bc[:], b_proj.partition_broadcast(BLK)).then_inc(wts_in, 16)
                    sp.dma_start(hm_main[:], head_main).then_inc(loaded, 16)
                    sp.dma_start(hm_rest[:], head_rest).then_inc(loaded, 16)
                    load_expert(sp, N_EXP, 0)
                    load_expert(sp, N_EXP, 1)

                @block.gpsimd
                def _(pool):
                    nc.gpsimd.memset(ident[:], 0.0).then_inc(made, 1)
                    nc.gpsimd.memset(causal[:], 1.0).then_inc(made, 1)
                    nc.gpsimd.memset(ln_eps_tile[:], 1e-6).then_inc(made, 1)
                    nc.gpsimd.memset(logmel[:], 1.0).then_inc(made, 1)
                    nc.gpsimd.memset(minus_half[:], -0.5).then_inc(made, 1)
                    pool.wait_ge(made, 5)
                    nc.gpsimd.affine_select(out=ident[:], in_=ident[:], compare_op=ALU.not_equal, fill=1.0, base=0,
                                            pattern=[[-1, P]], channel_multiplier=1).then_inc(made, 1)
                    nc.gpsimd.affine_select(out=causal[:], in_=causal[:], compare_op=ALU.is_ge, fill=0.0, base=0,
                                            pattern=[[1, BLK]], channel_multiplier=-1).then_inc(made, 1)
                    nc.gpsimd.memset(v_aug[:], 1.0).then_inc(made, 1)
                    nc.gpsimd.memset(state[:, 0, :], 0.0).then_inc(made, 1)
                    nc.gpsimd.memset(state_r[:], 0.0).then_inc(made, 1)
                    pool.wait_ge(made, 10)
                    nc.gpsimd.memset(qf[REST:P, 1, :], 0.0).then_inc(made, 1)
                    nc.gpsimd.memset(kh[REST:P, HEADS_MAIN:HEADS, :], 0.0).then_inc(made, 1)
                    pool.wait_ge(made, 12)
                    nc.gpsimd.memset(empty_slot[:], 0.0).then_inc(made, 1)
                    pool.wait_ge(made, 13)
                    nc.gpsimd.memset(empty_slot[:, D:D + 1].bitcast(I32), NOWHERE).then_inc(made, 1)
                    pool.wait_ge(wts_in, 16 * N_SMALL)
                    nc.gpsimd.memset(ln_b_wide[:], 0.0).then_inc(wide_b, 1)
                    pool.wait_ge(wide_b, 1)
                    nc.gpsimd.tensor_scalar(ln_b_wide[:, 0, :], ln_b_wide[:, 0, :], ln_b[:, 0:1], None,
                                            ALU.add).then_inc(wide_b, 1)
                    nc.gpsimd.tensor_scalar(ln_b_wide[0:REST, 1, :], ln_b_wide[0:REST, 1, :], ln_b[0:REST, 1:2], None,
                                            ALU.add).then_inc(wide_b, 1)
                    root(pool, 0)
                    root(pool, 1)

                @block.tensor
                def _(pe):
                    def spectrum_of(n):
                        nc.tensor.matmul(bank[0][0:2 * N_BINS, 0:N_TOK], dft_sb[:], fr[:, n, :],
                                         start=True, stop=True).then_inc(spectrum, 1)

                    def tokens_of(n, first):
                        pe.wait_ge(squared, n + 1)
                        if not first:
                            pe.wait_ge(logged, n)
                        nc.tensor.matmul(bank[2][0:N_MEL, 0:N_TOK], mel_sb[:], squares[:],
                                         start=True, stop=True).then_inc(melled, 1)

                    def features_of(n, first):
                        pe.wait_ge(logged, n + 1)
                        if not first:
                            pe.wait_ge(token_out, 2 * n)
                        for t in range(N_BLK):
                            mm = nc.tensor.matmul(bank[4 + t // 2][0:BLK, (t % 2) * D:(t % 2 + 1) * D],
                                                  logmel[:, t * BLK:(t + 1) * BLK], to_h[:],
                                                  start=(t % 2 == 0), stop=(t % 2 == 1), skip_group_check=True)
                            if t % 2:
                                mm.then_inc(token_mm, 1)

                    pe.wait_ge(made, 4)
                    pe.wait_ge(frames_in, 48)
                    spectrum_of(0)
                    tokens_of(0, True)
                    spectrum_of(1)
                    pe.wait_ge(wts_in, 16 * N_SMALL)
                    nc.tensor.matmul(bank[3][0:N_MEL, 0:D], dct_sb[:], wm_sb[:], start=True, stop=True).then_inc(fused, 1)
                    pe.wait_ge(pack_in, 48)
                    pe.wait_ge(wide_b, 3)
                    for n, (lo, m) in enumerate([(COL_Q, P), (COL_Q + P, REST), (COL_K, P), (COL_K + P, REST)]):
                        nc.tensor.matmul(bank[6][0:m, n:n + 1], pack_raw[:, 0, lo:lo + m], ln_b[:, 0:1],
                                         start=(n == 0), stop=False, skip_group_check=True)
                        nc.tensor.matmul(bank[6][0:m, n:n + 1], pack_raw[0:REST, 1, lo:lo + m], ln_b[0:REST, 1:2],
                                         start=False, stop=True, skip_group_check=True)
                    nc.tensor.matmul(bank[1][0:BLK, 0:D], ln_b_wide[:, 0, :], pack_raw[:, 0, COL_V:COL_V + D],
                                     start=True, stop=False)
                    nc.tensor.matmul(bank[1][0:BLK, 0:D], ln_b_wide[0:REST, 1, :], pack_raw[0:REST, 1, COL_V:COL_V + D],
                                     start=False, stop=True).then_inc(bias_mm, 1)
                    pe.wait_ge(fused_out, 1)
                    features_of(0, True)
                    with pe.Fori(1, N_SEQ - 1) as n:
                        tokens_of(n, False)
                        spectrum_of(n + 1)
                        features_of(n, False)
                    tokens_of(N_SEQ - 1, False)
                    features_of(N_SEQ - 1, False)

                @block.scalar
                def _(act):
                    def square_of(n, first):
                        act.wait_ge(spectrum, n + 1)
                        if not first:
                            act.wait_ge(melled, n)
                        nc.scalar.activation(squares[:], bank[0][0:2 * N_BINS, 0:N_TOK], ACT.Square).then_inc(squared, 1)

                    def log_of(n, first):
                        act.wait_ge(melled, n + 1)
                        if not first:
                            act.wait_ge(token_mm, 2 * n)
                        nc.scalar.activation(logmel[0:N_MEL, :], bank[2][0:N_MEL, 0:N_TOK], ACT.Ln,
                                             bias=ln_eps_tile[0:N_MEL, :]).then_inc(logged, 1)

                    act.wait_ge(made, 4)
                    square_of(0, True)
                    log_of(0, True)
                    act.wait_ge(scaled, 2)
                    nc.scalar.copy(pack_hi[:, 0, :], pack_raw[:, 0, :]).then_inc(split_hi, 1)
                    nc.scalar.copy(pack_hi[:, 1, :], pack_raw[:, 1, :]).then_inc(split_hi, 1)
                    nc.scalar.copy(w_router[:], pack_raw[:, :, COL_R:COL_R + N_EXP]).then_inc(split_hi, 1)
                    nc.scalar.mul(bgate_half[:, 0:1], bgate[:, 0:1], 0.5)
                    nc.scalar.mul(bgate_half[0:REST, 1:2], bgate[0:REST, 1:2], 0.5).then_inc(split_hi, 1)
                    with act.Fori(1, N_SEQ) as n:
                        square_of(n, False)
                        log_of(n, False)

                @block.vector
                def _(dve):
                    dve.wait_ge(wts_in, 16 * N_SMALL)
                    dve.wait_ge(fused, 1)
                    nc.vector.tensor_copy(to_h[0:N_MEL, :], bank[3][0:N_MEL, 0:D]).then_inc(fused_out, 1)
                    dve.wait_ge(bias_mm, 1)
                    for n, m in enumerate([P, REST, P, REST]):
                        nc.vector.tensor_tensor(bqk[0:m, n:n + 1], bank[6][0:m, n:n + 1], bqk[0:m, n:n + 1],
                                                ALU.add).then_inc(bias_out, 1)
                    nc.vector.tensor_tensor(bv_bc[:], bank[1][0:BLK, 0:D], bv_bc[:], ALU.add).then_inc(bias_out, 1)
                    for part in range(2):
                        nc.vector.tensor_scalar(pack_raw[:, part, 0:3 * D], pack_raw[:, part, 0:3 * D],
                                                ln_g[:, part:part + 1], None, ALU.mult).then_inc(scaled, 1)
                    for part in range(2):
                        dve.wait_ge(split_hi, part + 1)
                        nc.vector.tensor_tensor(pack_lo[:, part, :], pack_raw[:, part, :],
                                                pack_hi[:, part, :].bitcast(F32), ALU.subtract).then_inc(split_lo, 1)

                    def tokens_out(n):
                        for pair in range(2):
                            dve.wait_ge(token_mm, 2 * n + pair + 1)
                            nc.vector.tensor_copy(h_all[:, n, 2 * pair:2 * pair + 2, :],
                                                  bank[4 + pair][0:BLK, 0:2 * D].rearrange("p (t d) -> p t d", t=2)
                                                  ).then_inc(token_out, 1)

                    with dve.Fori(0, N_SEQ - 2) as n:
                        tokens_out(n)
                    norm_h_stats(dve, 0, 0)
                    tokens_out(N_SEQ - 2)
                    norm_h_apply(dve, 0, 0)
                    norm_hn_stats(dve, 0, 0)
                    norm_hn_apply(dve, 0, 0)
                    tokens_out(N_SEQ - 1)

        hi_hn, hi_z, hi_a = sem("hi_hn"), sem("hi_z"), sem("hi_a")
        lo_hn, lo_z, lo_a = sem("lo_hn"), sem("lo_z"), sem("lo_a")
        x_copied = sem("x_copied")
        by_expert, t_logits = sem("by_expert"), sem("t_logits")
        mm_gk, mm_q, mm_v = sem("mm_gk"), sem("mm_q"), sem("mm_v")
        tanh_done, gate_done = sem("tanh_done"), sem("gate_done")
        kg_done, kexp_done, kpos_done, kf_done = sem("kg_done"), sem("kexp_done"), sem("kpos_done"), sem("kf_done")
        kh_dve, kh_act, kh_pool = sem("kh_dve"), sem("kh_act"), sem("kh_pool")
        qexp_done, qpos_done, qf_done = sem("qexp_done"), sem("qpos_done"), sem("qf_done")
        v_done, t_k, ktok_done, mm_kv, state_done = (sem("v_done"), sem("t_k"), sem("ktok_done"), sem("mm_kv"),
                                                     sem("state_done"))
        scores_done, probs_dve, probs_act, probs_pool = (sem("scores_done"), sem("probs_dve"), sem("probs_act"),
                                                         sem("probs_pool"))
        pv_done, den_done, rden_done, attn_done = sem("pv_done"), sem("den_done"), sem("rden_done"), sem("attn_done")
        hb_done, mm_proj, h_done, mm_rt, logits_done = (sem("hb_done"), sem("mm_proj"), sem("h_done"), sem("mm_rt"),
                                                        sem("logits_done"))
        x_stored, emptied = sem("x_stored"), sem("emptied")
        masked = sem("masked")
        N_SC = N_BLK * N_GRP

        def halves(t3):
            return [(t3[:, 0, :], P), (t3[0:REST, 1, :], REST)]

        with nc.Block() as block:
            @block.sync
            def _(sp):
                sp.sem_inc(x_stored, 16)
                sp.dma_start(slots_dram.rearrange("(t p) c -> p t c", p=P),
                             empty_slot[:].unsqueeze(1).broadcast_to((P, N_TILE, D + N_META))).then_inc(emptied, 16)
                with sp.Fori(0, N_SEQ) as n:
                    sp.wait_ge(x2_done, n + 1)
                    stand(sp, passed)
                    sp.dma_start(x_dram[bass.ds(n * N_TOK, N_TOK), :].rearrange("(t p) d -> p t d", p=BLK),
                                 x2[:]).then_inc(x_stored, 16)
                    sp.wait_ge(x_stored, 16 * n + 32)
                    stand(sp, passed)
                sp.wait_ge(emptied, 16)

            @block.tensor
            def _(pe):
                def transpose_main(src, dst, signal):
                    for t in range(N_BLK):
                        mm = nc.tensor.transpose(dst[:, t * BLK:(t + 1) * BLK], src[:, t, 0:P], ident[0:BLK, 0:BLK])
                    mm.then_inc(signal, 1)

                def transpose_rest(src, dst, signal):
                    for t in range(N_BLK):
                        mm = nc.tensor.transpose(dst[0:REST, t * BLK:(t + 1) * BLK], src[:, t, P:D],
                                                 ident[0:BLK, 0:BLK])
                    mm.then_inc(signal, 1)

                def project(dst, m, col, x):
                    o = dst[0:m, 0:N_TOK]
                    c = slice(col, col + m)
                    nc.tensor.matmul(o, pack_hi[:, 0, c], x[:, 0, :], start=True, stop=False)
                    nc.tensor.matmul(o, pack_hi[:, 0, c], x[:, 1, :], start=False, stop=False)
                    nc.tensor.matmul(o, pack_lo[:, 0, c], x[:, 0, :], start=False, stop=False)
                    nc.tensor.matmul(o, pack_hi[:, 1, c], x[:, 2, :], start=False, stop=False)
                    return nc.tensor.matmul(o, pack_lo[:, 1, c], x[:, 2, :], start=False, stop=True)

                def project_block(o, x, t, c, first=True, last=True):
                    b = slice(t * BLK, (t + 1) * BLK)
                    nc.tensor.matmul(o, x[:, 0, b], pack_hi[:, 0, c], start=first, stop=False, skip_group_check=True)
                    nc.tensor.matmul(o, x[:, 0, b], pack_lo[:, 0, c], start=False, stop=False, skip_group_check=True)
                    nc.tensor.matmul(o, x[:, 1, b], pack_hi[:, 0, c], start=False, stop=False, skip_group_check=True)
                    nc.tensor.matmul(o, x[:, 2, b], pack_hi[:, 1, c], start=False, stop=False, skip_group_check=True)
                    return nc.tensor.matmul(o, x[:, 2, b], pack_lo[:, 1, c], start=False, stop=last,
                                            skip_group_check=True)

                def front_hn_main(n):
                    pe.wait_ge(hn_done, n + 1)
                    at_least(pe, qf_done, 2 * n)
                    transpose_main(hn, bank[0], t_hn)

                def front_hn_rest(n):
                    transpose_rest(hn, bank[1], t_hn)

                def front_z(n):
                    pe.wait_ge(z_done, n + 1)
                    at_least(pe, state_done, 2 * n)
                    transpose_main(z, bank[2], t_z)
                    transpose_rest(z, bank[3], t_z)

                def front_gate(n):
                    pe.wait_ge(lo_hn, 2 * n + 2)
                    project(bank[0], P, COL_G, hn_t).then_inc(mm_gk, 1)
                    project(bank[1], REST, COL_G + P, hn_t).then_inc(mm_gk, 1)

                def front_k(n):
                    pe.wait_ge(lo_z, 2 * n + 2)
                    project(bank[2], P, COL_K, z_t).then_inc(mm_gk, 1)
                    project(bank[3], REST, COL_K + P, z_t).then_inc(mm_gk, 1)

                def front_q(n):
                    pe.wait_ge(tanh_done, 2 * n + 1)
                    project(bank[0], P, COL_Q, z_t).then_inc(mm_q, 1)
                    pe.wait_ge(tanh_done, 2 * n + 2)
                    project(bank[1], REST, COL_Q + P, z_t).then_inc(mm_q, 1)
                    for pair in range(2):
                        pe.wait_ge(kg_done, 2 * n + pair + 1)
                        for t in (2 * pair, 2 * pair + 1):
                            o = bank[2 + pair][0:BLK, (t % 2) * D:(t % 2 + 1) * D]
                            mm = project_block(o, z_t, t, slice(COL_V, COL_V + D), first=(t % 2 == 0))
                        mm.then_inc(mm_v, 1)

                def front_state(n):
                    pe.wait_ge(kf_done, 2 * n + 2)
                    for t in range(N_BLK - 1):
                        b = slice(t * BLK, (t + 1) * BLK)
                        dst = bank[4 + t // 2][0:BLK, (t % 2) * D:(t % 2 + 1) * D]
                        nc.tensor.transpose(dst[:, 0:P], kf[:, 0, b], ident[:])
                        mm = nc.tensor.transpose(dst[:, P:D], kf[0:REST, 1, b], ident[0:REST, 0:REST])
                    mm.then_inc(t_k, 1)
                    pe.wait_ge(v_done, 2 * n + 2)
                    pe.wait_ge(ktok_done, n + 1)
                    nm, nr = HEADS_MAIN * VA, (HEADS - HEADS_MAIN) * VA
                    for t in range(N_BLK - 1):
                        mm = nc.tensor.matmul(bank[2][:, t * nm:(t + 1) * nm], k_tok[:, t, 0:P],
                                              v_aug[:, t, 0:HEADS_MAIN, :], start=True, stop=True,
                                              skip_group_check=True)
                    mm.then_inc(mm_kv, 1)
                    for t in range(N_BLK - 1):
                        mm = nc.tensor.matmul(bank[3][0:REST, t * nr:(t + 1) * nr], k_tok[:, t, P:D],
                                              v_aug[:, t, HEADS_MAIN:HEADS, :], start=True, stop=True,
                                              skip_group_check=True)
                    mm.then_inc(mm_kv, 1)

                def scores(n, g):
                    t, grp = divmod(g, N_GRP)
                    b = slice(t * BLK, (t + 1) * BLK)
                    if g >= 2:
                        wait_probs(n, g - 2)
                    if g == 0:
                        pe.wait_ge(kh_dve, n + 1)
                    if g in (1, 2):
                        pe.wait_ge(kh_act, 2 * n + g)
                    if g == 2:
                        pe.wait_ge(kh_pool, n + 1)
                    for j in range(GRP):
                        h = grp * GRP + j
                        mm = nc.tensor.matmul(bank[4 + g % 2][0:BLK, j * BLK:(j + 1) * BLK], kh[:, h, b],
                                              qf[:, h // HEADS_MAIN, b], start=True, stop=True, skip_group_check=True)
                    mm.then_inc(scores_done, 1)

                def wait_probs(n, g):
                    if g % 2 == 0:
                        pe.wait_ge(probs_dve, n * (N_SC // 2) + g // 2 + 1)
                    else:
                        pe.wait_ge(probs_pool, n * (N_SC // 2) + g // 2 + 1)

                def attention(n, nxt, tail):
                    pe.wait_ge(qf_done, 2 * n + 2)
                    scores(n, 0)
                    scores(n, 1)
                    pe.wait_ge(state_done, 2 * n + 2)
                    for t in range(N_BLK):
                        o = bank[6 + t % 2]
                        b = slice(t * BLK, (t + 1) * BLK)
                        nm = HEADS_MAIN * VA
                        if t >= 2:
                            pe.wait_ge(attn_done, n * N_BLK + t - 1)
                        nc.tensor.matmul(o[0:BLK, 0:nm], qf[:, 0, b], state[:, t, :], start=True, stop=False,
                                         skip_group_check=True)
                        nc.tensor.matmul(o[0:BLK, nm:HEADS * VA], qf[:, 1, b], state_r[:, t, :], start=False, stop=False,
                                         skip_group_check=True)
                        for grp in range(N_GRP):
                            g = t * N_GRP + grp
                            if g + 2 < N_SC:
                                scores(n, g + 2)
                            if tail is not None and g == 4:
                                tail_x(tail)
                            if tail is not None and g in (7, 8):
                                tail_router(tail, g - 7)
                            if tail is not None and g == 10:
                                tail_logits(tail)
                            if nxt is not None and g == N_SC - 2:
                                front_hn_main(nxt)
                            if nxt is not None and g == N_SC - 1:
                                front_hn_rest(nxt)
                            wait_probs(n, g)
                            for j in range(GRP):
                                h = grp * GRP + j
                                mm = nc.tensor.matmul(o[0:BLK, h * VA:(h + 1) * VA],
                                                      probs[:, g % 3, j * BLK:(j + 1) * BLK], v_aug[:, t, h, :],
                                                      start=False, stop=True, skip_group_check=True)
                        mm.then_inc(pv_done, 1)

                def attention_transpose(n):
                    pe.wait_ge(attn_done, N_BLK * n + N_BLK)
                    transpose_main(attn, bank[4], t_a)
                    transpose_rest(attn, bank[5], t_a)

                def attention_project(n):
                    pe.wait_ge(lo_a, 2 * n + 2)
                    for t in range(N_BLK):
                        mm = project_block(bank[6 + t // 2][0:BLK, (t % 2) * D:(t % 2 + 1) * D], a_t, t,
                                           slice(COL_P, COL_P + D), first=(t % 2 == 0))
                        if t % 2:
                            mm.then_inc(mm_proj, 1)

                def tail_x(n):
                    pe.wait_ge(x2_done, n + 1)
                    transpose_main(x2, bank[0], t_x)
                    transpose_rest(x2, bank[1], t_x)

                def tail_router(n, half):
                    if half == 0:
                        pe.wait_ge(x_copied, 2 * n + 2)
                        nc.tensor.matmul(bank[2][0:N_EXP, 0:N_TOK], w_router[:, 0, :], x_t[:, 0, :], start=True,
                                         stop=False, skip_group_check=True)
                    else:
                        nc.tensor.matmul(bank[2][0:N_EXP, 0:N_TOK], w_router[0:REST, 1, :], x_t[0:REST, 1, :],
                                         start=False, stop=True, skip_group_check=True).then_inc(mm_rt, 1)

                def tail_logits(n):
                    pe.wait_ge(by_expert, n + 1)
                    stand(pe, passed)
                    for t in range(N_BLK):
                        mm = nc.tensor.transpose(bank[3][0:BLK, t * N_EXP:(t + 1) * N_EXP],
                                                 logits_t[:, t * BLK:(t + 1) * BLK], ident[0:N_EXP, 0:N_EXP])
                    mm.then_inc(t_logits, 1)

                def turn(n, nxt, tail):
                    if n is not None:
                        attention(n, nxt, tail)
                    else:
                        front_hn_main(nxt)
                        front_hn_rest(nxt)
                    if tail is not None:
                        pe.wait_ge(logits_done, tail + 1)
                    if nxt is not None:
                        front_z(nxt)
                    if n is not None:
                        attention_transpose(n)
                    if nxt is not None:
                        front_gate(nxt)
                    if n is not None:
                        attention_project(n)
                    if nxt is not None:
                        front_k(nxt)
                        front_q(nxt)
                        front_state(nxt)

                pe.wait_ge(loaded, 32)
                turn(None, 0, None)
                turn(0, 1, None)
                with pe.Fori(1, N_SEQ - 1) as n:
                    turn(n, n + 1, n - 1)
                turn(N_SEQ - 1, None, N_SEQ - 2)
                tail_x(N_SEQ - 1)
                tail_router(N_SEQ - 1, 0)
                tail_router(N_SEQ - 1, 1)
                tail_logits(N_SEQ - 1)

            @block.scalar
            def _(act):
                def hi_parts(src_main, src_rest, dst, ready, n, signal):
                    act.wait_ge(ready, 2 * n + 1)
                    nc.scalar.copy(dst[:, 0, :], src_main[:, 0:N_TOK]).then_inc(signal, 1)
                    act.wait_ge(ready, 2 * n + 2)
                    nc.scalar.copy(dst[0:REST, 2, :], src_rest[0:REST, 0:N_TOK]).then_inc(signal, 1)

                def tail_copy(n):
                    act.wait_ge(t_x, 2 * n + 1)
                    nc.scalar.copy(x_t[:, 0, :], bank[0][:, 0:N_TOK]).then_inc(x_copied, 1)
                    act.wait_ge(t_x, 2 * n + 2)
                    nc.scalar.copy(x_t[0:REST, 1, :], bank[1][0:REST, 0:N_TOK]).then_inc(x_copied, 1)

                def tail_router(n):
                    act.wait_ge(mm_rt, n + 1)
                    nc.scalar.copy(logits_t, bank[2][0:N_EXP, 0:N_TOK]).then_inc(by_expert, 1)

                def attention(n, tail):
                    for g in range(1, N_SC, 2):
                        if tail is not None and g == 11:
                            tail_router(tail)
                        if tail is not None and g == 7:
                            tail_copy(tail)
                        act.wait_ge(scores_done, n * N_SC + g + 1)
                        nc.scalar.copy(probs[:, g % 3, :], bank[5][0:BLK, 0:GRP * BLK]).then_inc(probs_act, 1)

                def front_hi(n):
                    hi_parts(bank[0], bank[1], hn_t, t_hn, n, hi_hn)
                    hi_parts(bank[2], bank[3], z_t, t_z, n, hi_z)

                def front(n):
                    for half, (dst, m) in enumerate(halves(gate)):
                        act.wait_ge(mm_gk, 4 * n + half + 1)
                        nc.scalar.activation(dst, bank[half][0:m, 0:N_TOK], ACT.Tanh, bias=bgate_half[0:m, half:half + 1],
                                             scale=0.5).then_inc(tanh_done, 1)
                    for half, (dst, m) in enumerate(halves(gate)):
                        act.wait_ge(tanh_done, 2 * n + half + 1)
                        nc.scalar.activation(dst, dst, ACT.Copy, bias=0.5, scale=0.5).then_inc(gate_done, 1)
                    for half, (dst, m) in enumerate(halves(k_exp)):
                        act.wait_ge(kg_done, 2 * n + half + 1)
                        nc.scalar.activation(dst, kg[0:m, half, :], ACT.Exp).then_inc(kexp_done, 1)

                def front_q(n):
                    for half, (dst, m) in enumerate(halves(q_exp)):
                        act.wait_ge(mm_q, 2 * n + half + 1)
                        act.wait_ge(kf_done, 2 * n + half + 1)
                        nc.scalar.activation(dst, bank[half][0:m, 0:N_TOK], ACT.Exp,
                                             bias=bqk[0:m, half:half + 1]).then_inc(qexp_done, 1)
                        nc.scalar.activation(q_pos[0:m, half, :], bank[half][0:m, 0:N_TOK], ACT.Relu,
                                             bias=bqk[0:m, half:half + 1]).then_inc(qpos_done, 1)

                def head_rows(n, grp):
                    act.wait_ge(kf_done, 2 * n + (1 if grp == 1 else 2))
                    for h in range(grp * GRP, (grp + 1) * GRP - (POOL_HEADS if grp == 2 else 0)):
                        half, m = (0, P) if h < HEADS_MAIN else (1, REST)
                        mask = (hm_main, hm_rest)[half]
                        j = h - half * HEADS_MAIN
                        ins = nc.scalar.activation(kh[0:m, h, :], kf[0:m, half, :], ACT.Copy, scale=mask[:, j:j + 1])
                    ins.then_inc(kh_act, 1)

                def front_state(n):
                    act.wait_ge(t_k, n + 1)
                    nc.scalar.copy(k_tok[:, 0:2, :], bank[4][0:BLK, 0:2 * D].rearrange("p (t d) -> p t d", t=2))
                    nc.scalar.copy(k_tok[:, 2, :], bank[5][0:BLK, 0:D]).then_inc(ktok_done, 1)

                def turn(n, nxt, tail):
                    if n is not None:
                        attention(n, tail)
                    if nxt is not None:
                        front_hi(nxt)
                    if n is not None:
                        hi_parts(bank[4], bank[5], a_t, t_a, n, hi_a)
                    if nxt is not None:
                        front(nxt)
                        front_q(nxt)
                        front_state(nxt)
                        head_rows(nxt, 1)
                        head_rows(nxt, 2)

                turn(None, 0, None)
                turn(0, 1, None)
                with act.Fori(1, N_SEQ - 1) as n:
                    turn(n, n + 1, n - 1)
                turn(N_SEQ - 1, None, N_SEQ - 2)
                tail_copy(N_SEQ - 1)
                tail_router(N_SEQ - 1)

            @block.vector
            def _(dve):
                def lo_parts(src_main, src_rest, dst, hi_ready, n, signal):
                    dve.wait_ge(hi_ready, 2 * n + 1)
                    nc.vector.tensor_tensor(dst[:, 1, :], src_main[:, 0:N_TOK], dst[:, 0, :].bitcast(F32),
                                            ALU.subtract).then_inc(signal, 1)
                    dve.wait_ge(hi_ready, 2 * n + 2)
                    nc.vector.tensor_tensor(dst[REST:P, 2, :], src_rest[0:REST, 0:N_TOK], dst[0:REST, 2, :].bitcast(F32),
                                            ALU.subtract).then_inc(signal, 1)

                def tail_stats(n, which):
                    dve.wait_ge(h_done, 2 * n + 2)
                    stand(dve, passed)
                    norm_stats(dve, lambda t: h_all[:, n, t, :], which)

                def tail_apply(n, which):
                    dve.wait_ge(x_stored, 16 * n + 16)
                    norm_apply(dve, lambda t: h_all[:, n, t, :], x2, which, x2_done)

                def tail_logits(n):
                    dve.wait_ge(t_logits, n + 1)
                    nc.vector.tensor_copy(logits[:, bass.ds(n * N_BLK, N_BLK), :],
                                          bank[3][0:BLK, 0:N_BLK * N_EXP].rearrange("p (t e) -> p t e", e=N_EXP)
                                          ).then_inc(logits_done, 1)

                def normalize(n, t):
                    o = bank[6 + t % 2][0:BLK, 0:HEADS * VA].rearrange("p (h e) -> p h e", e=VA)
                    dve.wait_ge(pv_done, N_BLK * n + t + 1)
                    nc.vector.tensor_scalar(den[:], o[:, :, DH], 1e-6, None, ALU.add).then_inc(den_done, 1)
                    dve.wait_ge(den_done, N_BLK * n + t + 1)
                    nc.vector.reciprocal(rden[:], den[:]).then_inc(rden_done, 1)
                    dve.wait_ge(rden_done, N_BLK * n + t + 1)
                    nc.vector.tensor_tensor(attn[:, t, :].rearrange("p (h e) -> p h e", e=DH), o[:, :, 0:DH],
                                            rden[:].unsqueeze(2).broadcast_to((BLK, HEADS, DH)),
                                            ALU.mult).then_inc(attn_done, 1)

                def attention(n, nxt, tail):
                    for g in range(N_SC):
                        if g % 2 == 0:
                            dve.wait_ge(scores_done, n * N_SC + g + 1)
                            nc.vector.tensor_tensor(probs[:, g % 3, :].rearrange("p (j l) -> p j l", j=GRP),
                                                    bank[4][0:BLK, 0:GRP * BLK].rearrange("p (j l) -> p j l", j=GRP),
                                                    causal[:].unsqueeze(1).broadcast_to((BLK, GRP, BLK)),
                                                    ALU.mult).then_inc(probs_dve, 1)
                        if g % N_GRP == 1 and g > N_GRP:
                            normalize(n, g // N_GRP - 1)
                        if tail is not None:
                            if g == 0:
                                tail_stats(tail, LN_PER_SEQ * n + 1)
                            if g == 3:
                                tail_apply(tail, LN_PER_SEQ * n + 1)
                        if nxt is not None:
                            if g == 4:
                                norm_h_stats(dve, nxt, LN_PER_SEQ * n + 2)
                            if g == 6:
                                norm_h_apply(dve, nxt, LN_PER_SEQ * n + 2)
                            if g == 7:
                                norm_hn_stats(dve, nxt, LN_PER_SEQ * n + 2)
                            if g == 9:
                                norm_hn_apply(dve, nxt, LN_PER_SEQ * n + 2)
                    if tail is not None:
                        tail_logits(tail)
                    normalize(n, N_BLK - 1)

                def attention_out(n):
                    lo_parts(bank[4], bank[5], a_t, hi_a, n, lo_a)
                    dve.wait_ge(hb_done, n + 1)
                    for pair in range(2):
                        dve.wait_ge(mm_proj, 2 * n + pair + 1)
                        ts = slice(2 * pair, 2 * pair + 2)
                        nc.vector.tensor_tensor(h_all[:, n, ts, :],
                                                bank[6 + pair][0:BLK, 0:2 * D].rearrange("p (t d) -> p t d", t=2),
                                                hb[:, ts, :], ALU.add).then_inc(h_done, 1)

                def front(n):
                    lo_parts(bank[0], bank[1], hn_t, hi_hn, n, lo_hn)
                    lo_parts(bank[2], bank[3], z_t, hi_z, n, lo_z)

                def front_k(n):
                    for half, (dst, m) in enumerate(halves(kg)):
                        dve.wait_ge(gate_done, 2 * n + half + 1)
                        dve.wait_ge(mm_gk, 4 * n + half + 3)
                        nc.vector.scalar_tensor_tensor(dst, bank[2 + half][0:m, 0:N_TOK], bqk[0:m, 2 + half:3 + half],
                                                       gate[0:m, half, :], ALU.add, ALU.mult).then_inc(kg_done, 1)
                    for half, (dst, m) in enumerate(halves(k_pos)):
                        dve.wait_ge(kg_done, 2 * n + half + 1)
                        nc.vector.tensor_scalar(dst, kg[0:m, half, :], 0.0, None, ALU.max).then_inc(kpos_done, 1)
                    for half, (dst, m) in enumerate(halves(kf)):
                        dve.wait_ge(kexp_done, 2 * n + half + 1)
                        dve.wait_ge(kpos_done, 2 * n + half + 1)
                        nc.vector.scalar_tensor_tensor(dst, k_exp[0:m, half, :], 1.0, k_pos[0:m, half, :],
                                                       ALU.min, ALU.add).then_inc(kf_done, 1)
                    dve.wait_ge(kf_done, 2 * n + 1)
                    for h in range(GRP):
                        ins = nc.vector.tensor_scalar(kh[:, h, :], kf[:, 0, :], hm_main[:, h:h + 1], None, ALU.mult)
                    ins.then_inc(kh_dve, 1)

                def front_v(n):
                    for pair in range(2):
                        dve.wait_ge(mm_v, 2 * n + pair + 1)
                        for t in (2 * pair, 2 * pair + 1):
                            ins = nc.vector.tensor_tensor(
                                v_aug[:, t, :, 0:DH],
                                bank[2 + pair][0:BLK, (t % 2) * D:(t % 2 + 1) * D].rearrange("p (h e) -> p h e", e=DH),
                                bv_bc[:].rearrange("p (h e) -> p h e", e=DH), ALU.add)
                        ins.then_inc(v_done, 1)

                def front_q(n):
                    for half, (dst, m) in enumerate(halves(q_pos)):
                        dve.wait_ge(qexp_done, 2 * n + half + 1)
                        dve.wait_ge(qpos_done, 2 * n + half + 1)
                        nc.vector.scalar_tensor_tensor(qf[0:m, half, :], q_exp[0:m, half, :], 1.0, dst, ALU.min,
                                                       ALU.add).then_inc(qf_done, 1)

                def front_state(n):
                    for half, (dst, heads, mask, m) in enumerate([
                            (state, HEADS_MAIN, hm_main, P), (state_r, HEADS - HEADS_MAIN, hm_rest, REST)]):
                        dve.wait_ge(mm_kv, 2 * n + half + 1)
                        for t in range(N_BLK - 1):
                            ins = nc.vector.tensor_tensor(
                                dst[0:m, t + 1, :].rearrange("p (h e) -> p h e", e=VA),
                                bank[2 + half][0:m, t * heads * VA:(t + 1) * heads * VA].rearrange(
                                    "p (h e) -> p h e", e=VA),
                                mask[:].unsqueeze(2).broadcast_to((m, heads, VA)), ALU.mult)
                        ins.then_inc(masked, 1)
                    for t in range(1, N_BLK - 1):
                        dve.wait_ge(masked, 4 * n + 2 * t)
                        ins = nc.vector.tensor_tensor(state[:, t + 1, :], state[:, t + 1, :], state[:, t, :], ALU.add)
                        if t == 1:
                            ins.then_inc(masked, 1)
                        ins2 = nc.vector.tensor_tensor(state_r[0:REST, t + 1, :], state_r[0:REST, t + 1, :],
                                                       state_r[0:REST, t, :], ALU.add)
                        if t == 1:
                            ins2.then_inc(masked, 1)
                    ins.then_inc(state_done, 1)
                    ins2.then_inc(state_done, 1)

                def turn(n, nxt, tail):
                    if n is not None:
                        attention(n, nxt, tail)
                    if nxt is not None:
                        front(nxt)
                    if n is not None:
                        attention_out(n)
                    if nxt is not None:
                        front_k(nxt)
                        front_v(nxt)
                        front_q(nxt)
                        front_state(nxt)

                dve.wait_ge(loaded, 32)
                turn(None, 0, None)
                turn(0, 1, None)
                with dve.Fori(1, N_SEQ - 1) as n:
                    turn(n, n + 1, n - 1)
                turn(N_SEQ - 1, None, N_SEQ - 2)
                tail_stats(N_SEQ - 1, LN_PER_SEQ * N_SEQ - 1)
                tail_apply(N_SEQ - 1, LN_PER_SEQ * N_SEQ - 1)
                tail_logits(N_SEQ - 1)

            @block.gpsimd
            def _(pool):
                def attention(n, nxt, tail):
                    for g in range(1, N_SC, 2):
                        if g == 3 and tail is not None:
                            root(pool, 3 * n + 1)
                        if g in (7, 9) and nxt is not None:
                            root(pool, 3 * n + (2 if g == 7 else 3))
                        pool.wait_ge(probs_act, n * (N_SC // 2) + g // 2 + 1)
                        p3 = probs[:, g % 3, :].rearrange("p (j l) -> p j l", j=GRP)
                        nc.gpsimd.tensor_tensor(p3, p3, causal[:].unsqueeze(1).broadcast_to((BLK, GRP, BLK)),
                                                ALU.mult).then_inc(probs_pool, 1)

                def head_rows(n):
                    pool.wait_ge(kf_done, 2 * n + 2)
                    at_least(pool, scores_done, N_SC * n)
                    stand(pool, passed)
                    for h in range(HEADS - POOL_HEADS, HEADS):
                        j = h - HEADS_MAIN
                        ins = nc.gpsimd.tensor_scalar(kh[0:REST, h, :], kf[0:REST, 1, :], hm_rest[:, j:j + 1], None,
                                                      ALU.mult)
                    ins.then_inc(kh_pool, 1)

                def residual(n):
                    at_least(pool, h_done, 2 * n)
                    nc.gpsimd.tensor_tensor(hb[:], h_all[:, n, :, :],
                                            bproj_bc[:].unsqueeze(1).broadcast_to((BLK, N_BLK, D)),
                                            ALU.add).then_inc(hb_done, 1)

                def turn(n, nxt, tail):
                    if n is not None:
                        attention(n, nxt, tail)
                        residual(n)
                    if nxt is not None:
                        head_rows(nxt)

                pool.wait_ge(loaded, 32)
                turn(None, 0, None)
                turn(0, 1, None)
                with pool.Fori(1, N_SEQ - 1) as n:
                    turn(n, n + 1, n - 1)
                turn(N_SEQ - 1, None, N_SEQ - 2)
                root(pool, 3 * N_SEQ - 1)


def moe_stage(nc, passed, sem, bank, h_all, x_dram, slots_dram, y_dram, logits, ident, stage_up, stage_down,
              stage_in, load_expert, exp_bias, out):
    SHARED = N_EXP
    N_LAST = 4
    CARRY = N_ROW - N_LAST
    LAST = CARRY + N_TILE
    ALL_TILES = N_ROW + N_TILE
    X, H, Y, G, U = 0, 1, (2, 3), (4, 5), (6, 7)
    N_CONSTS = 10
    RING = 4
    with ExitStack() as ctx:
        def sb(name, shape, dt=F32):
            return ctx.enter_context(nc.sbuf_tensor(name, shape, dt))

        up_hi = sb("up_hi", [P, N_EXP + 1, 2, 2 * F], F32R)
        up_lo = sb("up_lo", [P, N_EXP + 1, 2, 2 * F], F32R)
        down_hi = sb("down_hi", [P, N_EXP + 1, N_CHUNK, D], F32R)
        down_lo = sb("down_lo", [P, N_EXP + 1, N_CHUNK, D], F32R)
        x_in = sb("x_in", [P, RING, D])
        x_t = sb("xm_t", [P, 2, 3, P], F32R)
        silu = sb("silu", [P, F])
        prod = sb("prod", [P, F])
        hid_hi = sb("hid_hi", [P, N_CHUNK, P], F32R)
        hid_lo = sb("hid_lo", [P, N_CHUNK, P], F32R)
        y_out = stage_up[:].rearrange("p a c -> p (a c)")[:, 0:RING * D].rearrange("p (m d) -> p m d", d=D)
        slot_meta = sb("slot_meta", [P, N_TILE, N_META])
        y_row = sb("y_row", [P, RING], I32)
        send = sb("send", [BLK, RING, TOP, D + N_META])
        send_to = sb("send_to", [BLK, RING, TOP], I32)
        bias_bc = sb("bias_bc", [BLK, N_EXP])
        earlier = sb("earlier", [BLK, N_EXP, N_EXP])
        prefer = sb("prefer", [BLK, N_EXP])
        before = sb("before", [BLK, BLK])
        ones = sb("ones", [BLK, BLK])
        tile_start = sb("tile_start", [BLK, N_ROW])
        tile_no = sb("tile_no", [1, N_TILE])
        row = sb("row", [BLK, N_ROW])
        row2 = sb("row2", [BLK, N_ROW])
        scores = logits
        picks = sb("picks", [BLK, N_ROW, N_EXP])
        chosen = sb("chosen", [BLK, N_ROW, N_EXP])
        work = sb("work", [BLK, N_TILE // 2 * N_EXP])
        filled = work[:, 0:N_EXP * N_ROW].rearrange("p (e r) -> p e r", e=N_EXP)
        over = work[0:1, :].rearrange("p (t e) -> p t e", e=N_EXP)
        best = prod[0:BLK, 0:N_ROW * N_EXP].rearrange("p (r e) -> p r e", e=N_EXP)
        sums = prod[0:BLK, N_ROW * N_EXP:N_ROW * N_EXP + N_EXP * N_EXP].rearrange("p (e j) -> p e j", e=N_EXP)
        prefix = [best, work[:, 0:N_ROW * N_EXP].rearrange("p (r e) -> p r e", e=N_EXP)]
        n_tiles = sb("n_tiles", [BLK, N_EXP])
        first_tile = sb("first_tile", [BLK, N_EXP])
        last_tile = sb("last_tile", [BLK, N_EXP])
        tile_expert_f = sb("tile_expert_f", [1, N_TILE])
        tile_expert = sb("tile_expert", [1, N_TILE], I32)
        slot = sb("slot", [BLK, TOP, N_ROW])
        meta = sb("meta", [BLK, N_ROW, TOP, N_META])

        bias_in, consts = sem("bias_in"), sem("consts")
        split_hi = [sem("split_hi_0"), sem("split_hi_1")]
        split_lo = [sem("split_lo_0"), sem("split_lo_1")]
        soft_in, soft_exp, counts_in, counted, order, routed = (sem("soft_in"), sem("soft_exp"), sem("counts_in"),
                                                                sem("counted"), sem("order"), sem("routed"))
        x_loaded = [sem(f"x_loaded{m}") for m in range(RING)]
        t_x, hi_x, lo_x, mm_g, mm_u = sem("m_t_x"), sem("m_hi_x"), sem("m_lo_x"), sem("mm_g"), sem("mm_u")
        silu_done, prod_done, t_h, hi_h, lo_h, mm_y = (sem("silu_done"), sem("prod_done"), sem("t_h"), sem("hi_h"),
                                                       sem("lo_h"), sem("mm_y"))
        added = sem("added")
        y_ready = sem("y_ready")
        y_sent = [sem(f"y_sent{m}") for m in range(RING)]                
        send_in = [sem(f"send_in{m}") for m in range(RING)]
        y_in = [sem(f"y_in{n}") for n in range(N_SEQ)]
        half_sum, summed, stored = sem("half_sum"), sem("summed"), sem("stored")
        rows_set = sem("rows_set")
        marked = sem("marked")
        x_sent = [sem(f"x_sent{m}") for m in range(RING)]

        def picks_of(n):
            return up_hi[0:BLK, n, :, :].bitcast(F32).rearrange("p a c -> p (a c)").rearrange(
                "p (t w d) -> p t w d", t=N_BLK, w=TOP)

        def block_of(i):
            return i - N_TILE if isinstance(i, int) and i >= LAST else i

        def up_part(weights, e, part):
            return weights[:, bass.ds(e, 1), part, :].rearrange("p o c -> p (o c)")

        def down_part(weights, e):
            return weights[:, bass.ds(e, 1), :, :].rearrange("p o f c -> p (o f) c")

        def split_lo_by(engine, ops, e, n, piece):
            engine.wait_ge(split_hi[piece], n + 1)
            stand(engine, passed)
            up = ops.tensor_tensor(up_part(up_lo, e, piece), stage_up[:, piece, :],
                                   up_part(up_hi, e, piece).bitcast(F32), ALU.subtract)
            if piece == 0:
                up.then_inc(split_lo[0], 1)
            else:
                ops.tensor_tensor(down_part(down_lo, e), stage_down[:], down_part(down_hi, e).bitcast(F32),
                                  ALU.subtract).then_inc(split_lo[1], 1)

        def over_tiles(engine, step, split_piece=None, start_run=lambda n: None, before_routed=None,
                       after_change=None):
            S, R = "shared", "routed"
            assert RING == N_LAST == 4 and RING * (N_EXP - 1) == CARRY and LAST % RING == 2
            start_run(3)
            step(0, 0, 0, S, None, S)
            for piece in range(2):
                if split_piece:
                    split_piece(1, piece)
                step(1 + piece, 0, 1 + piece, S, S, S)
            with engine.Fori(2, N_EXP) as e:
                start_run(4)
                for piece in range(2):
                    if split_piece:
                        split_piece(e, piece)
                    step(4 * e - 5 + 2 * piece, e - 2 + piece, (3, 1)[piece], S, S, S)
                    step(4 * e - 4 + 2 * piece, e - 1, (0, 2)[piece], S, S, S)
            start_run(2)
            step(CARRY - 1, CARRY // 4 - 1, 3, S, S, R)
            if before_routed:
                before_routed()
            step(CARRY, CARRY // 4, 0, R, S, R)
            if after_change:
                after_change()
            start_run(4)
            for i in range(CARRY + 1, CARRY + 5):
                step(i, i // 4, i % 4, R, R, R)
            with engine.Fori(CARRY // 4 + 1, LAST // 4) as q:
                start_run(4)
                for m in (1, 3):
                    step(4 * q + m, q, m, R, R, R)
                    step(4 * q + m + 1, q + m // 3, (m + 1) % 4, R, R, R)
            start_run(5)
            step(LAST - 1, LAST // 4, 1, R, R, S)
            for i in range(LAST, ALL_TILES):
                step(i, i // 4, i % 4, S, R if i == LAST else S, S if i < ALL_TILES - 1 else None)

        with nc.Block() as block:
            @block.sync
            def _(sp):
                sp.dma_start(bias_bc[:], exp_bias.partition_broadcast(BLK)).then_inc(bias_in, 16)

                def load_x(i, m, shared, k):
                    at_least(sp, t_x, i - RING + 1)
                    stand(sp, passed)
                    if shared:
                        sp.dma_start(x_in[0:BLK, m, :], x_dram[bass.ds(block_of(i) * BLK, BLK), :]).then_inc(x_loaded[m], 16)
                    else:
                        sp.dma_start(x_in[:, m, :], slots_dram[bass.ds(k * P, P), 0:D]).then_inc(x_loaded[m], 16)

                def load_send(j, turn, m):
                    at_least(sp, x_sent[m], 32 * turn)
                    stand(sp, passed)
                    for pick in range(TOP):
                        sp.dma_start(send[:, m, pick, 0:D], x_dram[bass.ds(j * BLK, BLK), :]).then_inc(send_in[m], 16)

                def load_slots(k, m):
                    load_x(CARRY + k, m, False, k)
                    sp.dma_start(slot_meta[:, bass.ds(k, 1), :],
                                 slots_dram[bass.ds(k * P, P), D:D + N_META].unsqueeze(1)).then_inc(x_loaded[m], 16)

                def next_expert(e, n, piece):
                    sp.wait_ge(split_lo[piece], n)
                    stand(sp, passed)
                    load_expert(sp, e, piece)

                sp.wait_ge(consts, 1)
                for i in range(RING):
                    load_x(i, i, True, 0)
                for j in range(RING):
                    load_send(j, 0, j)
                for e in (0, 1):
                    for piece in range(2):
                        next_expert(e, e + 1, piece)
                with sp.Fori(1, N_ROW // RING) as q:
                    for m in range(RING):
                        load_send(RING * q + m, q, m)
                for m in range(RING):
                    sp.wait_ge(x_sent[m], 32 * (N_ROW // RING))
                for m in range(RING):
                    sp.wait_ge(x_loaded[m], 16 * (CARRY // RING) + 16)
                for k in range(RING):
                    load_slots(k, k)
                with sp.Fori(1, N_TILE // RING) as q:
                    for m in range(RING):
                        load_slots(RING * q + m, m)
                for k in range(N_TILE // RING * RING, N_TILE):
                    load_slots(k, k % RING)
                for i in range(LAST, ALL_TILES):
                    load_x(i, i % RING, True, 0)
                for m in range(RING):
                    sp.wait_ge(y_sent[m], 16 * len(range(m, N_TILE, RING)))
                for n in range(N_SEQ):
                    rows = y_dram[n * N_TOK * TOP:(n + 1) * N_TOK * TOP, :]
                    sp.dma_start(picks_of(n), rows.rearrange("(t p w) d -> p t w d", p=BLK, w=TOP)).then_inc(y_in[n], 16)
                for n in range(N_SEQ):
                    sp.wait_ge(summed, n + 1)
                    sp.dma_start(out[n].rearrange("(t p) d -> p t d", p=BLK), h_all[:, n, :, :]).then_inc(stored, 16)
                sp.wait_ge(stored, 16 * N_SEQ)

            @block.gpsimd
            def _(pool):
                nc.gpsimd.memset(x_in[:], 0.0).then_inc(consts, 1)
                nc.gpsimd.memset(earlier[:], 1.0).then_inc(consts, 1)
                nc.gpsimd.memset(before[:], 1.0).then_inc(consts, 1)
                nc.gpsimd.memset(ones[:], 1.0).then_inc(consts, 1)
                nc.gpsimd.iota(tile_start[:], pattern=[[P, N_ROW]], base=0, channel_multiplier=0,
                               allow_small_or_imprecise_dtypes=True).then_inc(consts, 1)
                nc.gpsimd.iota(tile_no[:], pattern=[[1, N_TILE]], base=0, channel_multiplier=0,
                               allow_small_or_imprecise_dtypes=True).then_inc(consts, 1)
                nc.gpsimd.iota(prefer[:], pattern=[[-1, N_EXP]], base=N_EXP, channel_multiplier=0,
                               allow_small_or_imprecise_dtypes=True).then_inc(consts, 1)
                nc.gpsimd.iota(meta[:, :, :, 0].bitcast(I32), pattern=[[TOP * BLK, N_ROW], [1, TOP]], base=0,
                               channel_multiplier=TOP).then_inc(consts, 1)
                pool.wait_ge(consts, N_CONSTS - 2)
                nc.gpsimd.affine_select(out=earlier[:], in_=earlier[:], compare_op=ALU.is_ge, fill=0.0, base=-1,
                                        pattern=[[1, N_EXP], [-1, N_EXP]], channel_multiplier=0).then_inc(consts, 1)
                nc.gpsimd.affine_select(out=before[:], in_=before[:], compare_op=ALU.is_ge, fill=0.0, base=-1,
                                        pattern=[[1, BLK]], channel_multiplier=-1).then_inc(consts, 1)

                def send_block(j, turn, m):
                    at_least(pool, x_sent[m], 32 * turn)
                    stand(pool, passed)
                    nc.gpsimd.tensor_copy(send_to[:, m, :], slot[:, :, j]).then_inc(marked, 1)
                    pool.wait_ge(send_in[m], 32 * turn + 32)
                    stand(pool, passed)
                    nc.gpsimd.tensor_copy(send[:, m, :, D:D + N_META].bitcast(I32),
                                          meta[:, j, :, :].bitcast(I32)).then_inc(marked, 1)
                    pool.wait_ge(marked, 2 * j + 2)
                    stand(pool, passed)
                    for pick in range(TOP):
                        nc.gpsimd.indirect_dma_start(
                            out=slots_dram, out_offset=bass.IndirectOffsetOnAxis(ap=send_to[:, m, pick:pick + 1], axis=0),
                            in_=send[:, m, pick, :], in_offset=None, bounds_check=N_TILE * P - 1,
                            oob_is_err=False).then_inc(x_sent[m], 16)

                for n, e in enumerate([SHARED, 0]):
                    for piece in range(2):
                        split_lo_by(pool, nc.gpsimd, e, n, piece)
                pool.wait_ge(routed, 1)
                for j in range(RING):
                    send_block(j, 0, j)
                with pool.Fori(1, N_ROW // RING) as q:
                    for m in range(RING):
                        send_block(RING * q + m, q, m)

                def send_y(k, turn, m):
                    pool.wait_ge(t_x, CARRY + k + 1)
                    at_least(pool, y_sent[m], 16 * turn)
                    stand(pool, passed)
                    nc.gpsimd.tensor_copy(y_row[:, m:m + 1], slot_meta[:, bass.ds(k, 1), 0].bitcast(I32)
                                          ).then_inc(rows_set, 1)
                    pool.wait_ge(rows_set, k + 1)
                    pool.wait_ge(y_ready, k + 3)
                    stand(pool, passed)
                    nc.gpsimd.indirect_dma_start(
                        out=y_dram, out_offset=bass.IndirectOffsetOnAxis(ap=y_row[:, m:m + 1], axis=0),
                        in_=y_out[:, m, :], in_offset=None, bounds_check=N_ALL * TOP - 1,
                        oob_is_err=False).then_inc(y_sent[m], 16)

                for k in range(RING):
                    send_y(k, 0, k)
                with pool.Fori(1, N_TILE // RING) as q:
                    for m in range(RING):
                        send_y(RING * q + m, q, m)
                for k in range(N_TILE // RING * RING, N_TILE):
                    send_y(k, k // RING, k % RING)

            @block.tensor
            def _(pe):
                def transpose_x(i, turn, m, kind):
                    if kind == "shared" and isinstance(i, int) and i >= LAST:
                        pe.wait_ge(x_loaded[m], 16 * (N_ROW // RING) + 16 + 32 * len(range(m, N_TILE, RING)))
                    elif kind == "shared":
                        pe.wait_ge(x_loaded[m], 16 * turn + 16)
                    else:
                        pe.wait_ge(x_loaded[m], 32 * turn + 48 - 16 * (CARRY // RING))
                    at_least(pe, lo_x, i)
                    nc.tensor.transpose(bank[X][:, 0:P], x_in[:, m, 0:P], ident[:])
                    nc.tensor.transpose(bank[X][0:REST, P:2 * P], x_in[:, m, P:D], ident[:]).then_inc(t_x, 1)

                def gate_up(i, par, e):
                    pe.wait_ge(lo_x, i + 1)
                    at_least(pe, prod_done, i - 1)
                    for which, (b, signal) in enumerate([(G, mm_g), (U, mm_u)]):
                        c = slice(which * F, (which + 1) * F)
                        o = bank[b[par]][:, 0:F]
                        nc.tensor.matmul(o, x_t[:, par, 0, :], up_hi[:, e, 0, c], start=True, stop=False)
                        nc.tensor.matmul(o, x_t[:, par, 0, :], up_lo[:, e, 0, c], start=False, stop=False)
                        nc.tensor.matmul(o, x_t[:, par, 1, :], up_hi[:, e, 0, c], start=False, stop=False)
                        nc.tensor.matmul(o, x_t[:, par, 2, :], up_hi[:, e, 1, c], start=False, stop=False)
                        nc.tensor.matmul(o, x_t[:, par, 2, :], up_lo[:, e, 1, c], start=False, stop=True
                                         ).then_inc(signal, 1)

                def transpose_h(i):
                    at_least(pe, lo_h, i)
                    pe.wait_ge(prod_done, i + 1)
                    for f in range(N_CHUNK):
                        mm = nc.tensor.transpose(bank[H][:, f * P:(f + 1) * P], prod[:, f * P:(f + 1) * P], ident[:])
                    mm.then_inc(t_h, 1)

                def down(i, par, e, shared):
                    if isinstance(i, int) and i == 0:
                        pe.wait_ge(routed, 1)
                    pe.wait_ge(lo_h, i + 1)
                    if shared and isinstance(i, int) and i >= LAST + 2:
                        pe.wait_ge(added, CARRY + i - LAST - 1)
                    elif shared and not (isinstance(i, int) and i >= LAST):
                        at_least(pe, added, i - 1)
                    else:
                        pe.wait_ge(y_ready, i - CARRY + 1)
                    o = bank[Y[par]][:, 0:D]
                    for f in range(N_CHUNK):
                        nc.tensor.matmul(o, hid_hi[:, f, :], down_hi[:, e, f, :], start=(f == 0), stop=False)
                        nc.tensor.matmul(o, hid_hi[:, f, :], down_lo[:, e, f, :], start=False, stop=False)
                        mm = nc.tensor.matmul(o, hid_lo[:, f, :], down_hi[:, e, f, :], start=False,
                                              stop=(f == N_CHUNK - 1))
                    mm.then_inc(mm_y, 1)

                def expert_of(i, kind):
                    if kind != "routed":
                        return SHARED
                    return pe.value_load(tile_expert[0:1, bass.ds(i - CARRY, 1)], min_val=0, max_val=N_EXP - 1)

                known = {}
                left = [0]

                def start_run(n):
                    known.clear()
                    left[0] = n

                def step(i, turn, m, kind, prev, following):
                    par = m % 2
                    left[0] -= 1
                    if prev:
                        transpose_h(i - 1)
                    if following:
                        transpose_x(i + 1, turn + m // 3, (m + 1) % 4, following)
                    e = known["next"] if "next" in known else expert_of(i, kind)
                    gate_up(i, par, e)
                    last = known["this"] if "this" in known else expert_of(i - 1, prev)
                    known["this"] = e
                    if left[0] > 0:
                        known["next"] = expert_of(i + 1, following)
                    if prev:
                        down(i - 1, par ^ 1, last, prev == "shared")

                transpose_x(0, 0, 0, "shared")
                pe.wait_ge(consts, N_CONSTS)
                pe.wait_ge(counts_in, 1)
                flat = lambda a: a.rearrange("p r e -> p (r e)")
                nc.tensor.matmul(bank[Y[0]][0:BLK, 0:N_ROW * N_EXP], before[:], flat(chosen[:]), start=True, stop=False,
                                 skip_group_check=True)
                nc.tensor.matmul(bank[Y[0]][0:BLK, 0:N_ROW * N_EXP], ones[:], flat(prefix[1]), start=False, stop=True,
                                 skip_group_check=True)
                nc.tensor.matmul(bank[Y[1]][0:BLK, 0:N_EXP], ones[:], prefix[1][:, N_ROW - 1, :], start=True, stop=False)
                nc.tensor.matmul(bank[Y[1]][0:BLK, 0:N_EXP], ones[:], chosen[:, N_ROW - 1, :], start=False, stop=True
                                 ).then_inc(counted, 1)
                pe.wait_ge(split_lo[0], 1)
                pe.wait_ge(split_lo[1], 1)

                def before_routed():
                    for piece in range(2):
                        pe.wait_ge(split_lo[piece], N_EXP + 1)

                def after_change():
                    pe.wait_ge(added, CARRY)

                over_tiles(pe, step, start_run=start_run, before_routed=before_routed, after_change=after_change)
                transpose_h(ALL_TILES - 1)
                down(ALL_TILES - 1, 1, SHARED, True)

            @block.scalar
            def _(act):
                def split_hi_of(e, n, piece):
                    act.wait_ge(stage_in[piece], (16, 48)[piece] * n + (16, 48)[piece])
                    stand(act, passed)
                    if piece == 0:
                        nc.scalar.copy(up_part(up_hi, e, 0), stage_up[:, 0, :]).then_inc(split_hi[0], 1)
                    else:
                        nc.scalar.copy(up_part(up_hi, e, 1), stage_up[:, 1, :])
                        nc.scalar.copy(down_part(down_hi, e), stage_down[:]).then_inc(split_hi[1], 1)

                def hi_of_x(i, par):
                    at_least(act, mm_u, i - 1)
                    act.wait_ge(t_x, i + 1)
                    nc.scalar.copy(x_t[:, par, 0, :], bank[X][:, 0:P])
                    nc.scalar.copy(x_t[0:REST, par, 2, :], bank[X][0:REST, P:2 * P]).then_inc(hi_x, 1)

                def next_x(i, m):
                    act.dma_start(x_in[0:BLK, m, :], x_dram[bass.ds(i * BLK, BLK), :]).then_inc(x_loaded[m], 16)

                def split_piece(e, piece):
                    split_hi_of(e, e + 1, piece)
                    act.wait_ge(split_lo[1 - piece], e + 1 + piece)
                    stand(act, passed)
                    if piece == 0:
                        if not isinstance(e, int):
                            load_expert(act, e, 1)
                    else:
                        load_expert(act, e + 1, 0)

                def step(i, turn, m, kind, prev, following):
                    par = m % 2
                    if prev:
                        act.wait_ge(t_h, i)
                        at_least(act, mm_y, i - 1)
                        nc.scalar.copy(hid_hi[:], bank[H][:, 0:F].rearrange("p (f t) -> p f t", f=N_CHUNK)
                                       ).then_inc(hi_h, 1)
                    if following:
                        hi_of_x(i + 1, par ^ 1)
                    if kind == "shared" and following == "shared" and not (isinstance(i, int) and i >= LAST):
                        next_x(i + 1 + RING, (m + 1) % RING)
                    act.wait_ge(mm_g, i + 1)
                    at_least(act, prod_done, i)
                    nc.scalar.activation(silu[:], bank[G[par]][:, 0:F], ACT.Silu).then_inc(silu_done, 1)
                    if prev == "routed":
                        output(i - 1, turn - (m == 0) - CARRY // RING, (m - 1) % RING)

                def output(i, turn, m):
                    at_least(act, y_sent[m], 16 * turn)
                    act.wait_ge(mm_y, i + 1)
                    stand(act, passed)
                    nc.scalar.activation(y_out[:, m, :], bank[Y[m % 2]][:, 0:D], ACT.Copy,
                                         scale=slot_meta[:, bass.ds(i - CARRY, 1), 1]).then_inc(y_ready, 1)

                act.sem_inc(y_ready, 2)
                act.wait_ge(soft_in, 1)
                nc.scalar.activation(scores[:], scores[:], ACT.Exp).then_inc(soft_exp, 1)
                for n, e in enumerate([SHARED, 0]):
                    for piece in range(2):
                        split_hi_of(e, n, piece)
                    if n == 0:
                        hi_of_x(0, 0)
                        next_x(RING, 0)
                def before_routed():
                    act.wait_ge(stage_in[0], 16 * (N_EXP + 2))
                    for piece in range(2):
                        act.wait_ge(split_lo[piece], N_EXP + 1)

                over_tiles(act, step, before_routed=before_routed, split_piece=split_piece)
                act.wait_ge(t_h, ALL_TILES)
                act.wait_ge(mm_y, ALL_TILES - 1)
                nc.scalar.copy(hid_hi[:], bank[H][:, 0:F].rearrange("p (f t) -> p f t", f=N_CHUNK)).then_inc(hi_h, 1)

            @block.vector
            def _(dve):
                done = [0]

                def then(ins):
                    done[0] += 1
                    ins.then_inc(order, 1)
                    dve.wait_ge(order, done[0])

                def lo_of_x(i, par):
                    dve.wait_ge(hi_x, i + 1)
                    nc.vector.tensor_tensor(x_t[:, par, 1, :], bank[X][:, 0:P], x_t[:, par, 0, :].bitcast(F32),
                                            ALU.subtract)
                    nc.vector.tensor_tensor(x_t[REST:P, par, 2, :], bank[X][0:REST, P:2 * P],
                                            x_t[0:REST, par, 2, :].bitcast(F32), ALU.subtract).then_inc(lo_x, 1)

                wide = lambda r: r.unsqueeze(2).broadcast_to((BLK, N_ROW, N_EXP))
                per_row = lambda a: a.unsqueeze(1).broadcast_to((BLK, N_ROW, N_EXP))
                then(nc.vector.tensor_reduce(row[:], logits[:], axis=AX.X, op=ALU.max))
                nc.vector.tensor_tensor(scores[:], logits[:], wide(row[:]), ALU.subtract).then_inc(soft_in, 1)
                dve.wait_ge(soft_exp, 1)
                then(nc.vector.tensor_reduce(row[:], scores[:], axis=AX.X, op=ALU.add))
                then(nc.vector.reciprocal(row2[:], row[:]))
                then(nc.vector.tensor_tensor(scores[:], scores[:], wide(row2[:]), ALU.mult))
                dve.wait_ge(bias_in, 16)
                then(nc.vector.tensor_tensor(picks[:], scores[:], per_row(bias_bc[:]), ALU.add))
                dve.wait_ge(consts, N_CONSTS)
                for pick in range(TOP):
                    then(nc.vector.tensor_reduce(row[:], picks[:], axis=AX.X, op=ALU.max))
                    then(nc.vector.tensor_tensor(best, picks[:], wide(row[:]), ALU.is_equal))
                    then(nc.vector.tensor_tensor(best, best, per_row(prefer[:]), ALU.mult))
                    then(nc.vector.tensor_reduce(row[:], best, axis=AX.X, op=ALU.max))
                    then(nc.vector.tensor_tensor((chosen[:], best)[pick], best, wide(row[:]), ALU.is_equal))
                    if pick == 0:
                        then(nc.vector.scalar_tensor_tensor(picks[:], chosen[:], -BEATEN, picks[:], ALU.mult, ALU.add))
                then(nc.vector.tensor_tensor(chosen[:], chosen[:], best, ALU.add))
                for buffer in prefix:
                    nc.vector.memset(buffer[:, 0, :], 0.0)
                then(nc.vector.tensor_copy(prefix[0][:, 1:N_ROW, :], chosen[:, 0:N_ROW - 1, :]))
                now, dist = 0, 1
                while dist < N_ROW:
                    nc.vector.tensor_copy(prefix[1 - now][:, 0:dist, :], prefix[now][:, 0:dist, :])
                    then(nc.vector.tensor_tensor(prefix[1 - now][:, dist:N_ROW, :], prefix[now][:, dist:N_ROW, :],
                                                 prefix[now][:, 0:N_ROW - dist, :], ALU.add))
                    now, dist = 1 - now, 2 * dist
                assert now == 1
                nc.vector.tensor_copy(row[:, 0:1], row[:, 0:1]).then_inc(counts_in, 1)
                lo_of_x(0, 0)
                then(nc.vector.tensor_tensor(picks[:], chosen[:], scores[:], ALU.mult))
                then(nc.vector.tensor_reduce(row[:], picks[:], axis=AX.X, op=ALU.add))
                then(nc.vector.tensor_scalar(row[:], row[:], 1e-9, None, ALU.add))
                then(nc.vector.reciprocal(row2[:], row[:]))
                then(nc.vector.tensor_tensor(picks[:], picks[:], wide(row2[:]), ALU.mult))
                dve.wait_ge(counted, 1)
                then(nc.vector.tensor_copy(last_tile[:], bank[Y[1]][0:BLK, 0:N_EXP]))
                then(nc.vector.tensor_tensor(filled, last_tile[:].unsqueeze(2).broadcast_to((BLK, N_EXP, N_ROW)),
                                             tile_start[:].unsqueeze(1).broadcast_to((BLK, N_EXP, N_ROW)), ALU.is_gt))
                then(nc.vector.tensor_reduce(n_tiles[:], filled, axis=AX.X, op=ALU.add))
                then(nc.vector.tensor_tensor(sums, earlier[:],
                                             n_tiles[:].unsqueeze(1).broadcast_to((BLK, N_EXP, N_EXP)), ALU.mult))
                then(nc.vector.tensor_reduce(first_tile[:], sums, axis=AX.X, op=ALU.add))
                then(nc.vector.tensor_tensor(last_tile[:], first_tile[:], n_tiles[:], ALU.add))
                for half in (slice(0, N_TILE // 2), slice(N_TILE // 2, N_TILE)):
                    shape = (1, N_TILE // 2, N_EXP)
                    then(nc.vector.tensor_tensor(over, tile_no[:, half].unsqueeze(2).broadcast_to(shape),
                                                 last_tile[0:1, :].unsqueeze(1).broadcast_to(shape), ALU.is_ge))
                    then(nc.vector.tensor_reduce(tile_expert_f[:, half], over, axis=AX.X, op=ALU.add))
                then(nc.vector.tensor_scalar(tile_expert[:], tile_expert_f[:], float(N_EXP - 1), None, ALU.min))
                then(nc.vector.tensor_scalar(first_tile[:], first_tile[:], float(P), None, ALU.mult))
                then(nc.vector.tensor_tensor(scores[:], bank[Y[0]][0:BLK, 0:N_ROW * N_EXP].rearrange(
                    "p (r e) -> p r e", e=N_EXP), per_row(first_tile[:]), ALU.add))
                then(nc.vector.tensor_tensor(chosen[:], scores[:], chosen[:], ALU.mult))
                then(nc.vector.tensor_reduce(slot[:, 1, :], chosen[:], axis=AX.X, op=ALU.max))
                then(nc.vector.tensor_reduce(row[:], chosen[:], axis=AX.X, op=ALU.add))
                then(nc.vector.tensor_tensor(slot[:, 0, :], row[:], slot[:, 1, :], ALU.subtract))
                then(nc.vector.tensor_tensor(scores[:], scores[:], wide(slot[:, 1, :]), ALU.is_equal))
                then(nc.vector.tensor_tensor(scores[:], scores[:], picks[:], ALU.mult))
                then(nc.vector.tensor_tensor(picks[:], picks[:], scores[:], ALU.subtract))
                nc.vector.tensor_reduce(meta[:, :, 0, 1], picks[:], axis=AX.X, op=ALU.add)
                nc.vector.tensor_reduce(meta[:, :, 1, 1], scores[:], axis=AX.X, op=ALU.add).then_inc(routed, 1)

                def lo_of_h(i):
                    dve.wait_ge(hi_h, i + 1)
                    nc.vector.tensor_tensor(hid_lo[:], bank[H][:, 0:F].rearrange("p (f t) -> p f t", f=N_CHUNK),
                                            hid_hi[:].bitcast(F32), ALU.subtract).then_inc(lo_h, 1)

                h_rows = h_all[:].rearrange("p s t d -> p (s t) d")

                def add_shared(i, par):
                    dve.wait_ge(mm_y, i + 1)
                    h = h_rows[:, block_of(i), :]
                    nc.vector.tensor_tensor(h, bank[Y[par]][0:BLK, 0:D], h, ALU.add).then_inc(added, 1)

                def add_picks(n):
                    h = h_all[:, n, :, :]
                    dve.wait_ge(y_in[n], 16)
                    nc.vector.tensor_tensor(h, h, picks_of(n)[:, :, 0, :], ALU.add).then_inc(half_sum, 1)
                    dve.wait_ge(half_sum, n + 1)
                    nc.vector.tensor_tensor(h, h, picks_of(n)[:, :, 1, :], ALU.add).then_inc(summed, 1)

                def step(i, turn, m, kind, prev, following):
                    par = m % 2
                    if prev:
                        lo_of_h(i - 1)
                    if following:
                        lo_of_x(i + 1, par ^ 1)
                    dve.wait_ge(silu_done, i + 1)
                    dve.wait_ge(mm_u, i + 1)
                    at_least(dve, t_h, i)
                    nc.vector.tensor_tensor(prod[:], silu[:], bank[U[par]][:, 0:F], ALU.mult).then_inc(prod_done, 1)
                    if prev == "shared":
                        add_shared(i - 1, par ^ 1)
                    if isinstance(i, int) and i >= LAST + 3:
                        add_picks(i - LAST - 3)

                over_tiles(dve, step, split_piece=lambda e, piece: split_lo_by(dve, nc.vector, e, e + 1, piece))
                lo_of_h(ALL_TILES - 1)
                add_shared(ALL_TILES - 1, 1)
                for n in range(1, N_SEQ):
                    if n == N_SEQ - 1:
                        dve.wait_ge(added, N_ROW)
                    add_picks(n)


_IN_ORDER = ["frames", "dft", "mel2", "dct", "w_mfcc", "b_tok", "w_pack", "b_qk_col", "b_v", "b_gate_col", "ln_b_col",
             "ln_g_col", "b_proj", "head_main", "head_rest", "exp_bias", "w_up", "w_down"]


def lay_out(x, L0_tok_mel_filters, L0_tok_dct, L0_tok_w_proj, L0_tok_b_proj, L0_attn_W_qkv, L0_attn_b_qkv,
            L0_attn_W_gate, L0_attn_b_gate, L0_attn_W_proj, L0_attn_b_proj, L0_attn_ln_g, L0_attn_ln_b,
            L0_ffn_w_router, L0_ffn_expert_bias, L0_ffn_Wg, L0_ffn_Wu, L0_ffn_Wd, L0_ffn_sg, L0_ffn_su, L0_ffn_sd):
    k = np.arange(N_BINS)[None, :]
    j = np.arange(FRAME)[:, None]
    window = (0.54 - 0.46 * np.cos(2.0 * np.pi * j / (FRAME - 1)))
    angle = 2.0 * np.pi * ((j * k) % FRAME) / FRAME
    dft = np.concatenate([window * np.cos(angle), -window * np.sin(angle)], axis=1).astype(np.float32)
    head_of = np.arange(P)[:, None] // DH
    return {
        "frames": x.reshape(N_SEQ, N_TOK, STEP)[:, :, :FRAME].transpose(2, 0, 1),
        "dft": dft,
        "mel2": np.concatenate([L0_tok_mel_filters.T, L0_tok_mel_filters.T], axis=0),
        "dct": L0_tok_dct,
        "w_mfcc": L0_tok_w_proj,
        "b_tok": L0_tok_b_proj.reshape(1, D),
        "w_pack": np.concatenate([L0_attn_W_qkv, L0_attn_W_gate, L0_attn_W_proj, L0_ffn_w_router.T], axis=1),
        "b_qk_col": L0_attn_b_qkv[:2 * D].reshape(2 * D, 1),
        "b_v": L0_attn_b_qkv[2 * D:],
        "b_gate_col": L0_attn_b_gate.reshape(D, 1),
        "ln_b_col": L0_attn_ln_b.reshape(D, 1),
        "ln_g_col": L0_attn_ln_g.reshape(D, 1),
        "b_proj": L0_attn_b_proj,
        "head_main": (head_of == np.arange(HEADS_MAIN)[None, :]).astype(np.float32),
        "head_rest": (head_of[:REST] == np.arange(HEADS - HEADS_MAIN)[None, :]).astype(np.float32),
        "exp_bias": L0_ffn_expert_bias,
        "w_up": np.concatenate([
            np.concatenate([L0_ffn_Wg, L0_ffn_sg[None]], axis=0).transpose(0, 2, 1),
            np.concatenate([L0_ffn_Wu, L0_ffn_su[None]], axis=0).transpose(0, 2, 1)], axis=2),
        "w_down": np.concatenate([L0_ffn_Wd, L0_ffn_sd[None]], axis=0).transpose(0, 2, 1).reshape(
            N_EXP + 1, N_CHUNK, P, D).transpose(0, 2, 1, 3),
    }


def kernel(**inputs):
    import concourse.bacc as bacc
    from concourse.bass_utils import run_bass_kernel_spmd

    nc = bacc.Bacc("TRN2", target_bir_lowering=False, num_devices=1)
    laid = lay_out(**{name: np.asarray(a) for name, a in inputs.items()})
    arrays, args = {}, []
    for name in _IN_ORDER:
        a = np.ascontiguousarray(laid[name])
        arrays[f"in_{name}"] = a
        args.append(nc.dram_tensor(f"in_{name}", a.shape, mybir.dt.from_np(a.dtype), kind="ExternalInput").ap())
    out = nc.dram_tensor("out_dram", (N_SEQ, N_TOK, D), F32, kind="ExternalOutput").ap()
    build(nc, *args, out)
    got = run_bass_kernel_spmd(nc, [arrays], core_ids=[0])
    return got.results[0]["out_dram"]
```
